# Optimizing a Trainium2 kernel written in Bass

```python
import numpy as np
import jax
import jax.numpy as jnp

def _softmax(x, axis=-1):
    return jax.nn.softmax(x, axis=axis)

def _gelu(x):
    return jax.nn.gelu(x, approximate=True)

def _silu(x):
    return jax.nn.silu(x)

def _sigmoid(x):
    return jax.nn.sigmoid(x)

def _layernorm(x, axis=-1, eps=1e-05):
    m = jnp.mean(x, axis=axis, keepdims=True)
    v = jnp.var(x, axis=axis, keepdims=True)
    return (x - m) / jnp.sqrt(v + eps)

def _scatter_add(tgt, idx, src, axis=0):
    return tgt.at[idx].add(src)

def _segment_sum(src, seg, n):
    return jax.ops.segment_sum(src, seg, n)
kernel_name = 'mk_early_fusion_d1_tok_img256_r4_cecc44'

def setup_inputs(seed: int=0):
    np.random.seed(seed)
    _w = jnp.asarray

    def _rec_inputs():
        import jax
        import jax.numpy as jnp
        _rk = jax.random.key(seed)
        x = -0.000125008 + 0.999885 * jax.random.normal(jax.random.fold_in(_rk, 1), (16, 64, 128, 128), jnp.float32)
        txt = 7.55513e-05 + 0.28436 * jax.random.normal(jax.random.fold_in(_rk, 2), (16, 77, 64), jnp.float32)
        return (x, txt)
    x, txt = _rec_inputs()

    def _L0_tok_setup():
        import jax, jax.numpy as jnp
        import numpy as np
        D_MODEL = 64
        NHEAD = 8
        DS = 4
        OFFSET_SCALE = 4.0

        def bilinear_sample(fm, pts):
            B, C, H, W = fm.shape
            x = (pts[..., 0] + 1.0) * 0.5 * (W - 1)
            y = (pts[..., 1] + 1.0) * 0.5 * (H - 1)
            x0 = jnp.clip(jnp.floor(x), 0.0, W - 2)
            y0 = jnp.clip(jnp.floor(y), 0.0, H - 2)
            wx = jnp.clip(x - x0, 0.0, 1.0)
            wy = jnp.clip(y - y0, 0.0, 1.0)
            x0i = x0.astype(jnp.int32)
            y0i = y0.astype(jnp.int32)
            fm2 = fm.reshape(B, C, H * W)
            N, P = (pts.shape[1], pts.shape[2])

            def gather(yi, xi):
                idx = (yi * W + xi).reshape(B, N * P)
                g = jnp.take_along_axis(fm2, idx[:, None, :], axis=2)
                return g.reshape(B, C, N, P)
            v00 = gather(y0i, x0i)
            v01 = gather(y0i, x0i + 1)
            v10 = gather(y0i + 1, x0i)
            v11 = gather(y0i + 1, x0i + 1)
            wx_ = wx[:, None]
            wy_ = wy[:, None]
            out = v00 * (1 - wx_) * (1 - wy_) + v01 * wx_ * (1 - wy_) + v10 * (1 - wx_) * wy_ + v11 * wx_ * wy_
            return jnp.moveaxis(out, 1, -1)

        def layer_norm(x, g, b, eps=1e-05):
            mu = jnp.mean(x, axis=-1, keepdims=True)
            var = jnp.var(x, axis=-1, keepdims=True)
            return (x - mu) * jax.lax.rsqrt(var + eps) * g + b

        def reference_points(B, H, W):
            yc = jnp.linspace(-1.0, 1.0, H // DS)
            xc = jnp.linspace(-1.0, 1.0, W // DS)
            yg, xg = jnp.meshgrid(yc, xc, indexing='ij')
            ref = jnp.stack([xg.reshape(-1), yg.reshape(-1)], axis=-1)
            return jnp.broadcast_to(ref[None], (B,) + ref.shape)
        key = jax.random.key(seed)
        ks = jax.random.split(key, 6)
        B, C, H, W = (8, D_MODEL, 128, 128)
        s = 0.05
        return {'feature_map': jax.random.normal(ks[0], (B, C, H, W), jnp.float32), 'W_q': jax.random.normal(ks[1], (C, C), jnp.float32) * s, 'W_k': jax.random.normal(ks[2], (C, C), jnp.float32) * s, 'W_v': jax.random.normal(ks[3], (C, C), jnp.float32) * s, 'W_o1': jax.random.normal(ks[4], (C, C // DS), jnp.float32) * s, 'b_o1': jnp.zeros((C // DS,), jnp.float32), 'ln_g': jnp.ones((C // DS,), jnp.float32), 'ln_b': jnp.zeros((C // DS,), jnp.float32), 'W_o2': jax.random.normal(ks[5], (C // DS, NHEAD * 2), jnp.float32) * s, 'b_o2': jnp.zeros((NHEAD * 2,), jnp.float32)}
    _L0_tok_all = _L0_tok_setup()
    _L0_tok_in = {k: v for k, v in _L0_tok_all.items() if k in ('W_q', 'W_k', 'W_v', 'W_o1', 'b_o1', 'ln_g', 'ln_b', 'W_o2', 'b_o2')}
    del _L0_tok_all

    def _L0_attn_setup():
        import jax, jax.numpy as jnp
        import numpy as np
        STATE_DIM = 256
        INPUT_DIM = 64
        OUTPUT_DIM = 64
        KX = 10
        LAM = 5.0
        BSZ = 16
        SEQ = 512

        def _lds_forward(inputs, h0, A, B, C, M):
            bsz, L, _ = inputs.shape
            S = A.shape[0]
            kx = M.shape[-1]
            uB = jnp.einsum('bld,ds->bls', inputs, B)
            a = jnp.broadcast_to(A, (1, L, S))

            def combine(x, y):
                a1, b1 = x
                a2, b2 = y
                return (a1 * a2, a2 * b1 + b2)
            Pa, Pb = jax.lax.associative_scan(combine, (a, uB), axis=1)
            all_h = Pa * h0 + Pb
            lds_out = jnp.einsum('bls,so->blo', all_h, C)
            new_lds = jnp.pad(lds_out[:, kx:, :], ((0, 0), (0, kx), (0, 0)))
            ar = jnp.zeros_like(new_lds)
            for i in range(kx):
                x_i = jnp.pad(inputs, ((0, 0), (i, 0), (0, 0)))[:, :L, :]
                ar = ar + jnp.einsum('oj,blj->blo', M[:, :, i], x_i)
            return ar + new_lds
        key = jax.random.key(seed)
        ks = jax.random.split(key, 6)
        inputs = jax.random.normal(ks[0], (BSZ, SEQ, INPUT_DIM), dtype=jnp.float32)
        h0 = jax.random.normal(ks[1], (STATE_DIM,), dtype=jnp.float32)
        A = jnp.exp(-LAM * jax.random.uniform(ks[2], (STATE_DIM,), dtype=jnp.float32))
        B = jax.random.normal(ks[3], (INPUT_DIM, STATE_DIM), dtype=jnp.float32) / INPUT_DIM
        C = jax.random.normal(ks[4], (STATE_DIM, OUTPUT_DIM), dtype=jnp.float32) / STATE_DIM
        M = jax.random.normal(ks[5], (OUTPUT_DIM, INPUT_DIM, KX), dtype=jnp.float32) / OUTPUT_DIM
        return {'inputs': inputs, 'h0': h0, 'A': A, 'B': B, 'C': C, 'M': M}
    _L0_attn_all = _L0_attn_setup()
    _L0_attn_in = {k: v for k, v in _L0_attn_all.items() if k in ('h0', 'A', 'B', 'C', 'M')}
    del _L0_attn_all

    def _L0_ffn_setup():
        import jax, jax.numpy as jnp
        import numpy as np
        E, D, H, TOP_K = (6, 64, 64, 2)
        ROUTER_H = D // 2
        key = jax.random.key(seed)
        ks = jax.random.split(key, 12)
        s = 1.0 / np.sqrt(D)
        sh = 1.0 / np.sqrt(H)
        sr = 1.0 / np.sqrt(ROUTER_H)
        return {'features': jax.random.normal(ks[0], (8, 1024, D), dtype=jnp.float32), 'router_w1': jax.random.uniform(ks[1], (D, ROUTER_H), jnp.float32, -s, s), 'router_b1': jnp.zeros((ROUTER_H,), jnp.float32), 'router_w2': jax.random.uniform(ks[2], (ROUTER_H, E), jnp.float32, -sr, sr), 'router_b2': jnp.zeros((E,), jnp.float32), 'expert_w1': jax.random.uniform(ks[3], (E, D, H), jnp.float32, -s, s), 'expert_b1': jnp.zeros((E, H), jnp.float32), 'expert_w2': jax.random.uniform(ks[4], (E, H, H), jnp.float32, -sh, sh), 'expert_b2': jnp.zeros((E, H), jnp.float32), 'expert_w3': jax.random.uniform(ks[5], (E, H, D), jnp.float32, -sh, sh), 'expert_b3': jnp.zeros((E, D), jnp.float32)}
    _L0_ffn_all = _L0_ffn_setup()
    _L0_ffn_in = {k: v for k, v in _L0_ffn_all.items() if k in ('router_w1', 'router_b1', 'router_w2', 'router_b2', 'expert_w1', 'expert_b1', 'expert_w2', 'expert_b2', 'expert_w3', 'expert_b3')}
    del _L0_ffn_all
    return {'x': x, 'txt': txt, 'L0_tok_W_q': _L0_tok_in['W_q'], 'L0_tok_W_k': _L0_tok_in['W_k'], 'L0_tok_W_v': _L0_tok_in['W_v'], 'L0_tok_W_o1': _L0_tok_in['W_o1'], 'L0_tok_b_o1': _L0_tok_in['b_o1'], 'L0_tok_ln_g': _L0_tok_in['ln_g'], 'L0_tok_ln_b': _L0_tok_in['ln_b'], 'L0_tok_W_o2': _L0_tok_in['W_o2'], 'L0_tok_b_o2': _L0_tok_in['b_o2'], 'L0_attn_h0': _L0_attn_in['h0'], 'L0_attn_A': _L0_attn_in['A'], 'L0_attn_B': _L0_attn_in['B'], 'L0_attn_C': _L0_attn_in['C'], 'L0_attn_M': _L0_attn_in['M'], 'L0_ffn_router_w1': _L0_ffn_in['router_w1'], 'L0_ffn_router_b1': _L0_ffn_in['router_b1'], 'L0_ffn_router_w2': _L0_ffn_in['router_w2'], 'L0_ffn_router_b2': _L0_ffn_in['router_b2'], 'L0_ffn_expert_w1': _L0_ffn_in['expert_w1'], 'L0_ffn_expert_b1': _L0_ffn_in['expert_b1'], 'L0_ffn_expert_w2': _L0_ffn_in['expert_w2'], 'L0_ffn_expert_b2': _L0_ffn_in['expert_b2'], 'L0_ffn_expert_w3': _L0_ffn_in['expert_w3'], 'L0_ffn_expert_b3': _L0_ffn_in['expert_b3']}

def reference(x, txt, L0_tok_W_q, L0_tok_W_k, L0_tok_W_v, L0_tok_W_o1, L0_tok_b_o1, L0_tok_ln_g, L0_tok_ln_b, L0_tok_W_o2, L0_tok_b_o2, L0_attn_h0, L0_attn_A, L0_attn_B, L0_attn_C, L0_attn_M, L0_ffn_router_w1, L0_ffn_router_b1, L0_ffn_router_w2, L0_ffn_router_b2, L0_ffn_expert_w1, L0_ffn_expert_b1, L0_ffn_expert_w2, L0_ffn_expert_b2, L0_ffn_expert_w3, L0_ffn_expert_b3):
    import jax
    import jax.numpy as jnp

    def _L0_tok_ref(feature_map, W_q, W_k, W_v, W_o1, b_o1, ln_g, ln_b, W_o2, b_o2):
        import jax, jax.numpy as jnp
        import numpy as np
        D_MODEL = 64
        NHEAD = 8
        DS = 4
        OFFSET_SCALE = 4.0

        def bilinear_sample(fm, pts):
            B, C, H, W = fm.shape
            x = (pts[..., 0] + 1.0) * 0.5 * (W - 1)
            y = (pts[..., 1] + 1.0) * 0.5 * (H - 1)
            x0 = jnp.clip(jnp.floor(x), 0.0, W - 2)
            y0 = jnp.clip(jnp.floor(y), 0.0, H - 2)
            wx = jnp.clip(x - x0, 0.0, 1.0)
            wy = jnp.clip(y - y0, 0.0, 1.0)
            x0i = x0.astype(jnp.int32)
            y0i = y0.astype(jnp.int32)
            fm2 = fm.reshape(B, C, H * W)
            N, P = (pts.shape[1], pts.shape[2])

            def gather(yi, xi):
                idx = (yi * W + xi).reshape(B, N * P)
                g = jnp.take_along_axis(fm2, idx[:, None, :], axis=2)
                return g.reshape(B, C, N, P)
            v00 = gather(y0i, x0i)
            v01 = gather(y0i, x0i + 1)
            v10 = gather(y0i + 1, x0i)
            v11 = gather(y0i + 1, x0i + 1)
            wx_ = wx[:, None]
            wy_ = wy[:, None]
            out = v00 * (1 - wx_) * (1 - wy_) + v01 * wx_ * (1 - wy_) + v10 * (1 - wx_) * wy_ + v11 * wx_ * wy_
            return jnp.moveaxis(out, 1, -1)

        def layer_norm(x, g, b, eps=1e-05):
            mu = jnp.mean(x, axis=-1, keepdims=True)
            var = jnp.var(x, axis=-1, keepdims=True)
            return (x - mu) * jax.lax.rsqrt(var + eps) * g + b

        def reference_points(B, H, W):
            yc = jnp.linspace(-1.0, 1.0, H // DS)
            xc = jnp.linspace(-1.0, 1.0, W // DS)
            yg, xg = jnp.meshgrid(yc, xc, indexing='ij')
            ref = jnp.stack([xg.reshape(-1), yg.reshape(-1)], axis=-1)
            return jnp.broadcast_to(ref[None], (B,) + ref.shape)
        B, C, H, W = feature_map.shape
        dh = C // NHEAD
        ref = reference_points(B, H, W)
        Nq = ref.shape[1]
        q_feat = bilinear_sample(feature_map, ref[:, :, None, :])[:, :, 0]
        queries = q_feat @ W_q.T
        h = jax.nn.gelu(layer_norm(q_feat @ W_o1 + b_o1, ln_g, ln_b))
        off = (h @ W_o2 + b_o2).reshape(B, Nq, NHEAD, 2) * OFFSET_SCALE
        scale = jnp.array([2.0 / (W - 1), 2.0 / (H - 1)], jnp.float32)
        sampling_points = ref[:, :, None, :] + off * scale
        sampled = bilinear_sample(feature_map, sampling_points)
        keys = jnp.einsum('bnpc,dc->bnpd', sampled, W_k)
        values = jnp.einsum('bnpc,dc->bnpd', sampled, W_v)
        q = queries.reshape(B, Nq, NHEAD, dh)
        k = keys.reshape(B, Nq, NHEAD, NHEAD, dh)
        v = values.reshape(B, Nq, NHEAD, NHEAD, dh)
        scores = jnp.einsum('bnhd,bnphd->bnhp', q, k) / jnp.sqrt(jnp.float32(dh))
        attn = jax.nn.softmax(scores, axis=-1)
        out = jnp.einsum('bnhp,bnphd->bnhd', attn, v).reshape(B, Nq, C)
        return out

    def _L0_attn_ref(inputs, h0, A, B, C, M):
        import jax, jax.numpy as jnp
        import numpy as np
        STATE_DIM = 256
        INPUT_DIM = 64
        OUTPUT_DIM = 64
        KX = 10
        LAM = 5.0
        BSZ = 16
        SEQ = 512

        def _lds_forward(inputs, h0, A, B, C, M):
            bsz, L, _ = inputs.shape
            S = A.shape[0]
            kx = M.shape[-1]
            uB = jnp.einsum('bld,ds->bls', inputs, B)
            a = jnp.broadcast_to(A, (1, L, S))

            def combine(x, y):
                a1, b1 = x
                a2, b2 = y
                return (a1 * a2, a2 * b1 + b2)
            Pa, Pb = jax.lax.associative_scan(combine, (a, uB), axis=1)
            all_h = Pa * h0 + Pb
            lds_out = jnp.einsum('bls,so->blo', all_h, C)
            new_lds = jnp.pad(lds_out[:, kx:, :], ((0, 0), (0, kx), (0, 0)))
            ar = jnp.zeros_like(new_lds)
            for i in range(kx):
                x_i = jnp.pad(inputs, ((0, 0), (i, 0), (0, 0)))[:, :L, :]
                ar = ar + jnp.einsum('oj,blj->blo', M[:, :, i], x_i)
            return ar + new_lds
        return _lds_forward(inputs, h0, A, B, C, M)

    def _L0_ffn_ref(features, router_w1, router_b1, router_w2, router_b2, expert_w1, expert_b1, expert_w2, expert_b2, expert_w3, expert_b3):
        import jax, jax.numpy as jnp
        import numpy as np
        E, D, H, TOP_K = (6, 64, 64, 2)
        ROUTER_H = D // 2
        rh = jax.nn.relu(features @ router_w1 + router_b1)
        expert_logits = jax.nn.softmax(rh @ router_w2 + router_b2, axis=-1)
        top_w, top_i = jax.lax.top_k(expert_logits, TOP_K)
        routing_weights = jax.nn.softmax(top_w, axis=-1)
        h1 = jax.nn.relu(jnp.einsum('bsd,edh->bseh', features, expert_w1) + expert_b1)
        h2 = jax.nn.relu(jnp.einsum('bseh,ehf->bsef', h1, expert_w2) + expert_b2)
        expert_out = jnp.einsum('bsef,efo->bseo', h2, expert_w3) + expert_b3
        sel = jnp.take_along_axis(expert_out, top_i[:, :, :, None], axis=2)
        combined = jnp.sum(sel * routing_weights[..., None], axis=2)
        return combined
    h = _L0_tok_ref(x, L0_tok_W_q, L0_tok_W_k, L0_tok_W_v, L0_tok_W_o1, L0_tok_b_o1, L0_tok_ln_g, L0_tok_ln_b, L0_tok_W_o2, L0_tok_b_o2)
    h = jnp.concatenate([h, txt], axis=1)
    h = h + _L0_attn_ref(_layernorm(h, axis=-1), L0_attn_h0, L0_attn_A, L0_attn_B, L0_attn_C, L0_attn_M)
    h = h + _L0_ffn_ref(_layernorm(h, axis=-1), L0_ffn_router_w1, L0_ffn_router_b1, L0_ffn_router_w2, L0_ffn_router_b2, L0_ffn_expert_w1, L0_ffn_expert_b1, L0_ffn_expert_w2, L0_ffn_expert_b2, L0_ffn_expert_w3, L0_ffn_expert_b3)
    return h

_drawn_inputs = setup_inputs


def setup_inputs(seed=0):
    import zlib

    import numpy as np

    out = dict(_drawn_inputs(seed))
    spreads = {'L0_tok_b_o1': (0.0, 0.1),
     'L0_tok_ln_g': (1.0, 0.2),
     'L0_tok_ln_b': (0.0, 0.1),
     'L0_tok_b_o2': (0.0, 0.1),
     'L0_ffn_router_b1': (0.0, 0.1),
     'L0_ffn_router_b2': (0.0, 0.1),
     'L0_ffn_expert_b1': (0.0, 0.312),
     'L0_ffn_expert_b2': (0.0, 0.1),
     'L0_ffn_expert_b3': (0.0, 0.1)}
    factors = {'L0_attn_h0': 51.271}
    for name, (base, spread) in spreads.items():
        noise = np.random.default_rng([zlib.crc32(name.encode()), seed]).standard_normal(out[name].shape)
        drawn = base * np.exp(spread * noise) if base else spread * noise
        out[name] = jnp.asarray(drawn.astype(out[name].dtype))
    for name, factor in factors.items():
        out[name] = (out[name] * factor).astype(out[name].dtype)
    return out
```

```python
from contextlib import ExitStack

import numpy as np

import concourse.bass as bass
from concourse import mybir

F32 = mybir.dt.float32
U32 = mybir.dt.uint32
ALU = mybir.AluOpType
ACT = mybir.ActivationFunctionType
AX = mybir.AxisListType

P = 128
BATCH, CH, IMG = 16, 64, 128
HEADS, POINTS, HD, DS = 8, 8, 8, 4
GRID = IMG // DS
QUERIES = GRID * GRID
TILES = QUERIES // P
TXT = 77
SEQ = QUERIES + TXT
ROW_PAIRS = IMG - 1
OFFCH = CH // DS
OFFSETS = HEADS * 2
OFFSET_SCALE = 4.0
STATES, TAPS = 256, 10
SHALVES = STATES // P
EXPERTS = 6
PAIRS = EXPERTS // 2
ROUTER_H = CH // 2
TOKT = 9
CHUNKS, CT = 3, 3
CW = CT * P
PADW = TOKT * P
PAD = TAPS
NW = 96
QW = CH + OFFCH
EPS = 1e-5
ROUND = float(3 * 2 ** 22)
GELU_C = 2.0 * float(np.sqrt(2.0 / np.pi))
SM_SCALE = float(HD) ** -0.5
GATHER = 16 * POINTS

RING_READERS = ["dve"] * (CHUNKS * SHALVES + CHUNKS) + ["act"] * CHUNKS
for _c in range(CHUNKS):
    RING_READERS += ["act"] * (2 * PAIRS) + ["dve"] * (PAIRS + 1)
RING = len(RING_READERS)
RING_ACT = RING_READERS.count("act")
RING_DVE = RING - RING_ACT
USE_LDS = CHUNKS * SHALVES
USE_RH = USE_LDS + CHUNKS
USE_FFN = USE_RH + CHUNKS
FFN_USES = 3 * PAIRS + 1

OFFSET_STEPS = 25
ROUTE_STEPS = 19


def due(count):
    return not isinstance(count, int) or count > 0


def ring_count(reader, use):
    return RING_READERS[:use].count(reader)


def build(nc, fm_rows, qcorn, txt, wtab, reftab, ident_in, rank_in, wqo_in, wkv_in, bo1_in, lng_in,
          lnb_in, wo2_in, bo2_in, a_in, h0_in, bst_in, cst_in, mt_in, rw1_in, rb1_in, rw2_in,
          w1_in, b1_in, w2_in, b2_in, w3_in, b3_in, sel_in, out):
    with ExitStack() as ctx:
        def sb(name, shape, dt=F32):
            return ctx.enter_context(nc.sbuf_tensor(name, shape, dt))

        def pb(name, shape):
            return ctx.enter_context(nc.psum_tensor(name, shape, F32))

        def sem(name):
            return ctx.enter_context(nc.semaphore(name))

        corner_w = sb("corner_w", [P, 2, QUERIES])
        ref_pix = sb("ref_pix", [P, TILES, OFFSETS])
        ident = sb("ident", [P, P])
        rank = sb("rank", [P, EXPERTS])
        wqo = sb("wqo", [P, NW])
        wkv = sb("wkv", [P, 2 * CH])
        bo1 = sb("bo1", [P, OFFCH])
        lng = sb("lng", [P, OFFCH])
        lnb = sb("lnb", [P, OFFCH])
        wo2 = sb("wo2", [P, P])
        bo2 = sb("bo2", [P, OFFSETS])
        decay = sb("decay", [P, SHALVES])
        state0 = sb("state0", [P, SHALVES])
        bst = sb("bst", [P, STATES])
        cst = sb("cst", [P, SHALVES, NW])
        mt = sb("mt", [P, TAPS // 2, NW])
        rw1 = sb("rw1", [P, P])
        rb1 = sb("rb1", [P, 1])
        rw2 = sb("rw2", [P, NW])
        w1 = sb("w1", [P, PAIRS, P])
        b1 = sb("b1", [P, PAIRS])
        w2 = sb("w2", [P, PAIRS, P])
        b2 = sb("b2", [P, PAIRS])
        w3 = sb("w3", [P, PAIRS, NW])
        b3 = sb("b3", [P, NW])
        sel = sb("sel", [P, PAIRS, P])
        CONSTS = [(corner_w, wtab), (ref_pix, reftab), (ident, ident_in), (rank, rank_in),
                  (wqo, wqo_in), (wkv, wkv_in), (bo1, bo1_in), (lng, lng_in), (lnb, lnb_in),
                  (wo2, wo2_in), (bo2, bo2_in), (decay, a_in), (state0, h0_in), (bst, bst_in),
                  (cst, cst_in), (mt, mt_in), (rw1, rw1_in), (rb1, rb1_in), (rw2, rw2_in),
                  (w1, w1_in), (b1, b1_in), (w2, w2_in), (b2, b2_in), (w3, w3_in), (b3, b3_in),
                  (sel, sel_in)]

        qc = sb("qc", [P, 2, QUERIES])
        qo = [sb(f"qo{k}", [P, TILES, QW]) for k in range(2)]
        o1 = sb("o1", [P, TILES, OFFCH])
        o2 = sb("o2", [P, TILES, OFFCH])
        o3 = sb("o3", [P, TILES, OFFCH])
        o4 = sb("o4", [P, TILES, OFFCH])
        s8a = sb("s8a", [P, TILES])
        s8b = sb("s8b", [P, TILES])
        s8c = sb("s8c", [P, TILES])
        s8d = sb("s8d", [P, TILES])
        hT = sb("hT", [P, P])
        pix = sb("pix", [P, TILES * POINTS, 2])
        low = sb("low", [P, TILES * POINTS, 2])
        hats = sb("hats", [P, TILES * POINTS, 2, 2])
        w4 = [sb(f"w4_{k}", [P, TILES, POINTS * 4]) for k in range(2)]
        rowf = sb("rowf", [P, TILES * POINTS])
        batch_row = sb("batch_row", [P, 1])
        idx = [sb(f"idx{k}", [P, TILES * POINTS], U32) for k in range(2)]
        G = sb("G", [P, TILES, POINTS * 4 * CH])
        g2 = [sb(f"g2_{k}", [P, POINTS, 2 * CH]) for k in range(2)]
        sT = [sb(f"sT{k}", [P, POINTS, P]) for k in range(2)]
        prodk = sb("prodk", [P, POINTS, CH])
        prodv = sb("prodv", [P, POINTS, CH])
        scores = sb("scores", [P, POINTS, HEADS])
        smax = sb("smax", [P, HEADS])
        shifted = sb("shifted", [P, POINTS, HEADS])
        probs = sb("probs", [P, POINTS, HEADS])
        den = sb("den", [P, HEADS])
        rden = sb("rden", [P, HEADS])
        av = sb("av", [P, CH])
        H = [sb(f"H{k}", [P, TOKT, CH]) for k in range(2)]
        stats = sb("stats", [P, TOKT, 6])
        mv1 = sb("mv1", [P, TOKT, 2])
        mv2 = sb("mv2", [P, TOKT, 2])
        ve = [sb(f"ve{k}", [P, TOKT]) for k in range(2)]
        lnv = [sb(f"lnv{k}", [P, TOKT]) for k in range(2)]
        y0 = [sb(f"y0_{k}", [P, TOKT]) for k in range(2)]
        ny = [sb(f"ny{k}", [P, TOKT]) for k in range(2)]
        rstd = [sb(f"rstd{k}", [P, TOKT]) for k in range(2)]
        nmr = [sb(f"nmr{k}", [P, TOKT]) for k in range(2)]
        x1n = sb("x1n", [P, TOKT, 2, CH])
        X2 = sb("X2", [P, PAD + PADW + 2])
        states = sb("states", [P, SHALVES, PADW + TAPS])
        h1 = sb("h1", [P, TOKT, CH])
        x2n = sb("x2n", [P, TOKT, P])
        X3 = sb("X3", [P, PADW])
        rh = sb("rh", [P, PADW])
        r1 = sb("r1", [P, TOKT, EXPERTS])
        r2 = sb("r2", [P, TOKT, EXPERTS])
        r3 = sb("r3", [P, TOKT, EXPERTS])
        top1 = sb("top1", [P, TOKT, EXPERTS])
        top2 = sb("top2", [P, TOKT, EXPERTS])
        t9a = sb("t9a", [P, TOKT])
        t9b = sb("t9b", [P, TOKT])
        t9c = sb("t9c", [P, TOKT])
        gates = sb("gates", [P, TOKT, P])
        gT = sb("gT", [P, PADW])
        a1 = sb("a1", [P, PAIRS, CW])
        a2 = sb("a2", [P, PAIRS, CW])
        a3 = sb("a3", [P, PAIRS, CW])
        fin = [sb(f"fin{k}", [P, CT, CH]) for k in range(CHUNKS)]

        tbank = pb("tbank", [P, 2, 4, P])
        kv = pb("kv", [P, POINTS, 2 * CH])
        pA = pb("pA", [P, 512])
        pB = pb("pB", [P, 512])
        ring = pb("ring", [P, 2, 512])

        consts_in = sem("consts_in")
        cleared = sem("cleared")
        pool_passed = sem("pool_passed")
        dve_passed = sem("dve_passed")
        qc_in = sem("qc_in")
        qc_weighted = sem("qc_weighted")
        pA_full = sem("pA_full")
        qo_ready = sem("qo_ready")
        offset_step = sem("offset_step")
        off_var = sem("off_var")
        off_ln = sem("off_ln")
        off_y = sem("off_y")
        gelu_arg = sem("gelu_arg")
        gelu_exp = sem("gelu_exp")
        off_h = sem("off_h")
        hT_ready = sem("hT_ready")
        pix_ready = sem("pix_ready")
        idx_ready = sem("idx_ready")
        gather_in = [sem(f"gather_in{t}") for t in range(TILES)]
        g_weighted = sem("g_weighted")
        g_summed = sem("g_summed")
        t_full = sem("t_full")
        t_moved = sem("t_moved")
        kv_full = sem("kv_full")
        qk_done = sem("qk_done")
        scores_done = sem("scores_done")
        max_done = sem("max_done")
        shifted_ready = sem("shifted_ready")
        probs_ready = sem("probs_ready")
        av_done = sem("av_done")
        den_done = sem("den_done")
        avsum_done = sem("avsum_done")
        rden_done = sem("rden_done")
        h_ready = sem("h_ready")
        txt_in = sem("txt_in")
        stat_done = sem("stat_done")
        var_ready = sem("var_ready")
        ln_done = sem("ln_done")
        y_ready = sem("y_ready")
        newton_step = sem("newton_step")
        x1_ready = sem("x1_ready")
        pB_full = sem("pB_full")
        x2_low = sem("x2_low")
        x2_ready = sem("x2_ready")
        ring_full = sem("ring_full")
        ring_act = sem("ring_act")
        ring_dve = sem("ring_dve")
        x2n_ready = sem("x2n_ready")
        x3_ready = sem("x3_ready")
        route_step = sem("route_step")
        logits_read = sem("logits_read")
        route_exp = sem("route_exp")
        gap_ready = sem("gap_ready")
        gates_ready = sem("gates_ready")
        gT_ready = sem("gT_ready")
        out_done = [sem(f"out_done{k}") for k in range(CHUNKS)]

        block = ctx.enter_context(nc.Block())

        def schedule(eng, start, body, tail):
            start()
            body(0, 0, False, True)
            body(1, 1, True, True)
            with eng.Fori(0, (BATCH - 4) // 2) as i:
                body(2 * i + 2, 0, True, True)
                body(2 * i + 3, 1, True, True)
            body(BATCH - 2, 0, True, True)
            body(BATCH - 1, 1, True, False)
            tail()

        @block.sync
        def _(sp):
            for dst, src in CONSTS:
                sp.dma_start(dst[:], src).then_inc(consts_in, 16)

            def load_corners(b):
                if due(2 * b):
                    sp.wait_ge(qo_ready, 2 * b)
                sp.dma_start(qc[:], qcorn[bass.ds(b, 1)].rearrange("o p x q -> p (o x) q")).then_inc(qc_in, 16)

            def load_text(b, par):
                if not (isinstance(b, int) and b == 0):
                    sp.wait_ge(var_ready, 2 * (b - 1) + 1)
                sp.dma_start(H[par][0:TXT, TILES, :], txt[bass.ds(b, 1)].rearrange("o p c -> (o p) c")).then_inc(txt_in, 16)

            def store(s):
                for c in range(CHUNKS):
                    sp.wait_ge(ring_dve, s * RING_DVE + ring_count("dve", USE_FFN + FFN_USES * (c + 1)))
                    dst = out[bass.ds(s, 1), c * CW:min((c + 1) * CW, SEQ), :]
                    if c < CHUNKS - 1:
                        sp.dma_start(dst.rearrange("o (t p) c -> p (o t) c", p=P), fin[c][:]).then_inc(out_done[c], 16)
                    else:
                        full = dst[:, 0:(CT - 1) * P, :]
                        sp.dma_start(full.rearrange("o (t p) c -> p (o t) c", p=P), fin[c][:, 0:CT - 1, :]).then_inc(out_done[c], 16)
                        sp.dma_start(dst[:, (CT - 1) * P:, :].rearrange("o p c -> (o p) c"), fin[c][0:TXT, CT - 1, :]).then_inc(out_done[c], 16)

            def start():
                sp.wait_ge(cleared, 2)
                load_corners(0)

            def body(b, par, side, nxt):
                if nxt:
                    load_corners(b + 1)
                load_text(b, par)
                if side:
                    store(b - 1)

            def tail():
                store(BATCH - 1)
                for c in range(CHUNKS):
                    sp.wait_ge(out_done[c], 16 * BATCH * (2 if c == CHUNKS - 1 else 1))

            schedule(sp, start, body, tail)

        @block.gpsimd
        def _(pool):
            nc.gpsimd.memset(H[0][:], 0.0).then_inc(cleared, 1)
            nc.gpsimd.memset(H[1][:], 0.0).then_inc(cleared, 1)
            nc.gpsimd.memset(X2[:], 0.0).then_inc(cleared, 1)
            nc.gpsimd.memset(states[:], 0.0).then_inc(cleared, 1)
            nc.gpsimd.memset(X3[:], 0.0).then_inc(cleared, 1)
            nc.gpsimd.memset(gates[:], 0.0).then_inc(cleared, 1)
            nc.gpsimd.memset(x2n[:], 0.0).then_inc(cleared, 1)
            nc.gpsimd.memset(batch_row[:], 0.0).then_inc(cleared, 1)

            def body(b, par, side, nxt):
                pool.wait_ge(idx_ready, b + 1)
                for t in range(TILES):
                    if due((b - 1) * TILES + t + 1):
                        pool.wait_ge(g_summed, (b - 1) * TILES + t + 1)
                    pool.sem_inc(pool_passed, 1)
                    for k in range(POINTS):
                        nc.gpsimd.indirect_dma_start(
                            out=G[:, t, k * 4 * CH:(k + 1) * 4 * CH], out_offset=None, in_=fm_rows,
                            in_offset=bass.IndirectOffsetOnAxis(ap=idx[par][:, t * POINTS + k:t * POINTS + k + 1], axis=0),
                        ).then_inc(gather_in[t], 16)

            schedule(pool, lambda: None, body, lambda: None)

        @block.tensor
        def _(pe):
            pe.wait_ge(consts_in, 16 * len(CONSTS))
            pe.wait_ge(cleared, 8)

            def queries(b):
                pe.wait_ge(qc_weighted, b + 1)
                for half in range(2):
                    if half == 0:
                        if due(b):
                            pe.wait_ge(pix_ready, b)
                    else:
                        pe.wait_ge(qo_ready, 2 * b + 1)
                    for j in range(4):
                        t = 4 * half + j
                        for x in range(2):
                            mm = nc.tensor.matmul(pA[:, j * NW:(j + 1) * NW], qc[:, x, t * P:(t + 1) * P], wqo[:],
                                                  start=(x == 0), stop=(x == 1))
                    mm.then_inc(pA_full, 1)

            def offset_turn(b):
                pe.wait_ge(off_h, b + 1)
                nc.tensor.transpose(pA[:, 0:P], o4[:].rearrange("p t c -> p (t c)"), ident[:]).then_inc(pA_full, 1)

            def offset_out(b):
                pe.wait_ge(hT_ready, b + 1)
                nc.tensor.matmul(pA[:, 0:P], hT[:], wo2[:], start=True, stop=True).then_inc(pA_full, 1)

            def turn_samples(n, t):
                pe.wait_ge(g_summed, n + 1)
                for half in range(2):
                    if due(2 * (n - 1) + half + 1):
                        pe.wait_ge(t_moved, 2 * (n - 1) + half + 1)
                    for j in range(4):
                        mm = nc.tensor.transpose(tbank[:, half, j, :], g2[t % 2][:, 4 * half + j, :], ident[:])
                    mm.then_inc(t_full, 1)

            def project(n, t):
                if due(n):
                    pe.wait_ge(av_done, n)
                for half in range(2):
                    pe.wait_ge(t_moved, 2 * n + half + 1)
                    for j in range(4):
                        k = 4 * half + j
                        mm = nc.tensor.matmul(kv[:, k, :], sT[t % 2][:, k, :], wkv[:], start=True, stop=True)
                    mm.then_inc(kv_full, 1)

            def ring_free(s, use):
                u = use - 2
                if u < 0:
                    if due(s * RING_DVE):
                        pe.wait_ge(ring_dve, s * RING_DVE)
                    return
                reader = RING_READERS[u]
                per = RING_ACT if reader == "act" else RING_DVE
                pe.wait_ge(ring_act if reader == "act" else ring_dve, s * per + ring_count(reader, u + 1))

            def turn_x2(s, c):
                pe.wait_ge(x1_ready, s * TOKT + CT * (c + 1))
                if c == 0:
                    if due(s * CHUNKS):
                        pe.wait_ge(gT_ready, s * CHUNKS)
                else:
                    pe.wait_ge(x2_ready, s * CHUNKS + c)
                for j in range(CT):
                    mm = nc.tensor.transpose(pB[:, j * P:(j + 1) * P], x1n[:, c * CT + j].rearrange("p a c -> p (a c)"), ident[:])
                mm.then_inc(pB_full, 1)

            def drive(s, c):
                pe.wait_ge(x2_ready, s * CHUNKS + c + 1)
                w = min(CW, SEQ - c * CW)
                for v in range(SHALVES):
                    use = c * SHALVES + v
                    ring_free(s, use)
                    nc.tensor.matmul(ring[:, use % 2, 0:w], bst[:, v * P:(v + 1) * P],
                                     X2[:, PAD + c * CW:PAD + c * CW + w], start=True, stop=True).then_inc(ring_full, 1)

            def mix(s, c):
                use = USE_LDS + c
                ring_free(s, use)
                pe.wait_ge(ring_dve, s * RING_DVE + SHALVES * min(c + 2, CHUNKS))
                pe.wait_ge(x2_ready, s * CHUNKS + c + 1)
                for j in range(CT):
                    t0 = (c * CT + j) * P
                    dst = ring[:, use % 2, j * NW:(j + 1) * NW]
                    for i in range(TAPS // 2):
                        at = PAD + t0 - 2 * i
                        nc.tensor.matmul(dst, X2[:, at:at + P], mt[:, i, :], start=(i == 0), stop=False)
                    for v in range(SHALVES):
                        mm = nc.tensor.matmul(dst, states[:, v, t0 + TAPS:t0 + TAPS + P], cst[:, v, :],
                                              start=False, stop=(v == SHALVES - 1))
                mm.then_inc(ring_full, 1)

            def turn_x3(s, c):
                pe.wait_ge(x2n_ready, s * TOKT + CT * (c + 1))
                if c > 0:
                    pe.wait_ge(x3_ready, s * CHUNKS + c)
                for j in range(CT):
                    mm = nc.tensor.transpose(pB[:, j * P:(j + 1) * P], x2n[:, c * CT + j, :], ident[:])
                mm.then_inc(pB_full, 1)

            def router_hidden(s, c):
                use = USE_RH + c
                ring_free(s, use)
                pe.wait_ge(x3_ready, s * CHUNKS + c + 1)
                nc.tensor.matmul(ring[:, use % 2, 0:CW], rw1[:], X3[:, c * CW:(c + 1) * CW],
                                 start=True, stop=True).then_inc(ring_full, 1)

            def logits(s):
                pe.wait_ge(ring_act, s * RING_ACT + CHUNKS)
                for t in range(TOKT):
                    mm = nc.tensor.matmul(pB[:, t * EXPERTS:t * EXPERTS + NW], rh[:, t * P:(t + 1) * P], rw2[:],
                                          start=True, stop=True)
                mm.then_inc(pB_full, 1)

            def turn_gates(s, c):
                pe.wait_ge(gates_ready, s + 1)
                if c > 0:
                    pe.wait_ge(gT_ready, s * CHUNKS + c)
                for j in range(CT):
                    mm = nc.tensor.transpose(pB[:, j * P:(j + 1) * P], gates[:, c * CT + j, :], ident[:])
                mm.then_inc(pB_full, 1)

            def experts_up(s, c):
                for m in range(PAIRS):
                    use = USE_FFN + FFN_USES * c + m
                    ring_free(s, use)
                    nc.tensor.matmul(ring[:, use % 2, 0:CW], w1[:, m, :], X3[:, c * CW:(c + 1) * CW],
                                     start=True, stop=True).then_inc(ring_full, 1)
                for m in range(PAIRS):
                    use = USE_FFN + FFN_USES * c + PAIRS + m
                    ring_free(s, use)
                    pe.wait_ge(ring_act, s * RING_ACT + CHUNKS + 2 * PAIRS * c + m + 1)
                    nc.tensor.matmul(ring[:, use % 2, 0:CW], w2[:, m, :], a1[:, m, :],
                                     start=True, stop=True).then_inc(ring_full, 1)

            def experts_down(s, c):
                pe.wait_ge(gT_ready, s * CHUNKS + c + 1)
                for m in range(PAIRS):
                    use = USE_FFN + FFN_USES * c + 2 * PAIRS + m
                    ring_free(s, use)
                    nc.tensor.matmul(ring[:, use % 2, 0:CW], sel[:, m, :], gT[:, c * CW:(c + 1) * CW],
                                     start=True, stop=True).then_inc(ring_full, 1)
                use = USE_FFN + FFN_USES * c + 3 * PAIRS
                ring_free(s, use)
                pe.wait_ge(ring_dve, s * RING_DVE + ring_count("dve", use))
                for j in range(CT):
                    dst = ring[:, use % 2, j * NW:(j + 1) * NW]
                    for m in range(PAIRS):
                        nc.tensor.matmul(dst, a3[:, m, j * P:(j + 1) * P], w3[:, m, :], start=(m == 0), stop=False)
                    t0 = (c * CT + j) * P
                    mm = nc.tensor.matmul(dst, gT[:, t0:t0 + P], b3[:], start=False, stop=True)
                mm.then_inc(ring_full, 1)

            def before(b, s, t, side, nxt):
                if side and t == 2:
                    drive(s, 0)
                if side and t == 3:
                    drive(s, 1)
                    drive(s, 2)
                    mix(s, 0)
                    mix(s, 1)
                if side and t == 7:
                    experts_down(s, 0)
                if nxt and t == 4:
                    offset_turn(b + 1)

            def after(b, s, t, side, nxt):
                if nxt and t == 0:
                    queries(b + 1)
                if side and t == 1:
                    for c in range(CHUNKS):
                        turn_x2(s, c)
                if side and t == 3:
                    mix(s, 2)
                if side and t == 4:
                    for c in range(CHUNKS):
                        turn_x3(s, c)
                    for c in range(CHUNKS):
                        router_hidden(s, c)
                    logits(s)
                if nxt and t == 4:
                    offset_out(b + 1)
                if side and t == 5:
                    experts_up(s, 0)
                if side and t == 6:
                    for c in range(CHUNKS):
                        turn_gates(s, c)
                if side and t == 7:
                    for c in range(1, CHUNKS):
                        experts_up(s, c)
                        experts_down(s, c)

            def start():
                queries(0)
                offset_turn(0)
                offset_out(0)
                turn_samples(0, 0)
                project(0, 0)

            def body(b, par, side, nxt):
                for t in range(TILES):
                    more = nxt or t < TILES - 1
                    if more:
                        turn_samples(TILES * b + t + 1, (t + 1) % TILES)
                    before(b, b - 1, t, side, nxt)
                    if more:
                        project(TILES * b + t + 1, (t + 1) % TILES)
                    after(b, b - 1, t, side, nxt)

            def tail():
                for t in range(TILES):
                    before(BATCH, BATCH - 1, t, True, False)
                    after(BATCH, BATCH - 1, t, True, False)

            schedule(pe, start, body, tail)

        @block.scalar
        def _(act):
            act.wait_ge(consts_in, 16 * len(CONSTS))
            act.wait_ge(cleared, 8)

            def queries_out(b, par):
                for half in range(2):
                    act.wait_ge(pA_full, 4 * b + half + 1)
                    src = pA[:, 0:4 * NW].rearrange("p (t c) -> p t c", c=NW)[:, :, 0:QW]
                    nc.scalar.activation(qo[par][:, 4 * half:4 * half + 4, :], src, ACT.Copy).then_inc(qo_ready, 1)

            def offset_seed(b):
                act.wait_ge(off_var, b + 1)
                nc.scalar.activation(s8b[:], s8a[:], ACT.Ln).then_inc(off_ln, 1)
                act.wait_ge(off_ln, b + 1)
                nc.scalar.activation(s8c[:], s8b[:], ACT.Exp, scale=-0.5).then_inc(off_y, 1)

            def gelu_exponential(b):
                act.wait_ge(gelu_arg, b + 1)
                nc.scalar.activation(o3[:], o2[:], ACT.Exp, scale=-GELU_C).then_inc(gelu_exp, 1)

            def turned_hidden(b):
                act.wait_ge(pA_full, 4 * b + 3)
                nc.scalar.activation(hT[:], pA[:, 0:P], ACT.Copy).then_inc(hT_ready, 1)

            def move_samples(n, t):
                if due(2 * (n - 1)):
                    act.wait_ge(kv_full, 2 * (n - 1))
                for half in range(2):
                    act.wait_ge(t_full, 2 * n + half + 1)
                    nc.scalar.activation(sT[t % 2][:, 4 * half:4 * half + 4, :], tbank[:, half], ACT.Copy).then_inc(t_moved, 1)

            def exponential(n):
                act.wait_ge(shifted_ready, n + 1)
                nc.scalar.activation(probs[:], shifted[:], ACT.Exp, scale=SM_SCALE).then_inc(probs_ready, 1)

            def norm_seed(s, k):
                act.wait_ge(var_ready, 2 * s + k + 1)
                nc.scalar.activation(lnv[k][:], ve[k][:], ACT.Ln).then_inc(ln_done, 1)
                act.wait_ge(ln_done, 2 * s + k + 1)
                nc.scalar.activation(y0[k][:], lnv[k][:], ACT.Exp, scale=-0.5).then_inc(y_ready, 1)

            def normalize1(s, par):
                act.wait_ge(newton_step, s * 8 + 4)
                for t in range(TOKT):
                    src = H[par][:, t, :].unsqueeze(1).to_broadcast([P, 2, CH])
                    nc.scalar.activation(x1n[:, t], src, ACT.Identity, bias=nmr[0][:, t:t + 1],
                                         scale=rstd[0][:, t:t + 1]).then_inc(x1_ready, 1)

            def normalize2(s):
                act.wait_ge(newton_step, s * 8 + 8)
                for t in range(TOKT):
                    nc.scalar.activation(x2n[:, t, 0:CH], h1[:, t, :], ACT.Identity, bias=nmr[1][:, t:t + 1],
                                         scale=rstd[1][:, t:t + 1]).then_inc(x2n_ready, 1)

            def move_x2(s, c):
                act.wait_ge(pB_full, s * 10 + c + 1)
                at = PAD + c * CW
                nc.scalar.activation(X2[0:CH, at:at + CW], pB[0:CH, 0:CW], ACT.Copy).then_inc(x2_low, 1)
                nc.scalar.activation(X2[CH:P, at + 1:at + 1 + CW], pB[CH:P, 0:CW], ACT.Copy).then_inc(x2_ready, 1)

            def move_x3(s, c):
                act.wait_ge(pB_full, s * 10 + CHUNKS + c + 1)
                nc.scalar.activation(X3[0:CH, c * CW:(c + 1) * CW], pB[0:CH, 0:CW], ACT.Copy).then_inc(x3_ready, 1)

            def move_gates(s, c):
                act.wait_ge(pB_full, s * 10 + 2 * CHUNKS + 1 + c + 1)
                nc.scalar.activation(gT[:, c * CW:(c + 1) * CW], pB[:, 0:CW], ACT.Copy).then_inc(gT_ready, 1)

            def router_relu(s, c):
                use = USE_RH + c
                act.wait_ge(ring_full, s * RING + use + 1)
                nc.scalar.activation(rh[:, c * CW:(c + 1) * CW], ring[:, use % 2, 0:CW], ACT.Relu,
                                     bias=rb1[:, 0:1]).then_inc(ring_act, 1)

            def route_exponentials(s):
                act.wait_ge(logits_read, s + 1)
                nc.scalar.activation(r2[:], r1[:], ACT.Exp).then_inc(route_exp, 1)

            def gap_exponential(s):
                act.wait_ge(gap_ready, s + 1)
                nc.scalar.activation(t9b[:], t9a[:], ACT.Exp).then_inc(route_exp, 1)

            def expert_relus(s, c):
                for layer, (dst, bias) in enumerate(((a1, b1), (a2, b2))):
                    for m in range(PAIRS):
                        use = USE_FFN + FFN_USES * c + PAIRS * layer + m
                        act.wait_ge(ring_full, s * RING + use + 1)
                        if layer == 1 and m == 0:
                            act.wait_ge(ring_dve, s * RING_DVE + ring_count("dve", USE_FFN + FFN_USES * c))
                        nc.scalar.activation(dst[:, m, :], ring[:, use % 2, 0:CW], ACT.Relu,
                                             bias=bias[:, m:m + 1]).then_inc(ring_act, 1)

            def early(s, t, side):
                if side and t == 6:
                    gap_exponential(s)

            def late(b, s, par, t, side, nxt):
                if nxt and t == 0:
                    queries_out(b + 1, 1 - par)
                if side and t == 0:
                    norm_seed(s, 0)
                if side and t == 1:
                    normalize1(s, 1 - par)
                    for c in range(CHUNKS):
                        move_x2(s, c)
                if nxt and t == 1:
                    offset_seed(b + 1)
                if nxt and t == 2:
                    gelu_exponential(b + 1)
                if side and t == 3:
                    norm_seed(s, 1)
                if side and t == 4:
                    normalize2(s)
                    for c in range(CHUNKS):
                        move_x3(s, c)
                    for c in range(CHUNKS):
                        router_relu(s, c)
                if nxt and t == 4:
                    turned_hidden(b + 1)
                if side and t == 5:
                    route_exponentials(s)
                    expert_relus(s, 0)
                if side and t == 6:
                    for c in range(CHUNKS):
                        move_gates(s, c)
                if side and t == 7:
                    for c in range(1, CHUNKS):
                        expert_relus(s, c)

            def start():
                queries_out(0, 0)
                offset_seed(0)
                gelu_exponential(0)
                turned_hidden(0)
                move_samples(0, 0)

            def body(b, par, side, nxt):
                for t in range(TILES):
                    if nxt or t < TILES - 1:
                        move_samples(TILES * b + t + 1, (t + 1) % TILES)
                    early(b - 1, t, side)
                    exponential(TILES * b + t)
                    late(b, b - 1, par, t, side, nxt)

            def tail():
                for t in range(TILES):
                    early(BATCH - 1, t, True)
                    late(BATCH, BATCH - 1, 0, t, True, False)

            schedule(act, start, body, tail)

        @block.vector
        def _(dve):
            dve.wait_ge(consts_in, 16 * len(CONSTS))
            dve.wait_ge(cleared, 8)
            V = nc.vector

            V.tensor_scalar(bo2[:], bo2[:], OFFSET_SCALE, None, ALU.mult).then_inc(cleared, 1)
            dve.wait_ge(cleared, 9)
            V.tensor_tensor(ref_pix[:], ref_pix[:], bo2[:].unsqueeze(1).to_broadcast([P, TILES, OFFSETS]),
                            ALU.add).then_inc(cleared, 1)
            dve.wait_ge(cleared, 10)

            full = [P, TILES, OFFCH]

            class Steps:

                def __init__(self, semaphore, base, n):
                    self.semaphore, self.base, self.n = semaphore, base, n

                def __call__(self, ins):
                    self.n += 1
                    ins.then_inc(self.semaphore, 1)
                    dve.wait_ge(self.semaphore, self.base + self.n)

            def weight_corners(b):
                dve.wait_ge(qc_in, 16 * (b + 1))
                V.tensor_tensor(qc[:], qc[:], corner_w[:], ALU.mult).then_inc(qc_weighted, 1)

            def offset_stats(b, par):
                step = Steps(offset_step, b * OFFSET_STEPS, 0)
                dve.wait_ge(qo_ready, 2 * b + 2)
                step(V.tensor_tensor(o1[:], qo[par][:, :, CH:QW], bo1[:].unsqueeze(1).to_broadcast(full), ALU.add))
                step(V.tensor_reduce(s8a[:], o1[:], AX.X, ALU.add))
                step(V.tensor_scalar(s8a[:], s8a[:], 1.0 / OFFCH, None, ALU.mult))
                step(V.tensor_tensor(o1[:], o1[:], s8a[:].unsqueeze(2).to_broadcast(full), ALU.subtract))
                step(V.tensor_tensor(o2[:], o1[:], o1[:], ALU.mult))
                step(V.tensor_reduce(s8d[:], o2[:], AX.X, ALU.add))
                V.tensor_scalar(s8a[:], s8d[:], 1.0 / OFFCH, EPS, ALU.mult, ALU.add).then_inc(off_var, 1)

            def offset_norm(b):
                step = Steps(offset_step, b * OFFSET_STEPS, 6)
                dve.wait_ge(off_var, b + 1)
                dve.wait_ge(off_y, b + 1)
                step(V.scalar_tensor_tensor(s8d[:], s8c[:], -0.5, s8c[:], ALU.mult, ALU.mult))
                step(V.tensor_tensor(s8d[:], s8d[:], s8a[:], ALU.mult))
                step(V.scalar_tensor_tensor(s8d[:], s8d[:], 1.5, s8c[:], ALU.add, ALU.mult))
                step(V.tensor_tensor(o1[:], o1[:], s8d[:].unsqueeze(2).to_broadcast(full), ALU.mult))
                step(V.tensor_tensor(o1[:], o1[:], lng[:].unsqueeze(1).to_broadcast(full), ALU.mult))
                step(V.tensor_tensor(o1[:], o1[:], lnb[:].unsqueeze(1).to_broadcast(full), ALU.add))
                step(V.tensor_tensor(o2[:], o1[:], o1[:], ALU.mult))
                step(V.tensor_scalar(o2[:], o2[:], 0.044715, 1.0, ALU.mult, ALU.add))
                V.tensor_tensor(o2[:], o2[:], o1[:], ALU.mult).then_inc(gelu_arg, 1)

            def offset_gelu(b):
                step = Steps(offset_step, b * OFFSET_STEPS, 14)
                dve.wait_ge(gelu_exp, b + 1)
                step(V.tensor_scalar(o3[:], o3[:], 1.0, None, ALU.add))
                step(V.reciprocal(o3[:], o3[:]))
                V.tensor_tensor(o4[:], o1[:], o3[:], ALU.mult).then_inc(off_h, 1)

            def positions(b, par):
                step = Steps(offset_step, b * OFFSET_STEPS, 16)
                dve.wait_ge(pA_full, 4 * b + 4)
                flat = pix[:].rearrange("p s a -> p (s a)")
                V.scalar_tensor_tensor(flat, pA[:, 0:P], OFFSET_SCALE, ref_pix[:].rearrange("p t o -> p (t o)"),
                                       ALU.mult, ALU.add).then_inc(pix_ready, 1)
                dve.wait_ge(pix_ready, b + 1)
                step(V.tensor_scalar(pix[:], pix[:], 0.0, float(IMG - 1), ALU.max, ALU.min))
                step(V.tensor_scalar(low[:], pix[:], -0.5, ROUND, ALU.add, ALU.add))
                step(V.tensor_scalar(low[:], low[:], ROUND, float(IMG - 2), ALU.subtract, ALU.min))
                step(V.tensor_tensor(hats[:, :, :, 1], pix[:], low[:], ALU.subtract))
                step(V.tensor_scalar(hats[:, :, :, 0], hats[:, :, :, 1], -1.0, 1.0, ALU.mult, ALU.add))
                for x in range(2):
                    out4 = w4[par][:].rearrange("p t (k x y) -> p (t k) x y", x=2, y=2)[:, :, x, :]
                    step(V.tensor_tensor(out4, hats[:, :, 1, :],
                                         hats[:, :, 0, x:x + 1].to_broadcast([P, TILES * POINTS, 2]), ALU.mult))
                step(V.scalar_tensor_tensor(rowf[:], low[:, :, 1], float(IMG), low[:, :, 0], ALU.mult, ALU.add))
                V.tensor_scalar(idx[par][:], rowf[:], batch_row[:, 0:1], None, ALU.add).then_inc(idx_ready, 1)
                dve.wait_ge(idx_ready, b + 1)
                step(V.tensor_scalar(batch_row[:], batch_row[:], float(ROW_PAIRS * IMG), None, ALU.add))
                assert step.n == OFFSET_STEPS

            def weight_samples(n, b, par, t):
                dve.wait_ge(gather_in[t], GATHER * (b + 1))
                view = G[:, t, :].rearrange("p (k c) -> p k c", c=CH)
                V.tensor_tensor(view, view, w4[par][:, t, :].unsqueeze(2).to_broadcast([P, 4 * POINTS, CH]),
                                ALU.mult).then_inc(g_weighted, 1)

            def sum_samples(n, t):
                dve.wait_ge(g_weighted, n + 1)
                if due(2 * (n - 1)):
                    dve.wait_ge(t_full, 2 * (n - 1))
                view = G[:, t, :].rearrange("p (k x c) -> p k x c", x=2, c=2 * CH)
                V.tensor_tensor(g2[t % 2][:], view[:, :, 0, :], view[:, :, 1, :], ALU.add).then_inc(g_summed, 1)

            def scores_of(n, b, par, t):
                dve.wait_ge(kv_full, 2 * n + 2)
                q = qo[par][:, t, 0:CH].unsqueeze(1).to_broadcast([P, POINTS, CH])
                V.tensor_tensor(prodk[:], kv[:, :, 0:CH], q, ALU.mult).then_inc(qk_done, 1)

            def scores_sum(n):
                dve.wait_ge(qk_done, n + 1)
                V.tensor_reduce(scores[:], prodk[:].rearrange("p k (h d) -> p k h d", d=HD), AX.X,
                                ALU.add).then_inc(scores_done, 1)

            def scores_max(n):
                dve.wait_ge(scores_done, n + 1)
                V.tensor_reduce(smax[:], scores[:].rearrange("p k h -> p h k"), AX.X, ALU.max).then_inc(max_done, 1)

            def scores_shift(n):
                dve.wait_ge(max_done, n + 1)
                V.tensor_tensor(shifted[:], scores[:], smax[:].unsqueeze(1).to_broadcast([P, POINTS, HEADS]),
                                ALU.subtract).then_inc(shifted_ready, 1)

            def attend(n):
                dve.wait_ge(probs_ready, n + 1)
                V.tensor_tensor(prodv[:].rearrange("p k (h d) -> p k h d", d=HD),
                                kv[:, :, CH:2 * CH].rearrange("p k (h d) -> p k h d", d=HD),
                                probs[:].unsqueeze(3).to_broadcast([P, POINTS, HEADS, HD]), ALU.mult).then_inc(av_done, 1)
                V.tensor_reduce(den[:], probs[:].rearrange("p k h -> p h k"), AX.X, ALU.add).then_inc(den_done, 1)
                dve.wait_ge(av_done, n + 1)
                V.tensor_reduce(av[:], prodv[:].rearrange("p k c -> p c k"), AX.X, ALU.add).then_inc(avsum_done, 1)
                dve.wait_ge(den_done, n + 1)
                V.reciprocal(rden[:], den[:]).then_inc(rden_done, 1)

            def attended(n, par, t):
                dve.wait_ge(avsum_done, n + 1)
                dve.wait_ge(rden_done, n + 1)
                V.tensor_tensor(H[par][:, t, :].rearrange("p (h d) -> p h d", d=HD),
                                av[:].rearrange("p (h d) -> p h d", d=HD),
                                rden[:].unsqueeze(2).to_broadcast([P, HEADS, HD]), ALU.mult).then_inc(h_ready, 1)

            def norm_stats(s, k, src, mv):
                for t in range(TOKT):
                    V.bn_stats(stats[:, t, :], src[:, t, :]).then_inc(stat_done, 1)
                dve.wait_ge(stat_done, (2 * s + k) * 2 * TOKT + TOKT)
                dve.sem_inc(dve_passed, 1)
                for t in range(TOKT):
                    V.bn_aggr(mv[:, t, :], stats[:, t, :]).then_inc(stat_done, 1)
                dve.wait_ge(stat_done, (2 * s + k + 1) * 2 * TOKT)
                V.tensor_scalar(ve[k][:], mv[:, :, 1], EPS, None, ALU.add).then_inc(var_ready, 1)

            def norm_newton(s, k, mv):
                step = Steps(newton_step, s * 8, 4 * k)
                dve.wait_ge(var_ready, 2 * s + k + 1)
                dve.wait_ge(y_ready, 2 * s + k + 1)
                step(V.scalar_tensor_tensor(ny[k][:], y0[k][:], -0.5, y0[k][:], ALU.mult, ALU.mult))
                step(V.tensor_tensor(ny[k][:], ny[k][:], ve[k][:], ALU.mult))
                step(V.scalar_tensor_tensor(rstd[k][:], ny[k][:], 1.5, y0[k][:], ALU.add, ALU.mult))
                V.scalar_tensor_tensor(nmr[k][:], mv[:, :, 0], -1.0, rstd[k][:], ALU.mult, ALU.mult).then_inc(newton_step, 1)

            def scan(s, c):
                w = min(CW, SEQ - c * CW)
                for v in range(SHALVES):
                    use = c * SHALVES + v
                    dve.wait_ge(ring_full, s * RING + use + 1)
                    if c > 0:
                        dve.wait_ge(ring_dve, s * RING_DVE + use - SHALVES + 1)
                    first = state0[:, v:v + 1] if c == 0 else states[:, v, c * CW - 1:c * CW]
                    V.tensor_tensor_scan(states[:, v, c * CW:c * CW + w], decay[:, v:v + 1].to_broadcast([P, w]),
                                         ring[:, use % 2, 0:w], first, ALU.mult, ALU.add).then_inc(ring_dve, 1)

            def add_mixed(s, par, c):
                use = USE_LDS + c
                dve.wait_ge(ring_full, s * RING + use + 1)
                src = ring[:, use % 2, 0:CT * NW].rearrange("p (t c) -> p t c", c=NW)[:, :, 0:CH]
                V.tensor_tensor(h1[:, c * CT:(c + 1) * CT, :], src, H[par][:, c * CT:(c + 1) * CT, :],
                                ALU.add).then_inc(ring_dve, 1)

            wide = [P, TOKT, EXPERTS]

            def route(s):
                step = Steps(route_step, s * ROUTE_STEPS, 0)

                def spread(x):
                    return x[:].unsqueeze(2).to_broadcast(wide)

                lg = pB[:, 0:TOKT * EXPERTS].rearrange("p (t e) -> p t e", e=EXPERTS)
                dve.wait_ge(pB_full, s * 10 + 2 * CHUNKS + 1)
                step(V.tensor_reduce(t9a[:], lg, AX.X, ALU.max))
                V.tensor_tensor(r1[:], lg, spread(t9a), ALU.subtract).then_inc(logits_read, 1)

            def route_probs(s):
                step = Steps(route_step, s * ROUTE_STEPS, 1)

                def spread(x):
                    return x[:].unsqueeze(2).to_broadcast(wide)

                ranks = rank[:].unsqueeze(1).to_broadcast(wide)
                dve.wait_ge(route_exp, 2 * s + 1)
                step(V.tensor_reduce(t9a[:], r2[:], AX.X, ALU.add))
                step(V.reciprocal(t9a[:], t9a[:]))
                step(V.tensor_tensor(r2[:], r2[:], spread(t9a), ALU.mult))
                step(V.tensor_reduce(t9a[:], r2[:], AX.X, ALU.max))
                step(V.tensor_tensor(r1[:], r2[:], spread(t9a), ALU.is_ge))
                step(V.tensor_tensor(r1[:], r1[:], ranks, ALU.mult))
                step(V.tensor_reduce(t9b[:], r1[:], AX.X, ALU.max))
                step(V.tensor_tensor(top1[:], r1[:], spread(t9b), ALU.is_equal))
                step(V.scalar_tensor_tensor(r3[:], top1[:], -4.0, r2[:], ALU.mult, ALU.add))
                step(V.tensor_reduce(t9b[:], r3[:], AX.X, ALU.max))
                step(V.tensor_tensor(r1[:], r3[:], spread(t9b), ALU.is_ge))
                step(V.tensor_tensor(r1[:], r1[:], ranks, ALU.mult))
                step(V.tensor_reduce(t9c[:], r1[:], AX.X, ALU.max))
                step(V.tensor_tensor(top2[:], r1[:], spread(t9c), ALU.is_equal))
                V.tensor_tensor(t9a[:], t9b[:], t9a[:], ALU.subtract).then_inc(gap_ready, 1)

            def route_gates(s):
                step = Steps(route_step, s * ROUTE_STEPS, 15)

                def spread(x):
                    return x[:].unsqueeze(2).to_broadcast(wide)

                dve.wait_ge(route_exp, 2 * s + 2)
                step(V.tensor_scalar(t9c[:], t9b[:], 1.0, None, ALU.add))
                step(V.reciprocal(t9c[:], t9c[:]))
                step(V.tensor_tensor(r1[:], top2[:], spread(t9b), ALU.mult))
                step(V.tensor_tensor(r1[:], r1[:], top1[:], ALU.add))
                V.tensor_tensor(gates[:, :, 0:EXPERTS], r1[:], spread(t9c), ALU.mult).then_inc(gates_ready, 1)

            def gate_units(s, c):
                for m in range(PAIRS):
                    use = USE_FFN + FFN_USES * c + 2 * PAIRS + m
                    dve.wait_ge(ring_full, s * RING + use + 1)
                    dve.wait_ge(ring_act, s * RING_ACT + CHUNKS + 2 * PAIRS * c + PAIRS + m + 1)
                    V.tensor_tensor(a3[:, m, :], ring[:, use % 2, 0:CW], a2[:, m, :], ALU.mult).then_inc(ring_dve, 1)

            def finish(s, c):
                use = USE_FFN + FFN_USES * c + 3 * PAIRS
                dve.wait_ge(ring_full, s * RING + use + 1)
                if due(s * (32 if c == CHUNKS - 1 else 16)):
                    dve.wait_ge(out_done[c], s * (32 if c == CHUNKS - 1 else 16))
                src = ring[:, use % 2, 0:CT * NW].rearrange("p (t c) -> p t c", c=NW)[:, :, 0:CH]
                V.tensor_tensor(fin[c][:], src, h1[:, c * CT:(c + 1) * CT, :], ALU.add).then_inc(ring_dve, 1)

            def early(b, s, par, t, side, nxt):
                if nxt and t == 0:
                    weight_corners(b + 1)
                if side and t == 1:
                    norm_newton(s, 0, mv1)
                if nxt and t == 2:
                    offset_norm(b + 1)
                if side and t == 3:
                    scan(s, 1)
                    scan(s, 2)
                if side and t == 4:
                    norm_newton(s, 1, mv2)
                if side and t == 5:
                    route(s)
                if side and t == 6:
                    route_gates(s)
                if side and t == 7:
                    gate_units(s, 0)

            def late(b, s, par, t, side, nxt):
                if side and t == 0:
                    dve.wait_ge(txt_in, 16 * (s + 1))
                    dve.wait_ge(h_ready, TILES * (s + 1))
                    norm_stats(s, 0, H[1 - par], mv1)
                if nxt and t == 1:
                    offset_stats(b + 1, 1 - par)
                if side and t == 2:
                    scan(s, 0)
                if nxt and t == 2:
                    offset_gelu(b + 1)
                if side and t == 3:
                    for c in range(CHUNKS):
                        add_mixed(s, 1 - par, c)
                    dve.wait_ge(ring_dve, s * RING_DVE + ring_count("dve", USE_RH))
                    norm_stats(s, 1, h1, mv2)
                if nxt and t == 4:
                    positions(b + 1, 1 - par)
                if side and t == 5:
                    route_probs(s)
                if side and t == 7:
                    finish(s, 0)
                    for c in range(1, CHUNKS):
                        gate_units(s, c)
                        finish(s, c)

            def start():
                weight_corners(0)
                offset_stats(0, 0)
                offset_norm(0)
                offset_gelu(0)
                positions(0, 0)
                weight_samples(0, 0, 0, 0)
                sum_samples(0, 0)
                weight_samples(1, 0, 0, 1)

            def body(b, par, side, nxt):
                for t in range(TILES):
                    n = TILES * b + t
                    scores_of(n, b, par, t)
                    if nxt or t < TILES - 1:
                        sum_samples(n + 1, (t + 1) % TILES)
                    scores_sum(n)
                    early(b, b - 1, par, t, side, nxt)
                    scores_max(n)
                    scores_shift(n)
                    if t < TILES - 2:
                        weight_samples(n + 2, b, par, t + 2)
                    elif nxt:
                        weight_samples(n + 2, b + 1, 1 - par, t + 2 - TILES)
                    attend(n)
                    attended(n, par, t)
                    late(b, b - 1, par, t, side, nxt)

            def tail():
                for t in range(TILES):
                    early(BATCH, BATCH - 1, 0, t, True, False)
                    late(BATCH, BATCH - 1, 0, t, True, False)

            schedule(dve, start, body, tail)


_REF_COORD = np.arange(GRID) * (IMG - 1) / (GRID - 1)
_REF_LOW = np.minimum(np.floor(_REF_COORD), IMG - 2).astype(np.int64)


def _constants():
    hi = _REF_COORD - _REF_LOW
    axis = np.stack([1.0 - hi, hi])
    w = axis[:, None, :, None] * axis[None, :, None, :]
    wtab = np.repeat(w.reshape(2, 2, QUERIES), CH, axis=0).astype(np.float32)
    gy, gx = np.meshgrid(_REF_COORD, _REF_COORD, indexing="ij")
    pix = np.stack([gx.reshape(-1), gy.reshape(-1)], -1).reshape(TILES, P, 1, 2)
    reftab = np.broadcast_to(pix, (TILES, P, HEADS, 2)).reshape(TILES, P, OFFSETS).transpose(1, 0, 2)
    sel = np.zeros((P, PAIRS, P), np.float32)
    for e in range(EXPERTS):
        sel[e, e // 2, (e % 2) * CH:(e % 2 + 1) * CH] = 1.0
    return {
        "wtab": wtab,
        "reftab": np.ascontiguousarray(reftab).astype(np.float32),
        "ident_in": np.eye(P, dtype=np.float32),
        "rank_in": np.broadcast_to(np.arange(EXPERTS, 0, -1, dtype=np.float32), (P, EXPERTS)),
        "sel_in": sel,
    }


def _layout(x, txt, L0_tok_W_q, L0_tok_W_k, L0_tok_W_v, L0_tok_W_o1, L0_tok_b_o1, L0_tok_ln_g,
            L0_tok_ln_b, L0_tok_W_o2, L0_tok_b_o2, L0_attn_h0, L0_attn_A, L0_attn_B, L0_attn_C,
            L0_attn_M, L0_ffn_router_w1, L0_ffn_router_b1, L0_ffn_router_w2, L0_ffn_router_b2,
            L0_ffn_expert_w1, L0_ffn_expert_b1, L0_ffn_expert_w2, L0_ffn_expert_b2,
            L0_ffn_expert_w3, L0_ffn_expert_b3):
    rows = np.ascontiguousarray(x.transpose(0, 2, 3, 1))
    fm = np.empty((BATCH, ROW_PAIRS, IMG, 2, CH), np.float32)
    fm[:, :, :, 0] = rows[:, :-1]
    fm[:, :, :, 1] = rows[:, 1:]
    lo = _REF_LOW
    qcorn = np.empty((BATCH, 2, CH, 2, GRID, GRID), np.float32)
    for yc in range(2):
        for xc in range(2):
            qcorn[:, yc, :, xc] = x[:, :, lo + yc][:, :, :, lo + xc]
    def padded(shape, *parts):
        a = np.zeros(shape, np.float32)
        for at, part in parts:
            a[at] = part
        return a
    s = np.s_
    wqo = padded((2, CH, NW), (s[:, :, :CH], L0_tok_W_q.T), (s[:, :, CH:QW], L0_tok_W_o1)).reshape(P, NW)
    wkv = padded((2, CH, 2 * CH), (s[:, :, :CH], L0_tok_W_k.T), (s[:, :, CH:], L0_tok_W_v.T)).reshape(P, 2 * CH)
    wo2 = padded((TILES, OFFCH, TILES, OFFSETS), *[(s[t, :, t], L0_tok_W_o2) for t in range(TILES)]).reshape(P, P)
    every = lambda v: np.broadcast_to(v, (P,) + v.shape)
    mt = padded((2, CH, TAPS // 2, NW), (s[..., :CH], L0_attn_M.transpose(2, 1, 0).reshape(TAPS // 2, 2, CH, CH).transpose(1, 2, 0, 3)))
    pair = lambda v: v.reshape(PAIRS, P).T
    w1 = padded((P, PAIRS, 2, CH), (s[:CH], L0_ffn_expert_w1.reshape(PAIRS, 2, CH, CH).transpose(2, 0, 1, 3)))
    w2 = padded((2, CH, PAIRS, 2, CH), *[(s[e, :, :, e], L0_ffn_expert_w2[e::2].transpose(1, 0, 2)) for e in range(2)])
    w3 = padded((2, CH, PAIRS, NW), (s[..., :CH], L0_ffn_expert_w3.reshape(PAIRS, 2, CH, CH).transpose(1, 2, 0, 3)))
    return {
        "fm_rows": fm.reshape(-1, 2 * CH),
        "qcorn": qcorn.reshape(BATCH, P, 2, QUERIES),
        "txt": txt,
        "wqo_in": wqo, "wkv_in": wkv, "wo2_in": wo2,
        "bo1_in": every(L0_tok_b_o1), "lng_in": every(L0_tok_ln_g), "lnb_in": every(L0_tok_ln_b),
        "bo2_in": every(L0_tok_b_o2),
        "a_in": L0_attn_A.reshape(SHALVES, P).T, "h0_in": L0_attn_h0.reshape(SHALVES, P).T,
        "bst_in": padded((P, STATES), (s[:CH], L0_attn_B)),
        "cst_in": padded((P, SHALVES, NW), (s[..., :CH], L0_attn_C.reshape(SHALVES, P, CH).transpose(1, 0, 2))),
        "mt_in": mt.reshape(P, TAPS // 2, NW),
        "rw1_in": padded((P, P), (s[:CH, :ROUTER_H], L0_ffn_router_w1)),
        "rb1_in": padded((P, 1), (s[:ROUTER_H, 0], L0_ffn_router_b1), (s[ROUTER_H, 0], 1.0)),
        "rw2_in": padded((P, NW), (s[:ROUTER_H, :EXPERTS], L0_ffn_router_w2), (s[ROUTER_H, :EXPERTS], L0_ffn_router_b2)),
        "w1_in": w1.reshape(P, PAIRS, P), "b1_in": pair(L0_ffn_expert_b1),
        "w2_in": w2.reshape(P, PAIRS, P), "b2_in": pair(L0_ffn_expert_b2),
        "w3_in": w3.reshape(P, PAIRS, NW),
        "b3_in": padded((P, NW), (s[:EXPERTS, :CH], L0_ffn_expert_b3)),
    }


def kernel(**inputs):
    from concourse import bacc
    from concourse.bass_utils import run_bass_kernel_spmd

    arrays = {**_constants(), **_layout(**{k: np.asarray(v) for k, v in inputs.items()})}
    arrays = {f"in_{k}": np.ascontiguousarray(v) for k, v in arrays.items()}
    nc = bacc.Bacc("TRN2", target_bir_lowering=False, num_devices=1)
    args = {k[3:]: nc.dram_tensor(k, a.shape, mybir.dt.from_np(a.dtype), kind="ExternalInput").ap()
            for k, a in arrays.items()}
    out = nc.dram_tensor("out_0", (BATCH, SEQ, CH), F32, kind="ExternalOutput").ap()
    build(nc, out=out, **args)
    r = run_bass_kernel_spmd(nc, [arrays], core_ids=[0])
    return r.results[0]["out_0"]
```

```python
from contextlib import ExitStack

import numpy as np

import concourse.bass as bass
from concourse import mybir

F32 = mybir.dt.float32
U32 = mybir.dt.uint32
ALU = mybir.AluOpType
ACT = mybir.ActivationFunctionType
AX = mybir.AxisListType

P = 128
BATCH, CH, IMG = 16, 64, 128
HEADS, POINTS, HD, DS = 8, 8, 8, 4
GRID = IMG // DS
QUERIES = GRID * GRID
TILES = QUERIES // P
TXT = 77
SEQ = QUERIES + TXT
ROW_PAIRS = IMG - 1
OFFCH = CH // DS
OFFSETS = HEADS * 2
OFFSET_SCALE = 4.0
STATES, TAPS = 256, 10
SHALVES = STATES // P
EXPERTS = 6
PAIRS = EXPERTS // 2
ROUTER_H = CH // 2
TOKT = 9
CHUNKS, CT = 3, 3
CW = CT * P
PADW = TOKT * P
PAD = TAPS
NW = 96
QW = CH + OFFCH
EPS = 1e-5
ROUND = float(3 * 2 ** 22)
GELU_C = 2.0 * float(np.sqrt(2.0 / np.pi))
SM_SCALE = float(HD) ** -0.5
GATHER = 16 * POINTS

RING_USES = [("experts", "hidden", c) for c in range(CHUNKS)]
RING_USES += [("experts", "up0", k) for k in range(2 * PAIRS)]
RING_USES += [("mixer", "drive", k) for k in range(CHUNKS * SHALVES)]
RING_USES += [("experts", "gate0", 0), ("experts", "gate0", 1), ("mixer", "mix", 0),
              ("experts", "gate0", 2), ("mixer", "mix", 1), ("experts", "down", 0), ("mixer", "mix", 2)]
RING_USES += [("experts", "up1", k) for k in range(2 * PAIRS)]
RING_USES += [("experts", "gate1", m) for m in range(PAIRS)]
RING_USES += [("experts", "up2", k) for k in range(2 * PAIRS)]
RING_USES += [("experts", "down", 1)] + [("experts", "gate2", m) for m in range(PAIRS)] + [("experts", "down", 2)]


def reader_of(use):
    return "act" if use[1] == "hidden" or use[1].startswith("up") else "dve"


MIXER_USES = sum(u[0] == "mixer" for u in RING_USES)
EXPERT_USES = len(RING_USES) - MIXER_USES
EXPERT_ACT = sum(reader_of(u) == "act" for u in RING_USES)
EXPERT_DVE = EXPERT_USES - EXPERT_ACT
assert len(RING_USES) % 2 == 0

OFFSET_STEPS = 33
NORM_STEPS = 26
ROUTE_STEPS = 19


def bank(*use):
    return RING_USES.index(use) % 2


def fulls(*use):
    at = RING_USES.index(use)
    return sum(u[0] == use[0] for u in RING_USES[:at + 1])


def reads(*use):
    at = RING_USES.index(use)
    return sum(u[0] == use[0] and reader_of(u) == reader_of(use) for u in RING_USES[:at + 1])


def due(count):
    return not isinstance(count, int) or count > 0


def build(nc, fm_rows, qcorn, txt, wtab, reftab, ident_in, rank_in, wqo_in, wkv_in, bo1_in, lng_in,
          lnb_in, wo2_in, bo2_in, a_in, h0_in, bst_in, cst_in, mt_in, rw1_in, rb1_in, rw2_in,
          w1_in, b1_in, w2_in, b2_in, w3_in, b3_in, sel_in, out):
    with ExitStack() as ctx:
        def sb(name, shape, dt=F32):
            return ctx.enter_context(nc.sbuf_tensor(name, shape, dt))

        def pb(name, shape):
            return ctx.enter_context(nc.psum_tensor(name, shape, F32))

        def sem(name):
            return ctx.enter_context(nc.semaphore(name))

        corner_w = sb("corner_w", [P, 2, QUERIES])
        ref_pix = sb("ref_pix", [P, TILES, OFFSETS])
        ident = sb("ident", [P, P])
        rank = sb("rank", [P, EXPERTS])
        wqo = sb("wqo", [P, NW])
        wkv = sb("wkv", [P, 2 * CH])
        bo1 = sb("bo1", [P, OFFCH])
        lng = sb("lng", [P, OFFCH])
        lnb = sb("lnb", [P, OFFCH])
        wo2 = sb("wo2", [P, P])
        bo2 = sb("bo2", [P, OFFSETS])
        decay = sb("decay", [P, SHALVES])
        state0 = sb("state0", [P, SHALVES])
        bst = sb("bst", [P, STATES])
        cst = sb("cst", [P, SHALVES, NW])
        mt = sb("mt", [P, TAPS // 2, NW])
        rw1 = sb("rw1", [P, P])
        rb1 = sb("rb1", [P, 1])
        rw2 = sb("rw2", [P, NW])
        w1 = sb("w1", [P, PAIRS, P])
        b1 = sb("b1", [P, PAIRS])
        w2 = sb("w2", [P, PAIRS, P])
        b2 = sb("b2", [P, PAIRS])
        w3 = sb("w3", [P, PAIRS, NW])
        b3 = sb("b3", [P, NW])
        sel = sb("sel", [P, PAIRS, P])
        CONSTS = [(corner_w, wtab), (ref_pix, reftab), (ident, ident_in), (rank, rank_in),
                  (wqo, wqo_in), (wkv, wkv_in), (bo1, bo1_in), (lng, lng_in), (lnb, lnb_in),
                  (wo2, wo2_in), (bo2, bo2_in), (decay, a_in), (state0, h0_in), (bst, bst_in),
                  (cst, cst_in), (mt, mt_in), (rw1, rw1_in), (rb1, rb1_in), (rw2, rw2_in),
                  (w1, w1_in), (b1, b1_in), (w2, w2_in), (b2, b2_in), (w3, w3_in), (b3, b3_in),
                  (sel, sel_in)]

        qc = sb("qc", [P, 2, QUERIES])
        qo = [sb(f"qo{k}", [P, TILES, QW]) for k in range(2)]
        o1 = sb("o1", [P, TILES, OFFCH])
        o2 = sb("o2", [P, TILES, OFFCH])
        o3 = sb("o3", [P, TILES, OFFCH])
        o4 = sb("o4", [P, TILES, OFFCH])
        s8a = sb("s8a", [P, TILES])
        s8c = sb("s8c", [P, TILES])
        s8d = sb("s8d", [P, TILES])
        hT = sb("hT", [P, P])
        pix = sb("pix", [P, TILES * POINTS, 2])
        low = sb("low", [P, TILES * POINTS, 2])
        hats = sb("hats", [P, TILES * POINTS, 2, 2])
        w4 = [sb(f"w4_{k}", [P, TILES, POINTS * 4]) for k in range(2)]
        rowf = sb("rowf", [P, TILES * POINTS])
        batch_row = sb("batch_row", [P, 1])
        idx = [sb(f"idx{k}", [P, TILES * POINTS], U32) for k in range(2)]
        G = sb("G", [P, TILES, POINTS * 4 * CH])
        g2 = [sb(f"g2_{k}", [P, POINTS, 2 * CH]) for k in range(2)]
        sT = [sb(f"sT{k}", [P, POINTS, P]) for k in range(2)]
        prodk = sb("prodk", [P, POINTS, CH])
        prodv = sb("prodv", [P, POINTS, CH])
        scores = sb("scores", [P, POINTS, HEADS])
        smax = sb("smax", [P, HEADS])
        shifted = sb("shifted", [P, POINTS, HEADS])
        probs = sb("probs", [P, POINTS, HEADS])
        den = sb("den", [P, HEADS])
        rden = sb("rden", [P, HEADS])
        av = sb("av", [P, CH])
        H = [sb(f"H{k}", [P, TOKT, CH]) for k in range(2)]
        stats = sb("stats", [P, TOKT, 6])
        mv1 = sb("mv1", [P, TOKT, 2])
        mv2 = sb("mv2", [P, TOKT, 2])
        ve = sb("ve", [P, TOKT])
        y0 = sb("y0", [P, TOKT])
        ny = sb("ny", [P, TOKT])
        mark = sb("mark", [P, 1])
        rstd = [sb(f"rstd{k}", [P, TOKT]) for k in range(2)]
        nmr = [sb(f"nmr{k}", [P, TOKT]) for k in range(2)]
        x1n = sb("x1n", [P, TOKT, 2, CH])
        X2 = sb("X2", [P, PAD + PADW + 2])
        states = sb("states", [P, SHALVES, PADW + TAPS])
        h1 = [sb(f"h1_{k}", [P, TOKT, CH]) for k in range(2)]
        x2n = sb("x2n", [P, TOKT, P])
        X3 = sb("X3", [P, PADW])
        rh = sb("rh", [P, PADW])
        r1 = sb("r1", [P, TOKT, EXPERTS])
        r2 = sb("r2", [P, TOKT, EXPERTS])
        r3 = sb("r3", [P, TOKT, EXPERTS])
        top1 = sb("top1", [P, TOKT, EXPERTS])
        top2 = sb("top2", [P, TOKT, EXPERTS])
        t9a = sb("t9a", [P, TOKT])
        t9b = sb("t9b", [P, TOKT])
        t9c = sb("t9c", [P, TOKT])
        gates = sb("gates", [P, TOKT, P])
        gT = sb("gT", [P, PADW])
        a1 = sb("a1", [P, PAIRS, CW])
        a2 = sb("a2", [P, PAIRS, CW])
        a3 = sb("a3", [P, PAIRS, CW])
        fin = [sb(f"fin{k}", [P, CT, CH]) for k in range(CHUNKS)]

        tbank = pb("tbank", [P, 2, 4, P])
        kv = pb("kv", [P, POINTS, 2 * CH])
        pA = pb("pA", [P, 512])
        pB = pb("pB", [P, 512])
        ring = pb("ring", [P, 2, 512])

        consts_in = sem("consts_in")
        cleared = sem("cleared")
        pool_passed = sem("pool_passed")
        dve_passed = sem("dve_passed")
        qc_in = sem("qc_in")
        qc_weighted = sem("qc_weighted")
        pA_full = sem("pA_full")
        qo_ready = sem("qo_ready")
        offset_step = sem("offset_step")
        gelu_arg = sem("gelu_arg")
        gelu_exp = sem("gelu_exp")
        off_h = sem("off_h")
        hT_ready = sem("hT_ready")
        pix_ready = sem("pix_ready")
        idx_ready = sem("idx_ready")
        row_moved = sem("row_moved")
        gather_in = [sem(f"gather_in{t}") for t in range(TILES)]
        g_weighted = sem("g_weighted")
        g_summed = sem("g_summed")
        t_full = sem("t_full")
        t_moved = sem("t_moved")
        kv_full = sem("kv_full")
        qk_done = sem("qk_done")
        scores_done = sem("scores_done")
        max_done = sem("max_done")
        shifted_ready = sem("shifted_ready")
        probs_ready = sem("probs_ready")
        av_done = sem("av_done")
        den_done = sem("den_done")
        avsum_done = sem("avsum_done")
        rden_done = sem("rden_done")
        h_ready = sem("h_ready")
        txt_in = sem("txt_in")
        stat_done = sem("stat_done")
        var_ready = sem("var_ready")
        x1_ready = sem("x1_ready")
        x2_turned = sem("x2_turned")
        x3_turned = sem("x3_turned")
        gates_turned = sem("gates_turned")
        logits_full = sem("logits_full")
        x2_low = sem("x2_low")
        x2_ready = sem("x2_ready")
        norm_step = sem("norm_step")
        norm_ready = sem("norm_ready")
        mixer_full = sem("mixer_full")
        mixer_read = sem("mixer_read")
        expert_full = sem("expert_full")
        expert_act = sem("expert_act")
        expert_dve = sem("expert_dve")
        x2n_ready = sem("x2n_ready")
        x3_ready = sem("x3_ready")
        route_step = sem("route_step")
        logits_read = sem("logits_read")
        route_exp = sem("route_exp")
        gap_ready = sem("gap_ready")
        gates_ready = sem("gates_ready")
        gT_ready = sem("gT_ready")
        out_done = [sem(f"out_done{k}") for k in range(CHUNKS)]

        block = ctx.enter_context(nc.Block())

        def schedule(eng, start, body, tail):
            start()
            body(0, 0, False, False, True)
            body(1, 1, True, False, True)
            body(2, 0, True, True, True)
            with eng.Fori(0, (BATCH - 4) // 2) as i:
                body(2 * i + 3, 1, True, True, True)
                body(2 * i + 4, 0, True, True, True)
            body(BATCH - 1, 1, True, True, False)
            tail()

        @block.sync
        def _(sp):
            for dst, src in CONSTS:
                sp.dma_start(dst[:], src).then_inc(consts_in, 16)

            def load_corners(b):
                if due(2 * b):
                    sp.wait_ge(qo_ready, 2 * b)
                sp.dma_start(qc[:], qcorn[bass.ds(b, 1)].rearrange("o p x q -> p (o x) q")).then_inc(qc_in, 16)

            def load_text(b, par):
                if not (isinstance(b, int) and b == 0):
                    sp.wait_ge(var_ready, b)
                sp.dma_start(H[par][0:TXT, TILES, :], txt[bass.ds(b, 1)].rearrange("o p c -> (o p) c")).then_inc(txt_in, 16)

            def store(f):
                for c in range(CHUNKS):
                    sp.wait_ge(expert_dve, f * EXPERT_DVE + reads("experts", "down", c))
                    dst = out[bass.ds(f, 1), c * CW:min((c + 1) * CW, SEQ), :]
                    if c < CHUNKS - 1:
                        sp.dma_start(dst.rearrange("o (t p) c -> p (o t) c", p=P), fin[c][:]).then_inc(out_done[c], 16)
                    else:
                        full = dst[:, 0:(CT - 1) * P, :]
                        sp.dma_start(full.rearrange("o (t p) c -> p (o t) c", p=P), fin[c][:, 0:CT - 1, :]).then_inc(out_done[c], 16)
                        sp.dma_start(dst[:, (CT - 1) * P:, :].rearrange("o p c -> (o p) c"), fin[c][0:TXT, CT - 1, :]).then_inc(out_done[c], 16)

            def start():
                sp.wait_ge(cleared, 2)
                load_corners(0)

            def body(b, par, mixer, experts, nxt):
                if nxt:
                    load_corners(b + 1)
                load_text(b, par)
                if not isinstance(b, int) or b >= 3:
                    store(b - 3)

            def tail():
                for f in range(BATCH - 3, BATCH):
                    store(f)
                for c in range(CHUNKS):
                    sp.wait_ge(out_done[c], 16 * BATCH * (2 if c == CHUNKS - 1 else 1))

            schedule(sp, start, body, tail)

        @block.gpsimd
        def _(pool):
            nc.gpsimd.memset(H[0][:], 0.0).then_inc(cleared, 1)
            nc.gpsimd.memset(H[1][:], 0.0).then_inc(cleared, 1)
            nc.gpsimd.memset(X2[:], 0.0).then_inc(cleared, 1)
            nc.gpsimd.memset(states[:], 0.0).then_inc(cleared, 1)
            nc.gpsimd.memset(X3[:], 0.0).then_inc(cleared, 1)
            nc.gpsimd.memset(gates[:], 0.0).then_inc(cleared, 1)
            nc.gpsimd.memset(x2n[:], 0.0).then_inc(cleared, 1)
            nc.gpsimd.memset(batch_row[:], 0.0).then_inc(cleared, 1)

            def weight_corners(b):
                pool.wait_ge(qc_in, 16 * (b + 1))
                nc.gpsimd.tensor_tensor(qc[:], qc[:], corner_w[:], ALU.mult).then_inc(qc_weighted, 1)

            def start():
                pool.wait_ge(consts_in, 16 * len(CONSTS))
                weight_corners(0)

            def body(b, par, mixer, experts, nxt):
                if nxt:
                    weight_corners(b + 1)
                pool.wait_ge(idx_ready, b + 1)
                for t in range(TILES):
                    if due((b - 1) * TILES + t + 1):
                        pool.wait_ge(g_summed, (b - 1) * TILES + t + 1)
                    pool.sem_inc(pool_passed, 1)
                    for k in range(POINTS):
                        nc.gpsimd.indirect_dma_start(
                            out=G[:, t, k * 4 * CH:(k + 1) * 4 * CH], out_offset=None, in_=fm_rows,
                            in_offset=bass.IndirectOffsetOnAxis(ap=idx[par][:, t * POINTS + k:t * POINTS + k + 1], axis=0),
                        ).then_inc(gather_in[t], 16)

            schedule(pool, start, body, lambda: None)

        @block.tensor
        def _(pe):
            pe.wait_ge(consts_in, 16 * len(CONSTS))
            pe.wait_ge(cleared, 8)

            def queries(b):
                pe.wait_ge(qc_weighted, b + 1)
                for half in range(2):
                    if half == 0:
                        if due(b):
                            pe.wait_ge(pix_ready, b)
                    else:
                        pe.wait_ge(qo_ready, 2 * b + 1)
                    for j in range(4):
                        t = 4 * half + j
                        for x in range(2):
                            mm = nc.tensor.matmul(pA[:, j * NW:(j + 1) * NW], qc[:, x, t * P:(t + 1) * P], wqo[:],
                                                  start=(x == 0), stop=(x == 1))
                    mm.then_inc(pA_full, 1)

            def offset_turn(b):
                pe.wait_ge(off_h, b + 1)
                nc.tensor.transpose(pA[:, 0:P], o4[:].rearrange("p t c -> p (t c)"), ident[:]).then_inc(pA_full, 1)

            def offset_out(b):
                pe.wait_ge(hT_ready, b + 1)
                nc.tensor.matmul(pA[:, 0:P], hT[:], wo2[:], start=True, stop=True).then_inc(pA_full, 1)

            def turn_samples(n, t):
                pe.wait_ge(g_summed, n + 1)
                for half in range(2):
                    if due(2 * (n - 1) + half + 1):
                        pe.wait_ge(t_moved, 2 * (n - 1) + half + 1)
                    for j in range(4):
                        mm = nc.tensor.transpose(tbank[:, half, j, :], g2[t % 2][:, 4 * half + j, :], ident[:])
                    mm.then_inc(t_full, 1)

            def project(n, t):
                if due(n):
                    pe.wait_ge(av_done, n)
                for half in range(2):
                    pe.wait_ge(t_moved, 2 * n + half + 1)
                    for j in range(4):
                        k = 4 * half + j
                        mm = nc.tensor.matmul(kv[:, k, :], sT[t % 2][:, k, :], wkv[:], start=True, stop=True)
                    mm.then_inc(kv_full, 1)

            def ring_free(use, s, f, mixer, experts):
                at = RING_USES.index(use) - 2
                while at >= 0 and not (mixer if RING_USES[at][0] == "mixer" else experts):
                    at -= 2
                if at < 0:
                    if due(f * EXPERT_DVE):
                        pe.wait_ge(expert_dve, f * EXPERT_DVE)
                elif RING_USES[at][0] == "mixer":
                    pe.wait_ge(mixer_read, s * MIXER_USES + reads(*RING_USES[at]))
                elif reader_of(RING_USES[at]) == "act":
                    pe.wait_ge(expert_act, f * EXPERT_ACT + reads(*RING_USES[at]))
                else:
                    pe.wait_ge(expert_dve, f * EXPERT_DVE + reads(*RING_USES[at]))

            def turn_x2(s, c):
                pe.wait_ge(x1_ready, s * TOKT + CT * (c + 1))
                if c == 0:
                    if due(s):
                        pe.wait_ge(logits_read, s)
                else:
                    pe.wait_ge(x2_ready, s * CHUNKS + c)
                for j in range(CT):
                    mm = nc.tensor.transpose(pB[:, j * P:(j + 1) * P], x1n[:, c * CT + j].rearrange("p a c -> p (a c)"), ident[:])
                mm.then_inc(x2_turned, 1)

            def drive(go, s, c):
                pe.wait_ge(x2_ready, s * CHUNKS + c + 1)
                w = min(CW, SEQ - c * CW)
                for v in range(SHALVES):
                    use = ("mixer", "drive", c * SHALVES + v)
                    ring_free(use, *go)
                    nc.tensor.matmul(ring[:, bank(*use), 0:w], bst[:, v * P:(v + 1) * P],
                                     X2[:, PAD + c * CW:PAD + c * CW + w], start=True, stop=True).then_inc(mixer_full, 1)

            def mix(go, s, c):
                use = ("mixer", "mix", c)
                ring_free(use, *go)
                pe.wait_ge(mixer_read, s * MIXER_USES + SHALVES * min(c + 2, CHUNKS))
                for j in range(CT):
                    t0 = (c * CT + j) * P
                    dst = ring[:, bank(*use), j * NW:(j + 1) * NW]
                    for i in range(TAPS // 2):
                        at = PAD + t0 - 2 * i
                        nc.tensor.matmul(dst, X2[:, at:at + P], mt[:, i, :], start=(i == 0), stop=False)
                    for v in range(SHALVES):
                        mm = nc.tensor.matmul(dst, states[:, v, t0 + TAPS:t0 + TAPS + P], cst[:, v, :],
                                              start=False, stop=(v == SHALVES - 1))
                mm.then_inc(mixer_full, 1)

            def turn_x3(f, c):
                pe.wait_ge(x2n_ready, f * TOKT + CT * (c + 1))
                if c == 0:
                    if due(f * CHUNKS):
                        pe.wait_ge(gT_ready, f * CHUNKS)
                else:
                    pe.wait_ge(x3_ready, f * CHUNKS + c)
                for j in range(CT):
                    mm = nc.tensor.transpose(pB[:, j * P:(j + 1) * P], x2n[:, c * CT + j, :], ident[:])
                mm.then_inc(x3_turned, 1)

            def router_hidden(go, f, c):
                use = ("experts", "hidden", c)
                ring_free(use, *go)
                pe.wait_ge(x3_ready, f * CHUNKS + c + 1)
                nc.tensor.matmul(ring[:, bank(*use), 0:CW], rw1[:], X3[:, c * CW:(c + 1) * CW],
                                 start=True, stop=True).then_inc(expert_full, 1)

            def logits(f):
                pe.wait_ge(x3_ready, (f + 1) * CHUNKS)
                pe.wait_ge(expert_act, f * EXPERT_ACT + CHUNKS)
                for t in range(TOKT):
                    mm = nc.tensor.matmul(pB[:, t * EXPERTS:t * EXPERTS + NW], rh[:, t * P:(t + 1) * P], rw2[:],
                                          start=True, stop=True)
                mm.then_inc(logits_full, 1)

            def turn_gates(s, f, c, mixer):
                pe.wait_ge(gates_ready, f + 1)
                if c > 0:
                    pe.wait_ge(gT_ready, f * CHUNKS + c)
                elif mixer:
                    pe.wait_ge(x2_ready, (s + 1) * CHUNKS)
                for j in range(CT):
                    mm = nc.tensor.transpose(pB[:, j * P:(j + 1) * P], gates[:, c * CT + j, :], ident[:])
                mm.then_inc(gates_turned, 1)

            def experts_up(go, f, c):
                for m in range(PAIRS):
                    use = ("experts", f"up{c}", m)
                    ring_free(use, *go)
                    nc.tensor.matmul(ring[:, bank(*use), 0:CW], w1[:, m, :], X3[:, c * CW:(c + 1) * CW],
                                     start=True, stop=True).then_inc(expert_full, 1)
                for m in range(PAIRS):
                    use = ("experts", f"up{c}", PAIRS + m)
                    ring_free(use, *go)
                    pe.wait_ge(expert_act, f * EXPERT_ACT + reads("experts", f"up{c}", m))
                    nc.tensor.matmul(ring[:, bank(*use), 0:CW], w2[:, m, :], a1[:, m, :],
                                     start=True, stop=True).then_inc(expert_full, 1)

            def spread_gates(go, f, c, pairs):
                pe.wait_ge(gT_ready, f * CHUNKS + c + 1)
                for m in pairs:
                    use = ("experts", f"gate{c}", m)
                    ring_free(use, *go)
                    nc.tensor.matmul(ring[:, bank(*use), 0:CW], sel[:, m, :], gT[:, c * CW:(c + 1) * CW],
                                     start=True, stop=True).then_inc(expert_full, 1)

            def experts_down(go, f, c):
                use = ("experts", "down", c)
                ring_free(use, *go)
                pe.wait_ge(expert_dve, f * EXPERT_DVE + reads("experts", f"gate{c}", PAIRS - 1))
                for j in range(CT):
                    dst = ring[:, bank(*use), j * NW:(j + 1) * NW]
                    for m in range(PAIRS):
                        nc.tensor.matmul(dst, a3[:, m, j * P:(j + 1) * P], w3[:, m, :], start=(m == 0), stop=False)
                    t0 = (c * CT + j) * P
                    mm = nc.tensor.matmul(dst, gT[:, t0:t0 + P], b3[:], start=False, stop=True)
                mm.then_inc(expert_full, 1)

            def first(go, f, t, experts):
                if experts and t == 0:
                    for c in range(CHUNKS):
                        turn_x3(f, c)
                    for c in range(CHUNKS):
                        router_hidden(go, f, c)

            def before(go, b, s, f, t, mixer, experts, nxt):
                if experts and t == 0:
                    logits(f)
                if experts and t == 1:
                    experts_up(go, f, 0)
                if mixer and t == 2:
                    for c in range(CHUNKS):
                        turn_x2(s, c)
                if nxt and t == 3:
                    offset_turn(b + 1)
                if experts and t == 3:
                    for c in range(CHUNKS):
                        turn_gates(s, f, c, mixer)
                    spread_gates(go, f, 0, (0, 1))
                if experts and t == 4:
                    spread_gates(go, f, 0, (2,))
                if mixer and t == 4:
                    mix(go, s, 1)
                if mixer and t == 5:
                    mix(go, s, 2)
                if experts and t == 6:
                    spread_gates(go, f, 1, (0, 1))
                if experts and t == 7:
                    experts_up(go, f, 2)

            def after(go, b, s, f, t, mixer, experts, nxt):
                if nxt and t == 0:
                    queries(b + 1)
                if mixer and t == 2:
                    for c in range(CHUNKS):
                        drive(go, s, c)
                if nxt and t == 3:
                    offset_out(b + 1)
                if mixer and t == 3:
                    mix(go, s, 0)
                if experts and t == 4:
                    experts_down(go, f, 0)
                if experts and t == 5:
                    experts_up(go, f, 1)
                if experts and t == 6:
                    spread_gates(go, f, 1, (2,))
                if experts and t == 7:
                    experts_down(go, f, 1)
                    spread_gates(go, f, 2, (0, 1, 2))
                    experts_down(go, f, 2)

            def start():
                queries(0)
                offset_turn(0)
                offset_out(0)
                turn_samples(0, 0)
                project(0, 0)

            def body(b, par, mixer, experts, nxt):
                go = (b - 1, b - 2, mixer, experts)
                for t in range(TILES):
                    more = nxt or t < TILES - 1
                    first(go, b - 2, t, experts)
                    if more:
                        turn_samples(TILES * b + t + 1, (t + 1) % TILES)
                    before(go, b, b - 1, b - 2, t, mixer, experts, nxt)
                    if more:
                        project(TILES * b + t + 1, (t + 1) % TILES)
                    after(go, b, b - 1, b - 2, t, mixer, experts, nxt)

            def tail():
                for b, mixer in ((BATCH, True), (BATCH + 1, False)):
                    go = (b - 1, b - 2, mixer, True)
                    for t in range(TILES):
                        first(go, b - 2, t, True)
                        before(go, b, b - 1, b - 2, t, mixer, True, False)
                        after(go, b, b - 1, b - 2, t, mixer, True, False)

            schedule(pe, start, body, tail)

        @block.scalar
        def _(act):
            act.wait_ge(consts_in, 16 * len(CONSTS))
            act.wait_ge(cleared, 8)

            def queries_out(b, par):
                for half in range(2):
                    act.wait_ge(pA_full, 4 * b + half + 1)
                    src = pA[:, 0:4 * NW].rearrange("p (t c) -> p t c", c=NW)[:, :, 0:QW]
                    nc.scalar.activation(qo[par][:, 4 * half:4 * half + 4, :], src, ACT.Copy).then_inc(qo_ready, 1)

            def gelu_exponential(b):
                act.wait_ge(gelu_arg, b + 1)
                nc.scalar.activation(o3[:], o2[:], ACT.Exp, scale=-GELU_C).then_inc(gelu_exp, 1)

            def turned_hidden(b):
                act.wait_ge(pA_full, 4 * b + 3)
                nc.scalar.activation(hT[:], pA[:, 0:P], ACT.Copy).then_inc(hT_ready, 1)

            def move_samples(n, t):
                if due(2 * (n - 1)):
                    act.wait_ge(kv_full, 2 * (n - 1))
                for half in range(2):
                    act.wait_ge(t_full, 2 * n + half + 1)
                    nc.scalar.activation(sT[t % 2][:, 4 * half:4 * half + 4, :], tbank[:, half], ACT.Copy).then_inc(t_moved, 1)

            def exponential(n):
                act.wait_ge(shifted_ready, n + 1)
                nc.scalar.activation(probs[:], shifted[:], ACT.Exp, scale=SM_SCALE).then_inc(probs_ready, 1)

            def normalize1(s, par):
                act.wait_ge(norm_ready, 2 * s + 1)
                for t in range(TOKT):
                    src = H[par][:, t, :].unsqueeze(1).to_broadcast([P, 2, CH])
                    nc.scalar.activation(x1n[:, t], src, ACT.Identity, bias=nmr[0][:, t:t + 1],
                                         scale=rstd[0][:, t:t + 1]).then_inc(x1_ready, 1)

            def normalize2(s, par):
                act.wait_ge(norm_ready, 2 * s + 2)
                for t in range(TOKT):
                    nc.scalar.activation(x2n[:, t, 0:CH], h1[par][:, t, :], ACT.Identity, bias=nmr[1][:, t:t + 1],
                                         scale=rstd[1][:, t:t + 1]).then_inc(x2n_ready, 1)

            def move_x2(s, c):
                act.wait_ge(x2_turned, s * CHUNKS + c + 1)
                at = PAD + c * CW
                nc.scalar.activation(X2[0:CH, at:at + CW], pB[0:CH, 0:CW], ACT.Copy).then_inc(x2_low, 1)
                nc.scalar.activation(X2[CH:P, at + 1:at + 1 + CW], pB[CH:P, 0:CW], ACT.Copy).then_inc(x2_ready, 1)

            def move_x3(f, c):
                act.wait_ge(x3_turned, f * CHUNKS + c + 1)
                nc.scalar.activation(X3[0:CH, c * CW:(c + 1) * CW], pB[0:CH, 0:CW], ACT.Copy).then_inc(x3_ready, 1)

            def move_gates(f, c):
                act.wait_ge(gates_turned, f * CHUNKS + c + 1)
                nc.scalar.activation(gT[:, c * CW:(c + 1) * CW], pB[:, 0:CW], ACT.Copy).then_inc(gT_ready, 1)

            def router_relu(f, c):
                use = ("experts", "hidden", c)
                act.wait_ge(expert_full, f * EXPERT_USES + fulls(*use))
                nc.scalar.activation(rh[:, c * CW:(c + 1) * CW], ring[:, bank(*use), 0:CW], ACT.Relu,
                                     bias=rb1[:, 0:1]).then_inc(expert_act, 1)

            def route_exponentials(f):
                act.wait_ge(logits_read, f + 1)
                nc.scalar.activation(r2[:], r1[:], ACT.Exp).then_inc(route_exp, 1)

            def gap_exponential(f):
                act.wait_ge(gap_ready, f + 1)
                nc.scalar.activation(t9b[:], t9a[:], ACT.Exp).then_inc(route_exp, 1)

            def expert_relus(f, c):
                for layer, (dst, bias) in enumerate(((a1, b1), (a2, b2))):
                    for m in range(PAIRS):
                        use = ("experts", f"up{c}", PAIRS * layer + m)
                        act.wait_ge(expert_full, f * EXPERT_USES + fulls(*use))
                        nc.scalar.activation(dst[:, m, :], ring[:, bank(*use), 0:CW], ACT.Relu,
                                             bias=bias[:, m:m + 1]).then_inc(expert_act, 1)

            def first(f, t, experts):
                if experts and t == 0:
                    for c in range(CHUNKS):
                        move_x3(f, c)
                    for c in range(CHUNKS):
                        router_relu(f, c)

            def late(b, s, f, par, t, mixer, experts, nxt):
                if nxt and t == 0:
                    queries_out(b + 1, 1 - par)
                if experts and t == 1:
                    route_exponentials(f)
                    expert_relus(f, 0)
                if mixer and t == 1:
                    normalize1(s, 1 - par)
                if mixer and t == 2:
                    for c in range(CHUNKS):
                        move_x2(s, c)
                if nxt and t == 2:
                    gelu_exponential(b + 1)
                if experts and t == 2:
                    gap_exponential(f)
                if nxt and t == 3:
                    turned_hidden(b + 1)
                if experts and t == 3:
                    for c in range(CHUNKS):
                        move_gates(f, c)
                if experts and t == 5:
                    expert_relus(f, 1)
                if experts and t == 7:
                    expert_relus(f, 2)
                if mixer and t == 7:
                    normalize2(s, 1 - par)

            def start():
                queries_out(0, 0)
                gelu_exponential(0)
                turned_hidden(0)
                move_samples(0, 0)

            def body(b, par, mixer, experts, nxt):
                for t in range(TILES):
                    first(b - 2, t, experts)
                    if nxt or t < TILES - 1:
                        move_samples(TILES * b + t + 1, (t + 1) % TILES)
                    exponential(TILES * b + t)
                    late(b, b - 1, b - 2, par, t, mixer, experts, nxt)

            def tail():
                for b, mixer in ((BATCH, True), (BATCH + 1, False)):
                    for t in range(TILES):
                        first(b - 2, t, True)
                        late(b, b - 1, b - 2, b % 2, t, mixer, True, False)

            schedule(act, start, body, tail)

        @block.vector
        def _(dve):
            dve.wait_ge(consts_in, 16 * len(CONSTS))
            dve.wait_ge(cleared, 8)
            V = nc.vector

            V.tensor_scalar(bo2[:], bo2[:], OFFSET_SCALE, None, ALU.mult).then_inc(cleared, 1)
            dve.wait_ge(cleared, 9)
            V.tensor_tensor(ref_pix[:], ref_pix[:], bo2[:].unsqueeze(1).to_broadcast([P, TILES, OFFSETS]),
                            ALU.add).then_inc(cleared, 1)
            dve.wait_ge(cleared, 10)

            full = [P, TILES, OFFCH]

            class Steps:

                def __init__(self, base, n):
                    self.base, self.n = base, n

                def count(self):
                    return self.base + self.n

                def next(self):
                    self.n += 1

            def rsqrt(step, semaphore, y, u, v):
                I32 = mybir.dt.int32
                dve.wait_ge(semaphore, step.count())
                V.tensor_scalar(u.bitcast(I32), v.bitcast(I32), 1, None, ALU.logical_shift_right).then_inc(semaphore, 1)
                step.next()
                yield
                dve.wait_ge(semaphore, step.count())
                V.tensor_scalar(y.bitcast(I32), u.bitcast(I32), -1.0, float(0x5F375A00), ALU.mult, ALU.add).then_inc(semaphore, 1)
                step.next()
                yield
                for _ in range(3):
                    dve.wait_ge(semaphore, step.count())
                    V.scalar_tensor_tensor(u, y, -0.5, y, ALU.mult, ALU.mult).then_inc(semaphore, 1)
                    step.next()
                    yield
                    dve.wait_ge(semaphore, step.count())
                    V.tensor_tensor(u, u, v, ALU.mult).then_inc(semaphore, 1)
                    step.next()
                    yield
                    dve.wait_ge(semaphore, step.count())
                    V.scalar_tensor_tensor(y, u, 1.5, y, ALU.add, ALU.mult).then_inc(semaphore, 1)
                    step.next()
                    yield


            def offset_norm(b, par):
                step = Steps(b * OFFSET_STEPS, 0)

                def chain(ins):
                    ins.then_inc(offset_step, 1)
                    step.next()

                dve.wait_ge(qo_ready, 2 * b + 2)
                chain(V.tensor_tensor(o1[:], qo[par][:, :, CH:QW], bo1[:].unsqueeze(1).to_broadcast(full), ALU.add))
                yield
                dve.wait_ge(offset_step, step.count())
                chain(V.tensor_reduce(s8a[:], o1[:], AX.X, ALU.add))
                yield
                dve.wait_ge(offset_step, step.count())
                chain(V.tensor_scalar(s8a[:], s8a[:], 1.0 / OFFCH, None, ALU.mult))
                yield
                dve.wait_ge(offset_step, step.count())
                chain(V.tensor_tensor(o1[:], o1[:], s8a[:].unsqueeze(2).to_broadcast(full), ALU.subtract))
                yield
                dve.wait_ge(offset_step, step.count())
                chain(V.tensor_tensor(o2[:], o1[:], o1[:], ALU.mult))
                yield
                dve.wait_ge(offset_step, step.count())
                chain(V.tensor_reduce(s8d[:], o2[:], AX.X, ALU.add))
                yield
                dve.wait_ge(offset_step, step.count())
                chain(V.tensor_scalar(s8a[:], s8d[:], 1.0 / OFFCH, EPS, ALU.mult, ALU.add))
                yield
                yield from rsqrt(step, offset_step, s8c[:], s8d[:], s8a[:])
                dve.wait_ge(offset_step, step.count())
                chain(V.tensor_tensor(o1[:], o1[:], s8c[:].unsqueeze(2).to_broadcast(full), ALU.mult))
                yield
                dve.wait_ge(offset_step, step.count())
                chain(V.tensor_tensor(o1[:], o1[:], lng[:].unsqueeze(1).to_broadcast(full), ALU.mult))
                yield
                dve.wait_ge(offset_step, step.count())
                chain(V.tensor_tensor(o1[:], o1[:], lnb[:].unsqueeze(1).to_broadcast(full), ALU.add))
                yield
                dve.wait_ge(offset_step, step.count())
                chain(V.tensor_tensor(o2[:], o1[:], o1[:], ALU.mult))
                yield
                dve.wait_ge(offset_step, step.count())
                chain(V.tensor_scalar(o2[:], o2[:], 0.044715, 1.0, ALU.mult, ALU.add))
                yield
                dve.wait_ge(offset_step, step.count())
                V.tensor_tensor(o2[:], o2[:], o1[:], ALU.mult).then_inc(gelu_arg, 1)
                assert step.n == 23
                yield

            def offset_gelu(b):
                dve.wait_ge(gelu_exp, b + 1)
                V.tensor_scalar(o3[:], o3[:], 1.0, None, ALU.add).then_inc(offset_step, 1)
                yield
                dve.wait_ge(offset_step, b * OFFSET_STEPS + 24)
                V.reciprocal(o3[:], o3[:]).then_inc(offset_step, 1)
                yield
                dve.wait_ge(offset_step, b * OFFSET_STEPS + 25)
                V.tensor_tensor(o4[:], o1[:], o3[:], ALU.mult).then_inc(off_h, 1)
                yield

            def positions(b, par):
                step = Steps(b * OFFSET_STEPS, 25)

                def chain(ins):
                    ins.then_inc(offset_step, 1)
                    step.next()

                dve.wait_ge(pA_full, 4 * b + 4)
                V.scalar_tensor_tensor(pix[:].rearrange("p s a -> p (s a)"), pA[:, 0:P], OFFSET_SCALE,
                                       ref_pix[:].rearrange("p t o -> p (t o)"), ALU.mult, ALU.add).then_inc(pix_ready, 1)
                yield
                dve.wait_ge(pix_ready, b + 1)
                chain(V.tensor_scalar(pix[:], pix[:], 0.0, float(IMG - 1), ALU.max, ALU.min))
                yield
                dve.wait_ge(offset_step, step.count())
                chain(V.tensor_scalar(low[:], pix[:], -0.5, ROUND, ALU.add, ALU.add))
                yield
                dve.wait_ge(offset_step, step.count())
                chain(V.tensor_scalar(low[:], low[:], ROUND, float(IMG - 2), ALU.subtract, ALU.min))
                yield
                dve.wait_ge(offset_step, step.count())
                chain(V.scalar_tensor_tensor(rowf[:], low[:, :, 1], float(IMG), low[:, :, 0], ALU.mult, ALU.add))
                yield
                chain(V.tensor_tensor(hats[:, :, :, 1], pix[:], low[:], ALU.subtract))
                yield
                dve.wait_ge(offset_step, step.count())
                if due(b):
                    dve.wait_ge(row_moved, b)
                V.tensor_scalar(idx[par][:], rowf[:], batch_row[:, 0:1], None, ALU.add).then_inc(idx_ready, 1)
                yield
                chain(V.tensor_scalar(hats[:, :, :, 0], hats[:, :, :, 1], -1.0, 1.0, ALU.mult, ALU.add))
                yield
                for x in range(2):
                    out4 = w4[par][:].rearrange("p t (k x y) -> p (t k) x y", x=2, y=2)[:, :, x, :]
                    dve.wait_ge(offset_step, step.count())
                    chain(V.tensor_tensor(out4, hats[:, :, 1, :],
                                          hats[:, :, 0, x:x + 1].to_broadcast([P, TILES * POINTS, 2]), ALU.mult))
                    yield
                dve.wait_ge(idx_ready, b + 1)
                V.tensor_scalar(batch_row[:], batch_row[:], float(ROW_PAIRS * IMG), None, ALU.add).then_inc(row_moved, 1)
                assert step.n == OFFSET_STEPS
                yield

            def weight_samples(n, b, par, t):
                dve.wait_ge(gather_in[t], GATHER * (b + 1))
                dve.wait_ge(offset_step, (b + 1) * OFFSET_STEPS)
                view = G[:, t, :].rearrange("p (k c) -> p k c", c=CH)
                V.tensor_tensor(view, view, w4[par][:, t, :].unsqueeze(2).to_broadcast([P, 4 * POINTS, CH]),
                                ALU.mult).then_inc(g_weighted, 1)

            def sum_samples(n, t):
                dve.wait_ge(g_weighted, n + 1)
                if due(2 * (n - 1)):
                    dve.wait_ge(t_full, 2 * (n - 1))
                view = G[:, t, :].rearrange("p (k x c) -> p k x c", x=2, c=2 * CH)
                V.tensor_tensor(g2[t % 2][:], view[:, :, 0, :], view[:, :, 1, :], ALU.add).then_inc(g_summed, 1)

            def scores_of(n, b, par, t):
                dve.wait_ge(kv_full, 2 * n + 2)
                q = qo[par][:, t, 0:CH].unsqueeze(1).to_broadcast([P, POINTS, CH])
                V.tensor_tensor(prodk[:], kv[:, :, 0:CH], q, ALU.mult).then_inc(qk_done, 1)

            def scores_sum(n):
                dve.wait_ge(qk_done, n + 1)
                V.tensor_reduce(scores[:], prodk[:].rearrange("p k (h d) -> p k h d", d=HD), AX.X,
                                ALU.add).then_inc(scores_done, 1)

            def scores_max(n):
                dve.wait_ge(scores_done, n + 1)
                V.tensor_reduce(smax[:], scores[:].rearrange("p k h -> p h k"), AX.X, ALU.max).then_inc(max_done, 1)

            def scores_shift(n):
                dve.wait_ge(max_done, n + 1)
                V.tensor_tensor(shifted[:], scores[:], smax[:].unsqueeze(1).to_broadcast([P, POINTS, HEADS]),
                                ALU.subtract).then_inc(shifted_ready, 1)

            def attend(n):
                dve.wait_ge(probs_ready, n + 1)
                V.tensor_tensor(prodv[:].rearrange("p k (h d) -> p k h d", d=HD),
                                kv[:, :, CH:2 * CH].rearrange("p k (h d) -> p k h d", d=HD),
                                probs[:].unsqueeze(3).to_broadcast([P, POINTS, HEADS, HD]), ALU.mult).then_inc(av_done, 1)
                V.tensor_reduce(den[:], probs[:].rearrange("p k h -> p h k"), AX.X, ALU.add).then_inc(den_done, 1)

            def attend_sum(n):
                dve.wait_ge(av_done, n + 1)
                V.tensor_reduce(av[:], prodv[:].rearrange("p k c -> p c k"), AX.X, ALU.add).then_inc(avsum_done, 1)

            def attend_recip(n):
                dve.wait_ge(den_done, n + 1)
                V.reciprocal(rden[:], den[:]).then_inc(rden_done, 1)

            def attended(n, par, t):
                dve.wait_ge(avsum_done, n + 1)
                dve.wait_ge(rden_done, n + 1)
                V.tensor_tensor(H[par][:, t, :].rearrange("p (h d) -> p h d", d=HD),
                                av[:].rearrange("p (h d) -> p h d", d=HD),
                                rden[:].unsqueeze(2).to_broadcast([P, HEADS, HD]), ALU.mult).then_inc(h_ready, 1)

            def norm1_stats(s, par):
                dve.wait_ge(txt_in, 16 * (s + 1))
                dve.wait_ge(h_ready, TILES * (s + 1))
                for t in range(TOKT):
                    V.bn_stats(stats[:, t, :], H[par][:, t, :]).then_inc(stat_done, 1)
                    yield
                dve.wait_ge(stat_done, 4 * s * TOKT + TOKT)
                dve.sem_inc(dve_passed, 1)
                for t in range(TOKT):
                    V.bn_aggr(mv1[:, t, :], stats[:, t, :]).then_inc(stat_done, 1)
                    yield

            def norm2_stats(s, par, tiles):
                for t in tiles:
                    if t % CT == 0:
                        dve.wait_ge(mixer_read, s * MIXER_USES + reads("mixer", "mix", t // CT))
                    V.bn_stats(stats[:, t, :], h1[par][:, t, :]).then_inc(stat_done, 1)
                    yield
                if tiles[-1] == TOKT - 1:
                    dve.wait_ge(stat_done, 4 * s * TOKT + 3 * TOKT)
                    dve.sem_inc(dve_passed, 1)
                    for t in range(TOKT):
                        V.bn_aggr(mv2[:, t, :], stats[:, t, :]).then_inc(stat_done, 1)
                        yield

            def norm_scale(s, k, mv):
                step = Steps(s * NORM_STEPS, 13 * k)
                dve.wait_ge(stat_done, 4 * s * TOKT + 2 * (k + 1) * TOKT)
                V.tensor_scalar(ve[:], mv[:, :, 1], EPS, None, ALU.add).then_inc(norm_step, 1)
                step.next()
                if k == 0:
                    dve.wait_ge(norm_step, step.count())
                    V.tensor_copy(mark[:], ve[:, 0:1]).then_inc(var_ready, 1)
                yield
                yield from rsqrt(step, norm_step, y0[:], ny[:], ve[:])
                dve.wait_ge(norm_step, step.count())
                V.tensor_copy(rstd[k][:], y0[:]).then_inc(norm_step, 1)
                step.next()
                yield
                V.scalar_tensor_tensor(nmr[k][:], mv[:, :, 0], -1.0, y0[:], ALU.mult, ALU.mult).then_inc(norm_ready, 1)
                yield

            def scan(s, c):
                w = min(CW, SEQ - c * CW)
                for v in range(SHALVES):
                    use = ("mixer", "drive", c * SHALVES + v)
                    dve.wait_ge(mixer_full, s * MIXER_USES + fulls(*use))
                    if c > 0:
                        dve.wait_ge(mixer_read, s * MIXER_USES + reads(*use) - SHALVES)
                    lead = state0[:, v:v + 1] if c == 0 else states[:, v, c * CW - 1:c * CW]
                    V.tensor_tensor_scan(states[:, v, c * CW:c * CW + w], decay[:, v:v + 1].to_broadcast([P, w]),
                                         ring[:, bank(*use), 0:w], lead, ALU.mult, ALU.add).then_inc(mixer_read, 1)
                    yield

            def add_mixed(s, par, c):
                use = ("mixer", "mix", c)
                dve.wait_ge(mixer_full, s * MIXER_USES + fulls(*use))
                src = ring[:, bank(*use), 0:CT * NW].rearrange("p (t c) -> p t c", c=NW)[:, :, 0:CH]
                V.tensor_tensor(h1[par][:, c * CT:(c + 1) * CT, :], src, H[par][:, c * CT:(c + 1) * CT, :],
                                ALU.add).then_inc(mixer_read, 1)
                yield

            wide = [P, TOKT, EXPERTS]

            def spread(x):
                return x[:].unsqueeze(2).to_broadcast(wide)

            def route_shift(f):
                lg = pB[:, 0:TOKT * EXPERTS].rearrange("p (t e) -> p t e", e=EXPERTS)
                dve.wait_ge(logits_full, f + 1)
                V.tensor_reduce(t9a[:], lg, AX.X, ALU.max).then_inc(route_step, 1)
                yield
                dve.wait_ge(route_step, f * ROUTE_STEPS + 1)
                V.tensor_tensor(r1[:], lg, spread(t9a), ALU.subtract).then_inc(logits_read, 1)
                yield

            def route_top(f):
                step = Steps(f * ROUTE_STEPS, 1)

                def chain(ins):
                    ins.then_inc(route_step, 1)
                    step.next()

                ranks = rank[:].unsqueeze(1).to_broadcast(wide)
                dve.wait_ge(route_exp, 2 * f + 1)
                chain(V.tensor_reduce(t9a[:], r2[:], AX.X, ALU.add))
                yield
                dve.wait_ge(route_step, step.count())
                chain(V.reciprocal(t9a[:], t9a[:]))
                yield
                dve.wait_ge(route_step, step.count())
                chain(V.tensor_tensor(r2[:], r2[:], spread(t9a), ALU.mult))
                yield
                dve.wait_ge(route_step, step.count())
                chain(V.tensor_reduce(t9a[:], r2[:], AX.X, ALU.max))
                yield
                dve.wait_ge(route_step, step.count())
                chain(V.tensor_tensor(r1[:], r2[:], spread(t9a), ALU.is_ge))
                yield
                dve.wait_ge(route_step, step.count())
                chain(V.tensor_tensor(r1[:], r1[:], ranks, ALU.mult))
                yield
                dve.wait_ge(route_step, step.count())
                chain(V.tensor_reduce(t9b[:], r1[:], AX.X, ALU.max))
                yield
                dve.wait_ge(route_step, step.count())
                chain(V.tensor_tensor(top1[:], r1[:], spread(t9b), ALU.is_equal))
                yield
                dve.wait_ge(route_step, step.count())
                chain(V.scalar_tensor_tensor(r3[:], top1[:], -4.0, r2[:], ALU.mult, ALU.add))
                yield
                dve.wait_ge(route_step, step.count())
                chain(V.tensor_reduce(t9b[:], r3[:], AX.X, ALU.max))
                yield
                dve.wait_ge(route_step, step.count())
                chain(V.tensor_tensor(r1[:], r3[:], spread(t9b), ALU.is_ge))
                yield
                dve.wait_ge(route_step, step.count())
                chain(V.tensor_tensor(r1[:], r1[:], ranks, ALU.mult))
                yield
                dve.wait_ge(route_step, step.count())
                chain(V.tensor_reduce(t9c[:], r1[:], AX.X, ALU.max))
                yield
                dve.wait_ge(route_step, step.count())
                chain(V.tensor_tensor(top2[:], r1[:], spread(t9c), ALU.is_equal))
                yield
                dve.wait_ge(route_step, step.count())
                V.tensor_tensor(t9a[:], t9b[:], t9a[:], ALU.subtract).then_inc(gap_ready, 1)
                yield

            def route_gates(f):
                base = f * ROUTE_STEPS
                dve.wait_ge(route_exp, 2 * f + 2)
                V.tensor_scalar(t9c[:], t9b[:], 1.0, None, ALU.add).then_inc(route_step, 1)
                yield
                dve.wait_ge(route_step, base + 16)
                V.reciprocal(t9c[:], t9c[:]).then_inc(route_step, 1)
                yield
                V.tensor_tensor(r1[:], top2[:], spread(t9b), ALU.mult).then_inc(route_step, 1)
                yield
                dve.wait_ge(route_step, base + 18)
                V.tensor_tensor(r1[:], r1[:], top1[:], ALU.add).then_inc(route_step, 1)
                yield
                dve.wait_ge(route_step, base + 19)
                V.tensor_tensor(gates[:, :, 0:EXPERTS], r1[:], spread(t9c), ALU.mult).then_inc(gates_ready, 1)
                yield

            def gate_units(f, c, pairs):
                for m in pairs:
                    use = ("experts", f"gate{c}", m)
                    dve.wait_ge(expert_full, f * EXPERT_USES + fulls(*use))
                    dve.wait_ge(expert_act, f * EXPERT_ACT + reads("experts", f"up{c}", PAIRS + m))
                    V.tensor_tensor(a3[:, m, :], ring[:, bank(*use), 0:CW], a2[:, m, :], ALU.mult).then_inc(expert_dve, 1)
                    yield

            def finish(f, par, c):
                use = ("experts", "down", c)
                dve.wait_ge(expert_full, f * EXPERT_USES + fulls(*use))
                per = 32 if c == CHUNKS - 1 else 16
                if due(f * per):
                    dve.wait_ge(out_done[c], f * per)
                src = ring[:, bank(*use), 0:CT * NW].rearrange("p (t c) -> p t c", c=NW)[:, :, 0:CH]
                V.tensor_tensor(fin[c][:], src, h1[par][:, c * CT:(c + 1) * CT, :], ALU.add).then_inc(expert_dve, 1)
                yield

            def run(*stages):
                for stage in stages:
                    yield from stage

            def slot_chains(b, s, f, par, t, mixer, experts, nxt):
                early, late, last = [], [], []
                M, E, N = mixer, experts, nxt
                if t == 0:
                    early = [norm1_stats(s, 1 - par)] * M
                if t == 1:
                    early = [norm_scale(s, 0, mv1)] * M + [route_shift(f)] * E
                    late = [offset_norm(b + 1, 1 - par)] * N
                if t == 2:
                    late = [route_top(f)] * E
                if t == 3:
                    early = [offset_gelu(b + 1)] * N + [route_gates(f)] * E + [run(*[scan(s, c) for c in range(CHUNKS)])] * M
                    late = [gate_units(f, 0, (0, 1))] * E
                if t == 4:
                    early = [run(add_mixed(s, 1 - par, 0), norm2_stats(s, 1 - par, range(0, CT)))] * M + [positions(b + 1, 1 - par)] * N
                    late = [gate_units(f, 0, (2,))] * E
                if t == 5:
                    early = [run(add_mixed(s, 1 - par, 1), norm2_stats(s, 1 - par, range(CT, 2 * CT)))] * M + [finish(f, par, 0)] * E
                    late = [run(add_mixed(s, 1 - par, 2), norm2_stats(s, 1 - par, range(2 * CT, TOKT)))] * M
                if t == 6:
                    early = [norm_scale(s, 1, mv2)] * M
                    late = [gate_units(f, 1, range(PAIRS))] * E
                if t == 7:
                    last = [run(finish(f, par, 1), gate_units(f, 2, range(PAIRS)), finish(f, par, 2))] * E
                return early, late, last

            def fill(chains, rounds=1):
                for _ in range(rounds):
                    for c in chains:
                        next(c, None)

            def drain(chains):
                left = list(chains)
                while left:
                    left = [c for c in left if next(c, c) is not c]

            def start():
                drain([offset_norm(0, 0)])
                drain([offset_gelu(0)])
                drain([positions(0, 0)])
                weight_samples(0, 0, 0, 0)
                sum_samples(0, 0)
                weight_samples(1, 0, 0, 1)

            def body(b, par, mixer, experts, nxt):
                for t in range(TILES):
                    n = TILES * b + t
                    chains, late, last = slot_chains(b, b - 1, b - 2, par, t, mixer, experts, nxt)
                    scores_of(n, b, par, t)
                    fill(chains)
                    if nxt or t < TILES - 1:
                        sum_samples(n + 1, (t + 1) % TILES)
                    fill(chains)
                    scores_sum(n)
                    fill(chains, 2)
                    scores_max(n)
                    fill(chains, 2)
                    scores_shift(n)
                    if t < TILES - 2:
                        weight_samples(n + 2, b, par, t + 2)
                    elif nxt:
                        weight_samples(n + 2, b + 1, 1 - par, t + 2 - TILES)
                    chains = chains + late
                    fill(chains, 1)
                    attend(n)
                    fill(chains)
                    attend_sum(n)
                    attend_recip(n)
                    fill(chains)
                    attended(n, par, t)
                    drain(chains)
                    drain(last)

            def tail():
                for b, mixer in ((BATCH, True), (BATCH + 1, False)):
                    for t in range(TILES):
                        chains, late, last = slot_chains(b, b - 1, b - 2, b % 2, t, mixer, True, False)
                        drain(chains)
                        drain(late)
                        drain(last)

            schedule(dve, start, body, tail)


_REF_COORD = np.arange(GRID) * (IMG - 1) / (GRID - 1)
_REF_LOW = np.minimum(np.floor(_REF_COORD), IMG - 2).astype(np.int64)


def _constants():
    hi = _REF_COORD - _REF_LOW
    axis = np.stack([1.0 - hi, hi])
    w = axis[:, None, :, None] * axis[None, :, None, :]
    wtab = np.repeat(w.reshape(2, 2, QUERIES), CH, axis=0).astype(np.float32)
    gy, gx = np.meshgrid(_REF_COORD, _REF_COORD, indexing="ij")
    pix = np.stack([gx.reshape(-1), gy.reshape(-1)], -1).reshape(TILES, P, 1, 2)
    reftab = np.broadcast_to(pix, (TILES, P, HEADS, 2)).reshape(TILES, P, OFFSETS).transpose(1, 0, 2)
    sel = np.zeros((P, PAIRS, P), np.float32)
    for e in range(EXPERTS):
        sel[e, e // 2, (e % 2) * CH:(e % 2 + 1) * CH] = 1.0
    return {
        "wtab": wtab,
        "reftab": np.ascontiguousarray(reftab).astype(np.float32),
        "ident_in": np.eye(P, dtype=np.float32),
        "rank_in": np.broadcast_to(np.arange(EXPERTS, 0, -1, dtype=np.float32), (P, EXPERTS)),
        "sel_in": sel,
    }


def _layout(x, txt, L0_tok_W_q, L0_tok_W_k, L0_tok_W_v, L0_tok_W_o1, L0_tok_b_o1, L0_tok_ln_g,
            L0_tok_ln_b, L0_tok_W_o2, L0_tok_b_o2, L0_attn_h0, L0_attn_A, L0_attn_B, L0_attn_C,
            L0_attn_M, L0_ffn_router_w1, L0_ffn_router_b1, L0_ffn_router_w2, L0_ffn_router_b2,
            L0_ffn_expert_w1, L0_ffn_expert_b1, L0_ffn_expert_w2, L0_ffn_expert_b2,
            L0_ffn_expert_w3, L0_ffn_expert_b3):
    rows = np.ascontiguousarray(x.transpose(0, 2, 3, 1))
    fm = np.empty((BATCH, ROW_PAIRS, IMG, 2, CH), np.float32)
    fm[:, :, :, 0] = rows[:, :-1]
    fm[:, :, :, 1] = rows[:, 1:]
    lo = _REF_LOW
    qcorn = np.empty((BATCH, 2, CH, 2, GRID, GRID), np.float32)
    for yc in range(2):
        for xc in range(2):
            qcorn[:, yc, :, xc] = x[:, :, lo + yc][:, :, :, lo + xc]
    def padded(shape, *parts):
        a = np.zeros(shape, np.float32)
        for at, part in parts:
            a[at] = part
        return a
    s = np.s_
    wqo = padded((2, CH, NW), (s[:, :, :CH], L0_tok_W_q.T), (s[:, :, CH:QW], L0_tok_W_o1)).reshape(P, NW)
    wkv = padded((2, CH, 2 * CH), (s[:, :, :CH], L0_tok_W_k.T), (s[:, :, CH:], L0_tok_W_v.T)).reshape(P, 2 * CH)
    wo2 = padded((TILES, OFFCH, TILES, OFFSETS), *[(s[t, :, t], L0_tok_W_o2) for t in range(TILES)]).reshape(P, P)
    every = lambda v: np.broadcast_to(v, (P,) + v.shape)
    mt = padded((2, CH, TAPS // 2, NW), (s[..., :CH], L0_attn_M.transpose(2, 1, 0).reshape(TAPS // 2, 2, CH, CH).transpose(1, 2, 0, 3)))
    pair = lambda v: v.reshape(PAIRS, P).T
    w1 = padded((P, PAIRS, 2, CH), (s[:CH], L0_ffn_expert_w1.reshape(PAIRS, 2, CH, CH).transpose(2, 0, 1, 3)))
    w2 = padded((2, CH, PAIRS, 2, CH), *[(s[e, :, :, e], L0_ffn_expert_w2[e::2].transpose(1, 0, 2)) for e in range(2)])
    w3 = padded((2, CH, PAIRS, NW), (s[..., :CH], L0_ffn_expert_w3.reshape(PAIRS, 2, CH, CH).transpose(1, 2, 0, 3)))
    return {
        "fm_rows": fm.reshape(-1, 2 * CH),
        "qcorn": qcorn.reshape(BATCH, P, 2, QUERIES),
        "txt": txt,
        "wqo_in": wqo, "wkv_in": wkv, "wo2_in": wo2,
        "bo1_in": every(L0_tok_b_o1), "lng_in": every(L0_tok_ln_g), "lnb_in": every(L0_tok_ln_b),
        "bo2_in": every(L0_tok_b_o2),
        "a_in": L0_attn_A.reshape(SHALVES, P).T, "h0_in": L0_attn_h0.reshape(SHALVES, P).T,
        "bst_in": padded((P, STATES), (s[:CH], L0_attn_B)),
        "cst_in": padded((P, SHALVES, NW), (s[..., :CH], L0_attn_C.reshape(SHALVES, P, CH).transpose(1, 0, 2))),
        "mt_in": mt.reshape(P, TAPS // 2, NW),
        "rw1_in": padded((P, P), (s[:CH, :ROUTER_H], L0_ffn_router_w1)),
        "rb1_in": padded((P, 1), (s[:ROUTER_H, 0], L0_ffn_router_b1), (s[ROUTER_H, 0], 1.0)),
        "rw2_in": padded((P, NW), (s[:ROUTER_H, :EXPERTS], L0_ffn_router_w2), (s[ROUTER_H, :EXPERTS], L0_ffn_router_b2)),
        "w1_in": w1.reshape(P, PAIRS, P), "b1_in": pair(L0_ffn_expert_b1),
        "w2_in": w2.reshape(P, PAIRS, P), "b2_in": pair(L0_ffn_expert_b2),
        "w3_in": w3.reshape(P, PAIRS, NW),
        "b3_in": padded((P, NW), (s[:EXPERTS, :CH], L0_ffn_expert_b3)),
    }


def kernel(**inputs):
    from concourse import bacc
    from concourse.bass_utils import run_bass_kernel_spmd

    arrays = {**_constants(), **_layout(**{k: np.asarray(v) for k, v in inputs.items()})}
    arrays = {f"in_{k}": np.ascontiguousarray(v) for k, v in arrays.items()}
    nc = bacc.Bacc("TRN2", target_bir_lowering=False, num_devices=1)
    args = {k[3:]: nc.dram_tensor(k, a.shape, mybir.dt.from_np(a.dtype), kind="ExternalInput").ap()
            for k, a in arrays.items()}
    out = nc.dram_tensor("out_0", (BATCH, SEQ, CH), F32, kind="ExternalOutput").ap()
    build(nc, out=out, **args)
    r = run_bass_kernel_spmd(nc, [arrays], core_ids=[0])
    return r.results[0]["out_0"]
```

```python
from contextlib import ExitStack

import numpy as np

import concourse.bass as bass
from concourse import mybir

F32 = mybir.dt.float32
U32 = mybir.dt.uint32
ALU = mybir.AluOpType
ACT = mybir.ActivationFunctionType
AX = mybir.AxisListType

P = 128
BATCH, CH, IMG = 16, 64, 128
HEADS, POINTS, HD, DS = 8, 8, 8, 4
GRID = IMG // DS
QUERIES = GRID * GRID
TILES = QUERIES // P
TXT = 77
SEQ = QUERIES + TXT
ROW_PAIRS = IMG - 1
OFFCH = CH // DS
OFFSETS = HEADS * 2
OFFSET_SCALE = 4.0
STATES, TAPS = 256, 10
SHALVES = STATES // P
EXPERTS = 6
PAIRS = EXPERTS // 2
ROUTER_H = CH // 2
TOKT = 9
CHUNKS, CT = 3, 3
CW = CT * P
PADW = TOKT * P
PAD = TAPS
NW = 96
QW = CH + OFFCH
EPS = 1e-5
ROUND = float(3 * 2 ** 22)
GELU_C = 2.0 * float(np.sqrt(2.0 / np.pi))
SM_SCALE = float(HD) ** -0.5
SCALED = [2, 2, 2, 0, 0, 0, 2, 2]
TURN_FIRST = (5, 6)
GATHER = 16 * POINTS

RING_USES = [("rest", "up2", m) for m in range(PAIRS)]
RING_USES += [("rest", "gate1", 2), ("rest", "down", 1)]
RING_USES += [("rest", "up2", PAIRS + m) for m in range(PAIRS)]
RING_USES += [("experts", "hidden", c) for c in range(CHUNKS)]
RING_USES += [("rest", "gate2", m) for m in range(PAIRS)] + [("rest", "down", 2)]
RING_USES += [("experts", "up0", m) for m in range(PAIRS)]
RING_USES += [("mixer", "drive", v) for v in range(SHALVES)]
RING_USES += [("experts", "up0", PAIRS + m) for m in range(PAIRS)]
RING_USES += [("mixer", "drive", SHALVES + v) for v in range(SHALVES)]
RING_USES += [("experts", "up1", m) for m in range(PAIRS)]
RING_USES += [("mixer", "drive", 2 * SHALVES + v) for v in range(SHALVES)]
RING_USES += [("experts", "gate0", m) for m in range(PAIRS)] + [("experts", "down", 0)]
RING_USES += [("nobody", "skipped", 0)]
RING_USES += [("experts", "up1", PAIRS + m) for m in range(PAIRS)]
RING_USES += [("experts", "gate1", m) for m in range(PAIRS - 1)]
assert len(RING_USES) % 2 == 0
LAG = {"sampling": 0, "mixer": 1, "experts": 2, "rest": 3}
PLACE = {(what, which): at for at, (stage, what, which) in enumerate(RING_USES)}


def stage_of(*use):
    return RING_USES[PLACE[use]][0]


def reader_of(*use):
    return "act" if use[0] == "hidden" or use[0].startswith("up") else "dve"


def bank(*use):
    return PLACE[use] % 2


def fulls(batch, *use):
    stage = stage_of(*use)
    upto = sum(u[0] == stage for u in RING_USES[:PLACE[use] + 1])
    return batch * sum(u[0] == stage for u in RING_USES) + upto


def reads(batch, *use):
    same = [u[0] == stage_of(*use) and reader_of(*u[1:]) == reader_of(*use) for u in RING_USES]
    return batch * sum(same) + sum(same[:PLACE[use] + 1])


def active(stage, b):
    return not isinstance(b, int) or 0 <= b - LAG[stage] < BATCH


OFFSET_STEPS = 33
NORM_STEPS = 26
ROUTE_STEPS = 19


def due(count):
    return not isinstance(count, int) or count > 0


def build(nc, fm_rows, qcorn, txt, wtab, reftab, ident_in, rank_in, wqo_in, wkv_in, bo1_in, lng_in,
          lnb_in, wo2_in, bo2_in, a_in, h0_in, bst_in, cst_in, mt_in, rw1_in, rb1_in, rw2_in,
          w1_in, b1_in, w2_in, b2_in, w3_in, b3_in, sel_in, out):
    with ExitStack() as ctx:
        def sb(name, shape, dt=F32):
            return ctx.enter_context(nc.sbuf_tensor(name, shape, dt))

        def pb(name, shape):
            return ctx.enter_context(nc.psum_tensor(name, shape, F32))

        def sem(name):
            return ctx.enter_context(nc.semaphore(name))

        corner_w = sb("corner_w", [P, 2, QUERIES])
        ref_pix = sb("ref_pix", [P, TILES, OFFSETS])
        ident = sb("ident", [P, P])
        rank = sb("rank", [P, EXPERTS])
        wqo = sb("wqo", [P, NW])
        wkv = sb("wkv", [P, 2 * CH])
        bo1 = sb("bo1", [P, OFFCH])
        lng = sb("lng", [P, OFFCH])
        lnb = sb("lnb", [P, OFFCH])
        wo2 = sb("wo2", [P, P])
        bo2 = sb("bo2", [P, OFFSETS])
        decay = sb("decay", [P, SHALVES])
        state0 = sb("state0", [P, SHALVES])
        bst = sb("bst", [P, STATES])
        cst = sb("cst", [P, SHALVES, NW])
        mt = sb("mt", [P, TAPS // 2, NW])
        rw1 = sb("rw1", [P, P])
        rb1 = sb("rb1", [P, 1])
        rw2 = sb("rw2", [P, NW])
        w1 = sb("w1", [P, PAIRS, P])
        b1 = sb("b1", [P, PAIRS])
        w2 = sb("w2", [P, PAIRS, P])
        b2 = sb("b2", [P, PAIRS])
        w3 = sb("w3", [P, PAIRS, NW])
        b3 = sb("b3", [P, NW])
        sel = sb("sel", [P, PAIRS, P])
        SAMPLING_CONSTS = [(corner_w, wtab), (wqo, wqo_in), (bo1, bo1_in), (lng, lng_in), (lnb, lnb_in),
                           (bo2, bo2_in), (ref_pix, reftab), (ident, ident_in), (wo2, wo2_in), (wkv, wkv_in)]
        CONSTS = [(rank, rank_in), (decay, a_in), (state0, h0_in), (bst, bst_in), (cst, cst_in),
                  (mt, mt_in), (rw1, rw1_in), (rb1, rb1_in), (rw2, rw2_in), (w1, w1_in), (b1, b1_in),
                  (w2, w2_in), (b2, b2_in), (w3, w3_in), (b3, b3_in), (sel, sel_in)]

        qc = sb("qc", [P, 2, QUERIES])
        qo = [sb(f"qo{k}", [P, TILES, QW]) for k in range(2)]
        o1 = sb("o1", [P, TILES, OFFCH])
        o2 = sb("o2", [P, TILES, OFFCH])
        o3 = sb("o3", [P, TILES, OFFCH])
        o4 = sb("o4", [P, TILES, OFFCH])
        s8a = sb("s8a", [P, TILES])
        s8c = sb("s8c", [P, TILES])
        s8d = sb("s8d", [P, TILES])
        hT = sb("hT", [P, P])
        pix = sb("pix", [P, TILES * POINTS, 2])
        low = sb("low", [P, TILES * POINTS, 2])
        hats = sb("hats", [P, TILES * POINTS, 2, 2])
        w4 = [sb(f"w4_{k}", [P, TILES, POINTS * 4]) for k in range(2)]
        rowf = sb("rowf", [P, TILES * POINTS])
        batch_row = sb("batch_row", [P, 1])
        idx = [sb(f"idx{k}", [P, TILES * POINTS], U32) for k in range(2)]
        G = sb("G", [P, TILES, POINTS * 4 * CH])
        g2 = [sb(f"g2_{k}", [P, POINTS, 2 * CH]) for k in range(2)]
        sT = [sb(f"sT{k}", [P, POINTS, P]) for k in range(2)]
        prodk = sb("prodk", [P, POINTS, CH])
        prodv = sb("prodv", [P, POINTS, CH])
        scores = sb("scores", [P, POINTS, HEADS])
        smax = sb("smax", [P, HEADS])
        shifted = sb("shifted", [P, POINTS, HEADS])
        probs = sb("probs", [P, POINTS, HEADS])
        den = sb("den", [P, HEADS])
        rden = sb("rden", [P, HEADS])
        av = sb("av", [P, CH])
        H = [sb(f"H{k}", [P, TOKT, CH]) for k in range(2)]
        stats1 = sb("stats1", [P, TOKT, 6])
        stats2 = sb("stats2", [P, TOKT, 6])
        mv1 = sb("mv1", [P, TOKT, 2])
        mv2 = sb("mv2", [P, TOKT, 2])
        ve = sb("ve", [P, TOKT])
        y0 = sb("y0", [P, TOKT])
        ny = sb("ny", [P, TOKT])
        mark = sb("mark", [P, 1])
        rstd = [sb(f"rstd{k}", [P, TOKT]) for k in range(2)]
        nmr = [sb(f"nmr{k}", [P, TOKT]) for k in range(2)]
        x1n = sb("x1n", [P, TOKT, 2, CH])
        X2 = sb("X2", [P, PAD + PADW + 2])
        states = sb("states", [P, SHALVES, PADW + TAPS])
        h1 = [sb(f"h1_{k}", [P, TOKT, CH]) for k in range(2)]
        x2n = sb("x2n", [P, TOKT, P])
        X3 = sb("X3", [P, PADW])
        rh = sb("rh", [P, PADW])
        r1 = sb("r1", [P, TOKT, EXPERTS])
        r2 = sb("r2", [P, TOKT, EXPERTS])
        r3 = sb("r3", [P, TOKT, EXPERTS])
        top1 = sb("top1", [P, TOKT, EXPERTS])
        top2 = sb("top2", [P, TOKT, EXPERTS])
        t9a = sb("t9a", [P, TOKT])
        t9b = sb("t9b", [P, TOKT])
        t9c = sb("t9c", [P, TOKT])
        gates = sb("gates", [P, TOKT, P])
        gT = sb("gT", [P, PADW])
        a1 = sb("a1", [P, PAIRS, CW])
        a2 = sb("a2", [P, PAIRS, CW])
        a3 = sb("a3", [P, PAIRS, CW])
        fin = [sb(f"fin{k}", [P, CT, CH]) for k in range(CHUNKS)]

        tbank = pb("tbank", [P, 2, 4, P])
        kv = pb("kv", [P, POINTS, 2 * CH])
        pA = pb("pA", [P, 512])
        pB = pb("pB", [P, 512])
        ring = pb("ring", [P, 2, 512])

        sampling_consts_in = sem("sampling_consts_in")
        consts_in = sem("consts_in")
        cleared = sem("cleared")
        pool_passed = sem("pool_passed")
        dve_passed = sem("dve_passed")
        qc_in = sem("qc_in")
        qc_weighted = sem("qc_weighted")
        pA_full = sem("pA_full")
        qo_ready = sem("qo_ready")
        offset_step = sem("offset_step")
        gelu_arg = sem("gelu_arg")
        gelu_exp = sem("gelu_exp")
        off_h = sem("off_h")
        hT_ready = sem("hT_ready")
        pix_ready = sem("pix_ready")
        idx_ready = sem("idx_ready")
        row_moved = sem("row_moved")
        gather_in = [sem(f"gather_in{t}") for t in range(TILES)]
        g_weighted = sem("g_weighted")
        g_scaled = sem("g_scaled")
        g_summed = sem("g_summed")
        t_full = sem("t_full")
        t_moved = sem("t_moved")
        kv_full = sem("kv_full")
        qk_done = sem("qk_done")
        scores_done = sem("scores_done")
        max_done = sem("max_done")
        shifted_ready = sem("shifted_ready")
        probs_ready = sem("probs_ready")
        av_done = sem("av_done")
        den_done = sem("den_done")
        avsum_done = sem("avsum_done")
        rden_done = sem("rden_done")
        h_ready = sem("h_ready")
        txt_in = sem("txt_in")
        stat1_done = sem("stat1_done")
        stat2_done = sem("stat2_done")
        var_ready = sem("var_ready")
        x1_ready = sem("x1_ready")
        x2_turned = sem("x2_turned")
        x3_turned = sem("x3_turned")
        gates_turned = sem("gates_turned")
        logits_full = sem("logits_full")
        x2_ready = sem("x2_ready")
        norm_step = sem("norm_step")
        norm_ready = sem("norm_ready")
        mixer_full = sem("mixer_full")
        mixer_read = sem("mixer_read")
        mix_full = sem("mix_full")
        mix_read = sem("mix_read")
        expert_full = sem("expert_full")
        expert_act = sem("expert_act")
        expert_dve = sem("expert_dve")
        rest_full = sem("rest_full")
        rest_act = sem("rest_act")
        rest_dve = sem("rest_dve")
        full = {"mixer": mixer_full, "experts": expert_full, "rest": rest_full}
        read = {("mixer", "dve"): mixer_read, ("experts", "act"): expert_act, ("experts", "dve"): expert_dve,
                ("rest", "act"): rest_act, ("rest", "dve"): rest_dve}

        def full_of(*use):
            return full[stage_of(*use)]

        def read_of(*use):
            return read[stage_of(*use), reader_of(*use)]
        x2n_ready = sem("x2n_ready")
        x3_ready = sem("x3_ready")
        route_step = sem("route_step")
        logits_read = sem("logits_read")
        route_exp = sem("route_exp")
        gap_ready = sem("gap_ready")
        gates_ready = sem("gates_ready")
        gT_ready = sem("gT_ready")
        out_done = [sem(f"out_done{k}") for k in range(CHUNKS)]

        block = ctx.enter_context(nc.Block())

        def schedule(eng, start, body, tail):
            start()
            for b in range(4):
                body(b, b % 2, True)
            with eng.Fori(0, (BATCH - 6) // 2) as i:
                body(2 * i + 4, 0, True)
                body(2 * i + 5, 1, True)
            body(BATCH - 2, 0, True)
            body(BATCH - 1, 1, False)
            tail()

        @block.sync
        def _(sp):
            def load_corners(b):
                if due(2 * b):
                    sp.wait_ge(qo_ready, 2 * b)
                sp.dma_start(qc[:], qcorn[bass.ds(b, 1)].rearrange("o p x q -> p (o x) q")).then_inc(qc_in, 16)

            def load_text(b, par):
                if not (isinstance(b, int) and b == 0):
                    sp.wait_ge(var_ready, b)
                sp.dma_start(H[par][0:TXT, TILES, :], txt[bass.ds(b, 1)].rearrange("o p c -> (o p) c")).then_inc(txt_in, 16)

            def store(f):
                for c in range(CHUNKS):
                    sp.wait_ge(read_of("down", c), reads(f, "down", c))
                    dst = out[bass.ds(f, 1), c * CW:min((c + 1) * CW, SEQ), :]
                    if c < CHUNKS - 1:
                        sp.dma_start(dst.rearrange("o (t p) c -> p (o t) c", p=P), fin[c][:]).then_inc(out_done[c], 16)
                    else:
                        whole = dst[:, 0:(CT - 1) * P, :]
                        sp.dma_start(whole.rearrange("o (t p) c -> p (o t) c", p=P), fin[c][:, 0:CT - 1, :]).then_inc(out_done[c], 16)
                        sp.dma_start(dst[:, (CT - 1) * P:, :].rearrange("o p c -> (o p) c"), fin[c][0:TXT, CT - 1, :]).then_inc(out_done[c], 16)

            def start():
                load_corners(0)
                for dst, src in SAMPLING_CONSTS:
                    sp.dma_start(dst[:], src).then_inc(sampling_consts_in, 16)
                for dst, src in CONSTS:
                    sp.dma_start(dst[:], src).then_inc(consts_in, 16)
                sp.wait_ge(cleared, 2)

            def body(b, par, nxt):
                if nxt:
                    load_corners(b + 1)
                load_text(b, par)
                if not isinstance(b, int) or b >= 3:
                    store(b - 3)

            def tail():
                for f in range(BATCH - 3, BATCH):
                    store(f)
                for c in range(CHUNKS):
                    sp.wait_ge(out_done[c], 16 * BATCH * (2 if c == CHUNKS - 1 else 1))

            schedule(sp, start, body, tail)

        @block.gpsimd
        def _(pool):
            nc.gpsimd.memset(H[0][:], 0.0).then_inc(cleared, 1)
            nc.gpsimd.memset(H[1][:], 0.0).then_inc(cleared, 1)
            nc.gpsimd.memset(X2[:], 0.0).then_inc(cleared, 1)
            nc.gpsimd.memset(states[:], 0.0).then_inc(cleared, 1)
            nc.gpsimd.memset(X3[:], 0.0).then_inc(cleared, 1)
            nc.gpsimd.memset(gates[:], 0.0).then_inc(cleared, 1)
            nc.gpsimd.memset(x2n[:], 0.0).then_inc(cleared, 1)
            nc.gpsimd.memset(batch_row[:], 0.0).then_inc(cleared, 1)

            def weight_corners(b):
                pool.wait_ge(qc_in, 16 * (b + 1))
                nc.gpsimd.tensor_tensor(qc[:], qc[:], corner_w[:], ALU.mult).then_inc(qc_weighted, 1)

            def start():
                pool.wait_ge(sampling_consts_in, 16 * len(SAMPLING_CONSTS))
                weight_corners(0)

            def body(b, par, nxt):
                if nxt:
                    weight_corners(b + 1)
                pool.wait_ge(idx_ready, b + 1)
                for t in range(TILES):
                    if due((b - 1) * TILES + t + 1):
                        pool.wait_ge(g_summed, (b - 1) * TILES + t + 1)
                    pool.sem_inc(pool_passed, 1)
                    for k in range(POINTS):
                        nc.gpsimd.indirect_dma_start(
                            out=G[:, t, k * 4 * CH:(k + 1) * 4 * CH], out_offset=None, in_=fm_rows,
                            in_offset=bass.IndirectOffsetOnAxis(ap=idx[par][:, t * POINTS + k:t * POINTS + k + 1], axis=0),
                        ).then_inc(gather_in[t], 16)

            schedule(pool, start, body, lambda: None)

        @block.tensor
        def _(pe):
            pe.wait_ge(sampling_consts_in, 16 * len(SAMPLING_CONSTS))
            pe.wait_ge(cleared, 8)

            def queries(b, half):
                if half == 0:
                    pe.wait_ge(qc_weighted, b + 1)
                    if due(b):
                        pe.wait_ge(pix_ready, b)
                    if due((b - 2) * CHUNKS):
                        pe.wait_ge(mix_read, (b - 2) * CHUNKS)
                else:
                    pe.wait_ge(qo_ready, 2 * b + 1)
                for j in range(4):
                    t = 4 * half + j
                    for x in range(2):
                        mm = nc.tensor.matmul(pA[:, j * NW:(j + 1) * NW], qc[:, x, t * P:(t + 1) * P], wqo[:],
                                              start=(x == 0), stop=(x == 1))
                mm.then_inc(pA_full, 1)

            def offset_turn(b):
                if due((b - 1) * CHUNKS):
                    pe.wait_ge(x2_ready, (b - 1) * CHUNKS)
                pe.wait_ge(off_h, b + 1)
                nc.tensor.transpose(pA[:, 0:P], o4[:].rearrange("p t c -> p (t c)"), ident[:]).then_inc(pA_full, 1)

            def offset_out(b):
                pe.wait_ge(hT_ready, b + 1)
                nc.tensor.matmul(pA[:, 0:P], hT[:], wo2[:], start=True, stop=True).then_inc(pA_full, 1)

            def turn_samples(n, t):
                pe.wait_ge(g_summed, n + 1)
                for half in range(2):
                    if due(2 * (n - 1) + half + 1):
                        pe.wait_ge(t_moved, 2 * (n - 1) + half + 1)
                    for j in range(4):
                        mm = nc.tensor.transpose(tbank[:, half, j, :], g2[t % 2][:, 4 * half + j, :], ident[:])
                    mm.then_inc(t_full, 1)

            def project(n, t):
                if due(n):
                    pe.wait_ge(av_done, n)
                for half in range(2):
                    pe.wait_ge(t_moved, 2 * n + half + 1)
                    for j in range(4):
                        k = 4 * half + j
                        mm = nc.tensor.matmul(kv[:, k, :], sT[t % 2][:, k, :], wkv[:], start=True, stop=True)
                    mm.then_inc(kv_full, 1)

            def ring_free(b, *use):
                for back in range(2, 2 * len(RING_USES), 2):
                    at = PLACE[use] - back
                    rounds = 1 if at < 0 else 0
                    if at < -len(RING_USES):
                        return
                    stage, *last = RING_USES[at]
                    if stage != "nobody" and active(stage, b - rounds):
                        pe.wait_ge(read_of(*last), reads(b - rounds - LAG[stage], *last))
                        return

            def turn_x2(b, s, c, nxt):
                pe.wait_ge(x1_ready, s * TOKT + CT * (c + 1))
                if c > 0:
                    pe.wait_ge(x2_ready, s * CHUNKS + c)
                elif nxt:
                    pe.wait_ge(qo_ready, 2 * b + 4)
                elif due(s):
                    pe.wait_ge(mix_read, s * CHUNKS)
                for j in range(CT):
                    mm = nc.tensor.transpose(pA[:, j * P:(j + 1) * P], x1n[:, c * CT + j].rearrange("p a c -> p (a c)"), ident[:])
                mm.then_inc(x2_turned, 1)

            def drive(b, s, c):
                pe.wait_ge(x2_ready, s * CHUNKS + c + 1)
                w = min(CW, SEQ - c * CW)
                for v in range(SHALVES):
                    use = ("drive", c * SHALVES + v)
                    ring_free(b, *use)
                    nc.tensor.matmul(ring[:, bank(*use), 0:w], bst[:, v * P:(v + 1) * P],
                                     X2[:, PAD + c * CW:PAD + c * CW + w], start=True, stop=True).then_inc(mixer_full, 1)

            def mix(b, s, c, tiles, nxt, experts):
                if tiles[0] == 0:
                    if c == 0 and nxt:
                        pe.wait_ge(pix_ready, b + 2)
                    if c == 1 and experts:
                        pe.wait_ge(gT_ready, s * CHUNKS)
                    if c == 2:
                        pe.wait_ge(mix_read, s * CHUNKS + 1)
                    ahead = min(c + 1, CHUNKS - 1) * SHALVES + SHALVES - 1
                    pe.wait_ge(mixer_read, reads(s, "drive", ahead))
                for j in tiles:
                    t0 = (c * CT + j) * P
                    dst = (pA, pB, pA)[c][:, j * NW:(j + 1) * NW]
                    for i in range(TAPS // 2):
                        at = PAD + t0 - 2 * i
                        nc.tensor.matmul(dst, X2[:, at:at + P], mt[:, i, :], start=(i == 0), stop=False)
                    for v in range(SHALVES):
                        mm = nc.tensor.matmul(dst, states[:, v, t0 + TAPS:t0 + TAPS + P], cst[:, v, :],
                                              start=False, stop=(v == SHALVES - 1))
                if tiles[-1] == CT - 1:
                    mm.then_inc(mix_full, 1)

            def turn_x3(f, c):
                pe.wait_ge(x2n_ready, f * TOKT + CT * (c + 1))
                if c > 0:
                    pe.wait_ge(x3_ready, f * CHUNKS + c)
                for j in range(CT):
                    mm = nc.tensor.transpose(pB[:, j * P:(j + 1) * P], x2n[:, c * CT + j, :], ident[:])
                mm.then_inc(x3_turned, 1)

            def router_hidden(b, f, c):
                use = ("hidden", c)
                ring_free(b, *use)
                pe.wait_ge(x3_ready, f * CHUNKS + c + 1)
                nc.tensor.matmul(ring[:, bank(*use), 0:CW], rw1[:], X3[:, c * CW:(c + 1) * CW],
                                 start=True, stop=True).then_inc(expert_full, 1)

            def logits(f):
                pe.wait_ge(x3_ready, (f + 1) * CHUNKS)
                pe.wait_ge(expert_act, reads(f, "hidden", CHUNKS - 1))
                for t in range(TOKT):
                    mm = nc.tensor.matmul(pB[:, t * EXPERTS:t * EXPERTS + NW], rh[:, t * P:(t + 1) * P], rw2[:],
                                          start=True, stop=True)
                mm.then_inc(logits_full, 1)

            def turn_gates(f, c):
                pe.wait_ge(gates_ready, f + 1)
                if c > 0:
                    pe.wait_ge(gT_ready, f * CHUNKS + c)
                for j in range(CT):
                    mm = nc.tensor.transpose(pB[:, j * P:(j + 1) * P], gates[:, c * CT + j, :], ident[:])
                mm.then_inc(gates_turned, 1)

            def experts_up(b, f, c, layer, pairs=range(PAIRS)):
                for m in pairs:
                    use = (f"up{c}", PAIRS * layer + m)
                    ring_free(b, *use)
                    if layer == 0:
                        nc.tensor.matmul(ring[:, bank(*use), 0:CW], w1[:, m, :], X3[:, c * CW:(c + 1) * CW],
                                         start=True, stop=True).then_inc(full_of(*use), 1)
                    else:
                        pe.wait_ge(read_of(f"up{c}", m), reads(f, f"up{c}", m))
                        nc.tensor.matmul(ring[:, bank(*use), 0:CW], w2[:, m, :], a1[:, m, :],
                                         start=True, stop=True).then_inc(full_of(*use), 1)

            def spread_gates(b, f, c, pairs):
                pe.wait_ge(gT_ready, f * CHUNKS + c + 1)
                for m in pairs:
                    use = (f"gate{c}", m)
                    ring_free(b, *use)
                    nc.tensor.matmul(ring[:, bank(*use), 0:CW], sel[:, m, :], gT[:, c * CW:(c + 1) * CW],
                                     start=True, stop=True).then_inc(full_of(*use), 1)

            def experts_down(b, f, c):
                use = ("down", c)
                ring_free(b, *use)
                pe.wait_ge(read_of(f"gate{c}", PAIRS - 1), reads(f, f"gate{c}", PAIRS - 1))
                for j in range(CT):
                    dst = ring[:, bank(*use), j * NW:(j + 1) * NW]
                    for m in range(PAIRS):
                        nc.tensor.matmul(dst, a3[:, m, j * P:(j + 1) * P], w3[:, m, :], start=(m == 0), stop=False)
                    t0 = (c * CT + j) * P
                    mm = nc.tensor.matmul(dst, gT[:, t0:t0 + P], b3[:], start=False, stop=True)
                mm.then_inc(full_of(*use), 1)

            def before(b, t, nxt):
                M, E, R = active("mixer", b), active("experts", b), active("rest", b)
                s, f, g = b - 1, b - 2, b - 3
                if t == 0:
                    if R:
                        experts_up(b, g, 2, 0)
                        spread_gates(b, g, 1, (2,))
                    if nxt:
                        queries(b + 1, 0)
                if t == 1:
                    if E:
                        turn_x3(f, 0)
                    if R:
                        experts_up(b, g, 2, 1)
                    if E:
                        turn_x3(f, 1)
                if t == 2:
                    if M:
                        turn_x2(b, s, 0, nxt)
                    if E:
                        logits(f)
                if t == 3:
                    if E:
                        experts_up(b, f, 0, 0)
                    if M:
                        drive(b, s, 0)
                if t == 4:
                    if E:
                        experts_up(b, f, 1, 0)
                    if M:
                        mix(b, s, 0, (0,), nxt, E)
                if t == 5:
                    if E:
                        turn_gates(f, 0)
                    if M:
                        mix(b, s, 0, (2,), nxt, E)
                    if E:
                        turn_gates(f, 1)
                        spread_gates(b, f, 0, (0, 1))
                if t == 6:
                    if M:
                        mix(b, s, 1, (2,), nxt, E)
                    if E:
                        experts_down(b, f, 0)
                if t == 7:
                    if M:
                        mix(b, s, 2, (2,), nxt, E)
                    if E:
                        experts_up(b, f, 1, 1, (0, 1))

            def after(b, t, nxt):
                M, E, R = active("mixer", b), active("experts", b), active("rest", b)
                s, f, g = b - 1, b - 2, b - 3
                if t == 0:
                    if nxt:
                        queries(b + 1, 1)
                    if R:
                        experts_down(b, g, 1)
                if t == 1:
                    if E:
                        turn_x3(f, 2)
                        for c in range(CHUNKS):
                            router_hidden(b, f, c)
                    if R:
                        spread_gates(b, g, 2, (0, 1))
                if t == 2:
                    if M:
                        turn_x2(b, s, 1, nxt)
                    if R:
                        spread_gates(b, g, 2, (2,))
                    if M:
                        turn_x2(b, s, 2, nxt)
                    if R:
                        experts_down(b, g, 2)
                if t == 3:
                    if nxt:
                        offset_turn(b + 1)
                    if E:
                        experts_up(b, f, 0, 1)
                    if nxt:
                        offset_out(b + 1)
                    if M:
                        drive(b, s, 1)
                if t == 4 and M:
                    drive(b, s, 2)
                    mix(b, s, 0, (1,), nxt, E)
                if t == 5:
                    if E:
                        turn_gates(f, 2)
                        spread_gates(b, f, 0, (2,))
                    if M:
                        mix(b, s, 1, (0, 1), nxt, E)
                if t == 6 and M:
                    mix(b, s, 2, (0, 1), nxt, E)
                if t == 7 and E:
                    experts_up(b, f, 1, 1, (2,))
                    spread_gates(b, f, 1, (0, 1))

            def start():
                queries(0, 0)
                queries(0, 1)
                offset_turn(0)
                offset_out(0)
                turn_samples(0, 0)
                project(0, 0)
                turn_samples(1, 1)
                pe.wait_ge(consts_in, 16 * len(CONSTS))

            def body(b, par, nxt):
                for t in range(TILES):
                    before(b, t, nxt)
                    if nxt or t < TILES - 1:
                        project(TILES * b + t + 1, (t + 1) % TILES)
                    if t not in TURN_FIRST:
                        after(b, t, nxt)
                    if nxt or t < TILES - 2:
                        turn_samples(TILES * b + t + 2, (t + 2) % TILES)
                    if t in TURN_FIRST:
                        after(b, t, nxt)

            def tail():
                for b in range(BATCH, BATCH + LAG["rest"]):
                    for t in range(TILES):
                        before(b, t, False)
                        after(b, t, False)

            schedule(pe, start, body, tail)

        @block.scalar
        def _(act):
            act.wait_ge(sampling_consts_in, 16 * len(SAMPLING_CONSTS))
            act.wait_ge(cleared, 8)

            def queries_out(b, par):
                for half in range(2):
                    act.wait_ge(pA_full, 4 * b + half + 1)
                    src = pA[:, 0:4 * NW].rearrange("p (t c) -> p t c", c=NW)[:, :, 0:QW]
                    nc.scalar.activation(qo[par][:, 4 * half:4 * half + 4, :], src, ACT.Copy).then_inc(qo_ready, 1)

            def gelu_exponential(b):
                act.wait_ge(gelu_arg, b + 1)
                nc.scalar.activation(o3[:], o2[:], ACT.Exp, scale=-GELU_C).then_inc(gelu_exp, 1)

            def turned_hidden(b):
                act.wait_ge(pA_full, 4 * b + 3)
                nc.scalar.activation(hT[:], pA[:, 0:P], ACT.Copy).then_inc(hT_ready, 1)

            def move_samples(n, t):
                if due(2 * (n - 1)):
                    act.wait_ge(kv_full, 2 * (n - 1))
                for half in range(2):
                    act.wait_ge(t_full, 2 * n + half + 1)
                    nc.scalar.activation(sT[t % 2][:, 4 * half:4 * half + 4, :], tbank[:, half], ACT.Copy).then_inc(t_moved, 1)

            def scale_samples(b, par, t):
                if SCALED[t]:
                    act.wait_ge(gather_in[t], GATHER * (b + 1))
                    act.wait_ge(offset_step, (b + 1) * OFFSET_STEPS)
                for j in range(4 * SCALED[t]):
                    at = G[:, t, j * CH:(j + 1) * CH]
                    op = nc.scalar.activation(at, at, ACT.Copy, scale=w4[par][:, t, j:j + 1])
                if SCALED[t]:
                    op.then_inc(g_scaled, 1)

            def exponential(n):
                act.wait_ge(shifted_ready, n + 1)
                nc.scalar.activation(probs[:], shifted[:], ACT.Exp, scale=SM_SCALE).then_inc(probs_ready, 1)

            def normalize1(s, par, tiles):
                act.wait_ge(norm_ready, 2 * s + 1)
                for t in tiles:
                    src = H[par][:, t, :].unsqueeze(1).to_broadcast([P, 2, CH])
                    nc.scalar.activation(x1n[:, t], src, ACT.Identity, bias=nmr[0][:, t:t + 1],
                                         scale=rstd[0][:, t:t + 1]).then_inc(x1_ready, 1)

            def normalize2(s, par, tiles):
                act.wait_ge(norm_ready, 2 * s + 2)
                for t in tiles:
                    nc.scalar.activation(x2n[:, t, 0:CH], h1[par][:, t, :], ACT.Identity, bias=nmr[1][:, t:t + 1],
                                         scale=rstd[1][:, t:t + 1]).then_inc(x2n_ready, 1)

            def move_x2(s, c):
                act.wait_ge(x2_turned, s * CHUNKS + c + 1)
                at = PAD + c * CW
                nc.scalar.activation(X2[0:CH, at:at + CW], pA[0:CH, 0:CW], ACT.Copy)
                nc.scalar.activation(X2[CH:P, at + 1:at + 1 + CW], pA[CH:P, 0:CW], ACT.Copy).then_inc(x2_ready, 1)

            def move_x3(f, c):
                act.wait_ge(x3_turned, f * CHUNKS + c + 1)
                nc.scalar.activation(X3[0:CH, c * CW:(c + 1) * CW], pB[0:CH, 0:CW], ACT.Copy).then_inc(x3_ready, 1)

            def move_gates(f, c):
                act.wait_ge(gates_turned, f * CHUNKS + c + 1)
                nc.scalar.activation(gT[:, c * CW:(c + 1) * CW], pB[:, 0:CW], ACT.Copy).then_inc(gT_ready, 1)

            def router_relu(f, c):
                use = ("hidden", c)
                act.wait_ge(expert_full, fulls(f, *use))
                nc.scalar.activation(rh[:, c * CW:(c + 1) * CW], ring[:, bank(*use), 0:CW], ACT.Relu,
                                     bias=rb1[:, 0:1]).then_inc(expert_act, 1)

            def route_exponentials(f):
                act.wait_ge(logits_read, f + 1)
                nc.scalar.activation(r2[:], r1[:], ACT.Exp).then_inc(route_exp, 1)

            def gap_exponential(f):
                act.wait_ge(gap_ready, f + 1)
                nc.scalar.activation(t9b[:], t9a[:], ACT.Exp).then_inc(route_exp, 1)

            def expert_relus(f, c, layer, pairs=range(PAIRS)):
                dst, bias = ((a1, b1), (a2, b2))[layer]
                for m in pairs:
                    use = (f"up{c}", PAIRS * layer + m)
                    act.wait_ge(full_of(*use), fulls(f, *use))
                    nc.scalar.activation(dst[:, m, :], ring[:, bank(*use), 0:CW], ACT.Relu,
                                         bias=bias[:, m:m + 1]).then_inc(read_of(*use), 1)

            def before(b, par, t, nxt):
                M, E, R = active("mixer", b), active("experts", b), active("rest", b)
                s, f, g = b - 1, b - 2, b - 3
                if t == 0:
                    if R:
                        expert_relus(g, 2, 0, (0, 1))
                if t == 1:
                    if E:
                        move_x3(f, 0)
                    if R:
                        expert_relus(g, 2, 1, (0, 1))
                if t == 3:
                    if nxt:
                        gelu_exponential(b + 1)
                    if E:
                        route_exponentials(f)
                    if E:
                        expert_relus(f, 0, 0)
                if t == 4 and E:
                    expert_relus(f, 1, 0, (0, 1))
                if t == 5 and E:
                    move_gates(f, 0)

            def after(b, par, t, nxt):
                M, E, R = active("mixer", b), active("experts", b), active("rest", b)
                s, f, g = b - 1, b - 2, b - 3
                if t == 0:
                    if R:
                        expert_relus(g, 2, 0, (2,))
                    if nxt:
                        queries_out(b + 1, 1 - par)
                    if E:
                        normalize2(f, par, range(0, 2 * CT))
                if t == 1:
                    if R:
                        expert_relus(g, 2, 1, (2,))
                    if E:
                        normalize2(f, par, range(2 * CT, TOKT))
                        move_x3(f, 1)
                        move_x3(f, 2)
                        for c in range(CHUNKS):
                            router_relu(f, c)
                    if M:
                        normalize1(s, 1 - par, range(0, CT))
                if t == 2:
                    if M:
                        normalize1(s, 1 - par, range(CT, 2 * CT))
                        move_x2(s, 0)
                        normalize1(s, 1 - par, range(2 * CT, TOKT))
                        move_x2(s, 1)
                        move_x2(s, 2)
                if t == 3:
                    if nxt:
                        turned_hidden(b + 1)
                    if E:
                        expert_relus(f, 0, 1)
                if t == 4 and E:
                    expert_relus(f, 1, 0, (2,))
                    gap_exponential(f)
                if t == 5 and E:
                    move_gates(f, 1)
                    move_gates(f, 2)
                if t == 7 and E:
                    expert_relus(f, 1, 1)

            def start():
                queries_out(0, 0)
                gelu_exponential(0)
                turned_hidden(0)
                scale_samples(0, 0, 0)
                scale_samples(0, 0, 1)
                move_samples(0, 0)
                scale_samples(0, 0, 2)
                move_samples(1, 1)
                act.wait_ge(consts_in, 16 * len(CONSTS))

            def body(b, par, nxt):
                for t in range(TILES):
                    before(b, par, t, nxt)
                    exponential(TILES * b + t)
                    after(b, par, t, nxt)
                    if t < TILES - 3:
                        scale_samples(b, par, t + 3)
                    elif nxt:
                        scale_samples(b + 1, 1 - par, t + 3 - TILES)
                    if nxt or t < TILES - 2:
                        move_samples(TILES * b + t + 2, (t + 2) % TILES)

            def tail():
                for b in range(BATCH, BATCH + LAG["rest"]):
                    for t in range(TILES):
                        before(b, b % 2, t, False)
                        after(b, b % 2, t, False)

            schedule(act, start, body, tail)

        @block.vector
        def _(dve):
            dve.wait_ge(sampling_consts_in, 16 * len(SAMPLING_CONSTS))
            dve.wait_ge(cleared, 8)
            V = nc.vector

            V.tensor_scalar(bo2[:], bo2[:], OFFSET_SCALE, None, ALU.mult).then_inc(cleared, 1)
            dve.wait_ge(cleared, 9)
            V.tensor_tensor(ref_pix[:], ref_pix[:], bo2[:].unsqueeze(1).to_broadcast([P, TILES, OFFSETS]),
                            ALU.add).then_inc(cleared, 1)
            dve.wait_ge(cleared, 10)

            hidden_shape = [P, TILES, OFFCH]

            class Steps:

                def __init__(self, base, n):
                    self.base, self.n = base, n

                def count(self):
                    return self.base + self.n

                def next(self):
                    self.n += 1

            def rsqrt(step, semaphore, y, u, v):
                I32 = mybir.dt.int32
                dve.wait_ge(semaphore, step.count())
                V.tensor_scalar(u.bitcast(I32), v.bitcast(I32), 1, None, ALU.logical_shift_right).then_inc(semaphore, 1)
                step.next()
                yield
                dve.wait_ge(semaphore, step.count())
                V.tensor_scalar(y.bitcast(I32), u.bitcast(I32), -1.0, float(0x5F375A00), ALU.mult, ALU.add).then_inc(semaphore, 1)
                step.next()
                yield
                for _ in range(3):
                    dve.wait_ge(semaphore, step.count())
                    V.scalar_tensor_tensor(u, y, -0.5, y, ALU.mult, ALU.mult).then_inc(semaphore, 1)
                    step.next()
                    yield
                    dve.wait_ge(semaphore, step.count())
                    V.tensor_tensor(u, u, v, ALU.mult).then_inc(semaphore, 1)
                    step.next()
                    yield
                    dve.wait_ge(semaphore, step.count())
                    V.scalar_tensor_tensor(y, u, 1.5, y, ALU.add, ALU.mult).then_inc(semaphore, 1)
                    step.next()
                    yield


            def offset_norm(b, par):
                step = Steps(b * OFFSET_STEPS, 0)

                def chain(ins):
                    ins.then_inc(offset_step, 1)
                    step.next()

                dve.wait_ge(qo_ready, 2 * b + 2)
                chain(V.tensor_tensor(o1[:], qo[par][:, :, CH:QW], bo1[:].unsqueeze(1).to_broadcast(hidden_shape), ALU.add))
                yield
                dve.wait_ge(offset_step, step.count())
                chain(V.tensor_reduce(s8a[:], o1[:], AX.X, ALU.add))
                yield
                dve.wait_ge(offset_step, step.count())
                chain(V.tensor_scalar(s8a[:], s8a[:], 1.0 / OFFCH, None, ALU.mult))
                yield
                dve.wait_ge(offset_step, step.count())
                chain(V.tensor_tensor(o1[:], o1[:], s8a[:].unsqueeze(2).to_broadcast(hidden_shape), ALU.subtract))
                yield
                dve.wait_ge(offset_step, step.count())
                chain(V.tensor_tensor(o2[:], o1[:], o1[:], ALU.mult))
                yield
                dve.wait_ge(offset_step, step.count())
                chain(V.tensor_reduce(s8d[:], o2[:], AX.X, ALU.add))
                yield
                dve.wait_ge(offset_step, step.count())
                chain(V.tensor_scalar(s8a[:], s8d[:], 1.0 / OFFCH, EPS, ALU.mult, ALU.add))
                yield
                yield from rsqrt(step, offset_step, s8c[:], s8d[:], s8a[:])
                dve.wait_ge(offset_step, step.count())
                chain(V.tensor_tensor(o1[:], o1[:], s8c[:].unsqueeze(2).to_broadcast(hidden_shape), ALU.mult))
                yield
                dve.wait_ge(offset_step, step.count())
                chain(V.tensor_tensor(o1[:], o1[:], lng[:].unsqueeze(1).to_broadcast(hidden_shape), ALU.mult))
                yield
                dve.wait_ge(offset_step, step.count())
                chain(V.tensor_tensor(o1[:], o1[:], lnb[:].unsqueeze(1).to_broadcast(hidden_shape), ALU.add))
                yield
                dve.wait_ge(offset_step, step.count())
                chain(V.tensor_tensor(o2[:], o1[:], o1[:], ALU.mult))
                yield
                dve.wait_ge(offset_step, step.count())
                chain(V.tensor_scalar(o2[:], o2[:], 0.044715, 1.0, ALU.mult, ALU.add))
                yield
                dve.wait_ge(offset_step, step.count())
                V.tensor_tensor(o2[:], o2[:], o1[:], ALU.mult).then_inc(gelu_arg, 1)
                assert step.n == 23
                yield

            def offset_gelu(b):
                dve.wait_ge(gelu_exp, b + 1)
                V.tensor_scalar(o3[:], o3[:], 1.0, None, ALU.add).then_inc(offset_step, 1)
                yield
                dve.wait_ge(offset_step, b * OFFSET_STEPS + 24)
                V.reciprocal(o3[:], o3[:]).then_inc(offset_step, 1)
                yield
                dve.wait_ge(offset_step, b * OFFSET_STEPS + 25)
                V.tensor_tensor(o4[:], o1[:], o3[:], ALU.mult).then_inc(off_h, 1)
                yield

            def positions(b, par):
                step = Steps(b * OFFSET_STEPS, 25)

                def chain(ins):
                    ins.then_inc(offset_step, 1)
                    step.next()

                dve.wait_ge(pA_full, 4 * b + 4)
                V.scalar_tensor_tensor(pix[:].rearrange("p s a -> p (s a)"), pA[:, 0:P], OFFSET_SCALE,
                                       ref_pix[:].rearrange("p t o -> p (t o)"), ALU.mult, ALU.add).then_inc(pix_ready, 1)
                yield
                dve.wait_ge(pix_ready, b + 1)
                chain(V.tensor_scalar(pix[:], pix[:], 0.0, float(IMG - 1), ALU.max, ALU.min))
                yield
                dve.wait_ge(offset_step, step.count())
                chain(V.tensor_scalar(low[:], pix[:], -0.5, ROUND, ALU.add, ALU.add))
                yield
                dve.wait_ge(offset_step, step.count())
                chain(V.tensor_scalar(low[:], low[:], ROUND, float(IMG - 2), ALU.subtract, ALU.min))
                yield
                dve.wait_ge(offset_step, step.count())
                chain(V.scalar_tensor_tensor(rowf[:], low[:, :, 1], float(IMG), low[:, :, 0], ALU.mult, ALU.add))
                yield
                chain(V.tensor_tensor(hats[:, :, :, 1], pix[:], low[:], ALU.subtract))
                yield
                dve.wait_ge(offset_step, step.count())
                if due(b):
                    dve.wait_ge(row_moved, b)
                V.tensor_scalar(idx[par][:], rowf[:], batch_row[:, 0:1], None, ALU.add).then_inc(idx_ready, 1)
                yield
                chain(V.tensor_scalar(hats[:, :, :, 0], hats[:, :, :, 1], -1.0, 1.0, ALU.mult, ALU.add))
                yield
                for x in range(2):
                    out4 = w4[par][:].rearrange("p t (k x y) -> p (t k) x y", x=2, y=2)[:, :, x, :]
                    dve.wait_ge(offset_step, step.count())
                    chain(V.tensor_tensor(out4, hats[:, :, 1, :],
                                          hats[:, :, 0, x:x + 1].to_broadcast([P, TILES * POINTS, 2]), ALU.mult))
                    yield
                dve.wait_ge(idx_ready, b + 1)
                V.tensor_scalar(batch_row[:], batch_row[:], float(ROW_PAIRS * IMG), None, ALU.add).then_inc(row_moved, 1)
                assert step.n == OFFSET_STEPS
                yield

            def weight_samples(n, b, par, t):
                dve.wait_ge(gather_in[t], GATHER * (b + 1))
                dve.wait_ge(offset_step, (b + 1) * OFFSET_STEPS)
                at = 4 * SCALED[t]
                view = G[:, t, :].rearrange("p (k c) -> p k c", c=CH)[:, at:, :]
                V.tensor_tensor(view, view, w4[par][:, t, at:].unsqueeze(2).to_broadcast([P, 4 * POINTS - at, CH]),
                                ALU.mult).then_inc(g_weighted, 1)

            def sum_samples(n, b, t):
                dve.wait_ge(g_weighted, n + 1)
                if SCALED[t]:
                    dve.wait_ge(g_scaled, b * sum(k > 0 for k in SCALED) + sum(k > 0 for k in SCALED[:t + 1]))
                if due(2 * (n - 1)):
                    dve.wait_ge(t_full, 2 * (n - 1))
                view = G[:, t, :].rearrange("p (k x c) -> p k x c", x=2, c=2 * CH)
                V.tensor_tensor(g2[t % 2][:], view[:, :, 0, :], view[:, :, 1, :], ALU.add).then_inc(g_summed, 1)

            def scores_of(n, b, par, t):
                dve.wait_ge(kv_full, 2 * n + 2)
                q = qo[par][:, t, 0:CH].unsqueeze(1).to_broadcast([P, POINTS, CH])
                V.tensor_tensor(prodk[:], kv[:, :, 0:CH], q, ALU.mult).then_inc(qk_done, 1)

            def scores_sum(n):
                dve.wait_ge(qk_done, n + 1)
                V.tensor_reduce(scores[:], prodk[:].rearrange("p k (h d) -> p k h d", d=HD), AX.X,
                                ALU.add).then_inc(scores_done, 1)

            def scores_max(n):
                dve.wait_ge(scores_done, n + 1)
                V.tensor_reduce(smax[:], scores[:].rearrange("p k h -> p h k"), AX.X, ALU.max).then_inc(max_done, 1)

            def scores_shift(n):
                dve.wait_ge(max_done, n + 1)
                V.tensor_tensor(shifted[:], scores[:], smax[:].unsqueeze(1).to_broadcast([P, POINTS, HEADS]),
                                ALU.subtract).then_inc(shifted_ready, 1)

            def attend(n):
                dve.wait_ge(probs_ready, n + 1)
                V.tensor_tensor(prodv[:].rearrange("p k (h d) -> p k h d", d=HD),
                                kv[:, :, CH:2 * CH].rearrange("p k (h d) -> p k h d", d=HD),
                                probs[:].unsqueeze(3).to_broadcast([P, POINTS, HEADS, HD]), ALU.mult).then_inc(av_done, 1)
                V.tensor_reduce(den[:], probs[:].rearrange("p k h -> p h k"), AX.X, ALU.add).then_inc(den_done, 1)

            def attend_sum(n):
                dve.wait_ge(av_done, n + 1)
                V.tensor_reduce(av[:], prodv[:].rearrange("p k c -> p c k"), AX.X, ALU.add).then_inc(avsum_done, 1)

            def attend_recip(n):
                dve.wait_ge(den_done, n + 1)
                V.reciprocal(rden[:], den[:]).then_inc(rden_done, 1)

            def attended(n, par, t):
                dve.wait_ge(avsum_done, n + 1)
                dve.wait_ge(rden_done, n + 1)
                V.tensor_tensor(H[par][:, t, :].rearrange("p (h d) -> p h d", d=HD),
                                av[:].rearrange("p (h d) -> p h d", d=HD),
                                rden[:].unsqueeze(2).to_broadcast([P, HEADS, HD]), ALU.mult).then_inc(h_ready, 1)

            def norm1_stats(s, par, tiles):
                for t in tiles:
                    if t < TILES:
                        dve.wait_ge(h_ready, s * TILES + t + 1)
                    else:
                        dve.wait_ge(txt_in, 16 * (s + 1))
                    dve.sem_inc(dve_passed, 1)
                    V.bn_stats(stats1[:, t, :], H[par][:, t, :]).then_inc(stat1_done, 1)
                    yield
                if tiles[-1] == TOKT - 1:
                    dve.wait_ge(stat1_done, 2 * s * TOKT + TOKT)
                    dve.sem_inc(dve_passed, 1)
                    for t in range(TOKT):
                        V.bn_aggr(mv1[:, t, :], stats1[:, t, :]).then_inc(stat1_done, 1)
                        yield

            def norm2_stats(s, par, tiles):
                for t in tiles:
                    if t % CT == 0:
                        dve.wait_ge(mix_read, s * CHUNKS + t // CT + 1)
                    V.bn_stats(stats2[:, t, :], h1[par][:, t, :]).then_inc(stat2_done, 1)
                    yield
                if tiles[-1] == TOKT - 1:
                    dve.wait_ge(stat2_done, 2 * s * TOKT + TOKT)
                    dve.sem_inc(dve_passed, 1)
                    for t in range(TOKT):
                        V.bn_aggr(mv2[:, t, :], stats2[:, t, :]).then_inc(stat2_done, 1)
                        yield

            def norm_scale(s, k, mv):
                step = Steps(s * NORM_STEPS, 13 * k)
                dve.wait_ge((stat1_done, stat2_done)[k], 2 * (s + 1) * TOKT)
                V.tensor_scalar(ve[:], mv[:, :, 1], EPS, None, ALU.add).then_inc(norm_step, 1)
                step.next()
                if k == 0:
                    dve.wait_ge(norm_step, step.count())
                    V.tensor_copy(mark[:], ve[:, 0:1]).then_inc(var_ready, 1)
                yield
                yield from rsqrt(step, norm_step, y0[:], ny[:], ve[:])
                dve.wait_ge(norm_step, step.count())
                V.tensor_copy(rstd[k][:], y0[:]).then_inc(norm_step, 1)
                step.next()
                yield
                V.scalar_tensor_tensor(nmr[k][:], mv[:, :, 0], -1.0, y0[:], ALU.mult, ALU.mult).then_inc(norm_ready, 1)
                yield

            def scan(s, c):
                w = min(CW, SEQ - c * CW)
                for v in range(SHALVES):
                    use = ("drive", c * SHALVES + v)
                    dve.wait_ge(mixer_full, fulls(s, *use))
                    if c > 0:
                        dve.wait_ge(mixer_read, reads(s, "drive", (c - 1) * SHALVES + v))
                    lead = state0[:, v:v + 1] if c == 0 else states[:, v, c * CW - 1:c * CW]
                    V.tensor_tensor_scan(states[:, v, c * CW:c * CW + w], decay[:, v:v + 1].to_broadcast([P, w]),
                                         ring[:, bank(*use), 0:w], lead, ALU.mult, ALU.add).then_inc(mixer_read, 1)
                    yield

            def add_mixed(s, par, c):
                dve.wait_ge(mix_full, s * CHUNKS + c + 1)
                src = (pA, pB, pA)[c][:, 0:CT * NW].rearrange("p (t c) -> p t c", c=NW)[:, :, 0:CH]
                V.tensor_tensor(h1[par][:, c * CT:(c + 1) * CT, :], src, H[par][:, c * CT:(c + 1) * CT, :],
                                ALU.add).then_inc(mix_read, 1)
                yield

            wide = [P, TOKT, EXPERTS]

            def spread(x):
                return x[:].unsqueeze(2).to_broadcast(wide)

            def route_shift(f):
                lg = pB[:, 0:TOKT * EXPERTS].rearrange("p (t e) -> p t e", e=EXPERTS)
                dve.wait_ge(logits_full, f + 1)
                V.tensor_reduce(t9a[:], lg, AX.X, ALU.max).then_inc(route_step, 1)
                yield
                dve.wait_ge(route_step, f * ROUTE_STEPS + 1)
                V.tensor_tensor(r1[:], lg, spread(t9a), ALU.subtract).then_inc(logits_read, 1)
                yield

            def route_top(f):
                step = Steps(f * ROUTE_STEPS, 1)

                def chain(ins):
                    ins.then_inc(route_step, 1)
                    step.next()

                ranks = rank[:].unsqueeze(1).to_broadcast(wide)
                dve.wait_ge(route_exp, 2 * f + 1)
                chain(V.tensor_reduce(t9a[:], r2[:], AX.X, ALU.add))
                yield
                dve.wait_ge(route_step, step.count())
                chain(V.reciprocal(t9a[:], t9a[:]))
                yield
                dve.wait_ge(route_step, step.count())
                chain(V.tensor_tensor(r2[:], r2[:], spread(t9a), ALU.mult))
                yield
                dve.wait_ge(route_step, step.count())
                chain(V.tensor_reduce(t9a[:], r2[:], AX.X, ALU.max))
                yield
                dve.wait_ge(route_step, step.count())
                chain(V.tensor_tensor(r1[:], r2[:], spread(t9a), ALU.is_ge))
                yield
                dve.wait_ge(route_step, step.count())
                chain(V.tensor_tensor(r1[:], r1[:], ranks, ALU.mult))
                yield
                dve.wait_ge(route_step, step.count())
                chain(V.tensor_reduce(t9b[:], r1[:], AX.X, ALU.max))
                yield
                dve.wait_ge(route_step, step.count())
                chain(V.tensor_tensor(top1[:], r1[:], spread(t9b), ALU.is_equal))
                yield
                dve.wait_ge(route_step, step.count())
                chain(V.scalar_tensor_tensor(r3[:], top1[:], -4.0, r2[:], ALU.mult, ALU.add))
                yield
                dve.wait_ge(route_step, step.count())
                chain(V.tensor_reduce(t9b[:], r3[:], AX.X, ALU.max))
                yield
                dve.wait_ge(route_step, step.count())
                chain(V.tensor_tensor(r1[:], r3[:], spread(t9b), ALU.is_ge))
                yield
                dve.wait_ge(route_step, step.count())
                chain(V.tensor_tensor(r1[:], r1[:], ranks, ALU.mult))
                yield
                dve.wait_ge(route_step, step.count())
                chain(V.tensor_reduce(t9c[:], r1[:], AX.X, ALU.max))
                yield
                dve.wait_ge(route_step, step.count())
                chain(V.tensor_tensor(top2[:], r1[:], spread(t9c), ALU.is_equal))
                yield
                dve.wait_ge(route_step, step.count())
                V.tensor_tensor(t9a[:], t9b[:], t9a[:], ALU.subtract).then_inc(gap_ready, 1)
                yield

            def route_gates(f):
                base = f * ROUTE_STEPS
                dve.wait_ge(route_exp, 2 * f + 2)
                V.tensor_scalar(t9c[:], t9b[:], 1.0, None, ALU.add).then_inc(route_step, 1)
                yield
                dve.wait_ge(route_step, base + 16)
                V.reciprocal(t9c[:], t9c[:]).then_inc(route_step, 1)
                yield
                V.tensor_tensor(r1[:], top2[:], spread(t9b), ALU.mult).then_inc(route_step, 1)
                yield
                dve.wait_ge(route_step, base + 18)
                V.tensor_tensor(r1[:], r1[:], top1[:], ALU.add).then_inc(route_step, 1)
                yield
                dve.wait_ge(route_step, base + 19)
                V.tensor_tensor(gates[:, :, 0:EXPERTS], r1[:], spread(t9c), ALU.mult).then_inc(gates_ready, 1)
                yield

            def gate_units(f, c, pairs):
                for m in pairs:
                    use = (f"gate{c}", m)
                    dve.wait_ge(full_of(*use), fulls(f, *use))
                    unit = (f"up{c}", PAIRS + m)
                    dve.wait_ge(read_of(*unit), reads(f, *unit))
                    V.tensor_tensor(a3[:, m, :], ring[:, bank(*use), 0:CW], a2[:, m, :], ALU.mult).then_inc(read_of(*use), 1)
                    yield

            def finish(f, par, c):
                use = ("down", c)
                dve.wait_ge(full_of(*use), fulls(f, *use))
                per = 32 if c == CHUNKS - 1 else 16
                if due(f * per):
                    dve.wait_ge(out_done[c], f * per)
                src = ring[:, bank(*use), 0:CT * NW].rearrange("p (t c) -> p t c", c=NW)[:, :, 0:CH]
                V.tensor_tensor(fin[c][:], src, h1[par][:, c * CT:(c + 1) * CT, :], ALU.add).then_inc(read_of(*use), 1)
                yield

            def run(*stages):
                for stage in stages:
                    yield from stage

            def some(stage, steps):
                for _ in range(steps):
                    if next(stage, stage) is stage:
                        return
                    yield

            def slot_chains(b, par, nxt):
                M, E, R = active("mixer", b), active("experts", b), active("rest", b)
                s, f, g = b - 1, b - 2, b - 3
                S = active("sampling", b)
                top = route_top(f)
                norm = offset_norm(b + 1, 1 - par)
                chunk = lambda c: range(c * CT, (c + 1) * CT)
                return [
                    ([gate_units(g, 1, (0, 1))] * R + [norm_scale(f, 1, mv2)] * E,
                     [],
                     [norm1_stats(s, 1 - par, (TILES - 1, TILES))] * M,
                     [gate_units(g, 1, (2,))] * R),
                    ([norm_scale(s, 0, mv1)] * M,
                     [finish(g, 1 - par, 1)] * R,
                     [some(norm, 10)] * nxt,
                     []),
                    ([norm] * nxt,
                     [],
                     [gate_units(g, 2, (0, 1))] * R,
                     [route_shift(f)] * E + [gate_units(g, 2, (2,))] * R),
                    ([],
                     [finish(g, 1 - par, 2)] * R + [offset_gelu(b + 1)] * nxt,
                     [some(top, 8)] * E,
                     [scan(s, 0)] * M),
                    ([positions(b + 1, 1 - par)] * nxt + [scan(s, 1)] * M + [top] * E,
                     [],
                     [],
                     [route_gates(f)] * E),
                    ([scan(s, 2)] * M,
                     [],
                     [norm1_stats(b, par, (0, 1, 2))] * S,
                     [gate_units(f, 0, (0, 1))] * E + [run(add_mixed(s, 1 - par, 0), norm2_stats(s, 1 - par, chunk(0)))] * M),
                    ([gate_units(f, 0, (2,))] * E,
                     [],
                     [norm1_stats(b, par, (3, 4, 5))] * S,
                     [run(add_mixed(s, 1 - par, 1), norm2_stats(s, 1 - par, chunk(1)))] * M + [finish(f, par, 0)] * E),
                    ([],
                     [],
                     [norm1_stats(b, par, (6,))] * S,
                     [run(add_mixed(s, 1 - par, 2), norm2_stats(s, 1 - par, chunk(2)))] * M),
                ]

            def fill(chains, rounds=1):
                for _ in range(rounds):
                    for c in chains:
                        next(c, None)

            def drain(chains):
                left = list(chains)
                while left:
                    left = [c for c in left if next(c, c) is not c]

            def start():
                drain([offset_norm(0, 0)])
                drain([offset_gelu(0)])
                drain([positions(0, 0)])
                weight_samples(0, 0, 0, 0)
                sum_samples(0, 0, 0)
                weight_samples(1, 0, 0, 1)
                sum_samples(1, 0, 1)
                dve.wait_ge(consts_in, 16 * len(CONSTS))

            def body(b, par, nxt):
                slots = slot_chains(b, par, nxt)
                for t in range(TILES):
                    n = TILES * b + t
                    chains, mid, late, last = slots[t]
                    scores_of(n, b, par, t)
                    fill(chains)
                    scores_sum(n)
                    fill(chains, 2)
                    scores_max(n)
                    chains = chains + mid
                    fill(chains, 2)
                    scores_shift(n)
                    if t < TILES - 2:
                        weight_samples(n + 2, b, par, t + 2)
                    elif nxt:
                        weight_samples(n + 2, b + 1, 1 - par, t + 2 - TILES)
                    chains = chains + late
                    fill(chains, 1)
                    attend(n)
                    chains = chains + last
                    if t < TILES - 2:
                        sum_samples(n + 2, b, t + 2)
                    elif nxt:
                        sum_samples(n + 2, b + 1, t + 2 - TILES)
                    fill(chains)
                    attend_sum(n)
                    fill(chains)
                    attend_recip(n)
                    fill(chains)
                    attended(n, par, t)
                    drain(chains)

            def tail():
                for b in range(BATCH, BATCH + LAG["rest"]):
                    for early, mid, late, last in slot_chains(b, b % 2, False):
                        drain(early + mid)
                        drain(late + last)

            schedule(dve, start, body, tail)


_REF_COORD = np.arange(GRID) * (IMG - 1) / (GRID - 1)
_REF_LOW = np.minimum(np.floor(_REF_COORD), IMG - 2).astype(np.int64)


def _constants():
    hi = _REF_COORD - _REF_LOW
    axis = np.stack([1.0 - hi, hi])
    w = axis[:, None, :, None] * axis[None, :, None, :]
    wtab = np.repeat(w.reshape(2, 2, QUERIES), CH, axis=0).astype(np.float32)
    gy, gx = np.meshgrid(_REF_COORD, _REF_COORD, indexing="ij")
    pix = np.stack([gx.reshape(-1), gy.reshape(-1)], -1).reshape(TILES, P, 1, 2)
    reftab = np.broadcast_to(pix, (TILES, P, HEADS, 2)).reshape(TILES, P, OFFSETS).transpose(1, 0, 2)
    sel = np.zeros((P, PAIRS, P), np.float32)
    for e in range(EXPERTS):
        sel[e, e // 2, (e % 2) * CH:(e % 2 + 1) * CH] = 1.0
    return {
        "wtab": wtab,
        "reftab": np.ascontiguousarray(reftab).astype(np.float32),
        "ident_in": np.eye(P, dtype=np.float32),
        "rank_in": np.broadcast_to(np.arange(EXPERTS, 0, -1, dtype=np.float32), (P, EXPERTS)),
        "sel_in": sel,
    }


def _layout(x, txt, L0_tok_W_q, L0_tok_W_k, L0_tok_W_v, L0_tok_W_o1, L0_tok_b_o1, L0_tok_ln_g,
            L0_tok_ln_b, L0_tok_W_o2, L0_tok_b_o2, L0_attn_h0, L0_attn_A, L0_attn_B, L0_attn_C,
            L0_attn_M, L0_ffn_router_w1, L0_ffn_router_b1, L0_ffn_router_w2, L0_ffn_router_b2,
            L0_ffn_expert_w1, L0_ffn_expert_b1, L0_ffn_expert_w2, L0_ffn_expert_b2,
            L0_ffn_expert_w3, L0_ffn_expert_b3):
    rows = np.ascontiguousarray(x.transpose(0, 2, 3, 1))
    fm = np.empty((BATCH, ROW_PAIRS, IMG, 2, CH), np.float32)
    fm[:, :, :, 0] = rows[:, :-1]
    fm[:, :, :, 1] = rows[:, 1:]
    lo = _REF_LOW
    qcorn = np.empty((BATCH, 2, CH, 2, GRID, GRID), np.float32)
    for yc in range(2):
        for xc in range(2):
            qcorn[:, yc, :, xc] = x[:, :, lo + yc][:, :, :, lo + xc]
    def padded(shape, *parts):
        a = np.zeros(shape, np.float32)
        for at, part in parts:
            a[at] = part
        return a
    s = np.s_
    wqo = padded((2, CH, NW), (s[:, :, :CH], L0_tok_W_q.T), (s[:, :, CH:QW], L0_tok_W_o1)).reshape(P, NW)
    wkv = padded((2, CH, 2 * CH), (s[:, :, :CH], L0_tok_W_k.T), (s[:, :, CH:], L0_tok_W_v.T)).reshape(P, 2 * CH)
    wo2 = padded((TILES, OFFCH, TILES, OFFSETS), *[(s[t, :, t], L0_tok_W_o2) for t in range(TILES)]).reshape(P, P)
    every = lambda v: np.broadcast_to(v, (P,) + v.shape)
    mt = padded((2, CH, TAPS // 2, NW), (s[..., :CH], L0_attn_M.transpose(2, 1, 0).reshape(TAPS // 2, 2, CH, CH).transpose(1, 2, 0, 3)))
    pair = lambda v: v.reshape(PAIRS, P).T
    w1 = padded((P, PAIRS, 2, CH), (s[:CH], L0_ffn_expert_w1.reshape(PAIRS, 2, CH, CH).transpose(2, 0, 1, 3)))
    w2 = padded((2, CH, PAIRS, 2, CH), *[(s[e, :, :, e], L0_ffn_expert_w2[e::2].transpose(1, 0, 2)) for e in range(2)])
    w3 = padded((2, CH, PAIRS, NW), (s[..., :CH], L0_ffn_expert_w3.reshape(PAIRS, 2, CH, CH).transpose(1, 2, 0, 3)))
    return {
        "fm_rows": fm.reshape(-1, 2 * CH),
        "qcorn": qcorn.reshape(BATCH, P, 2, QUERIES),
        "txt": txt,
        "wqo_in": wqo, "wkv_in": wkv, "wo2_in": wo2,
        "bo1_in": every(L0_tok_b_o1), "lng_in": every(L0_tok_ln_g), "lnb_in": every(L0_tok_ln_b),
        "bo2_in": every(L0_tok_b_o2),
        "a_in": L0_attn_A.reshape(SHALVES, P).T, "h0_in": L0_attn_h0.reshape(SHALVES, P).T,
        "bst_in": padded((P, STATES), (s[:CH], L0_attn_B)),
        "cst_in": padded((P, SHALVES, NW), (s[..., :CH], L0_attn_C.reshape(SHALVES, P, CH).transpose(1, 0, 2))),
        "mt_in": mt.reshape(P, TAPS // 2, NW),
        "rw1_in": padded((P, P), (s[:CH, :ROUTER_H], L0_ffn_router_w1)),
        "rb1_in": padded((P, 1), (s[:ROUTER_H, 0], L0_ffn_router_b1), (s[ROUTER_H, 0], 1.0)),
        "rw2_in": padded((P, NW), (s[:ROUTER_H, :EXPERTS], L0_ffn_router_w2), (s[ROUTER_H, :EXPERTS], L0_ffn_router_b2)),
        "w1_in": w1.reshape(P, PAIRS, P), "b1_in": pair(L0_ffn_expert_b1),
        "w2_in": w2.reshape(P, PAIRS, P), "b2_in": pair(L0_ffn_expert_b2),
        "w3_in": w3.reshape(P, PAIRS, NW),
        "b3_in": padded((P, NW), (s[:EXPERTS, :CH], L0_ffn_expert_b3)),
    }


def kernel(**inputs):
    from concourse import bacc
    from concourse.bass_utils import run_bass_kernel_spmd

    arrays = {**_constants(), **_layout(**{k: np.asarray(v) for k, v in inputs.items()})}
    arrays = {f"in_{k}": np.ascontiguousarray(v) for k, v in arrays.items()}
    nc = bacc.Bacc("TRN2", target_bir_lowering=False, num_devices=1)
    args = {k[3:]: nc.dram_tensor(k, a.shape, mybir.dt.from_np(a.dtype), kind="ExternalInput").ap()
            for k, a in arrays.items()}
    out = nc.dram_tensor("out_0", (BATCH, SEQ, CH), F32, kind="ExternalOutput").ap()
    build(nc, out=out, **args)
    r = run_bass_kernel_spmd(nc, [arrays], core_ids=[0])
    return r.results[0]["out_0"]
```
